# Optimizing a Trainium2 kernel written in Bass

```python
import numpy as np
import jax
import jax.numpy as jnp

def _softmax(x, axis=-1):
    return jax.nn.softmax(x, axis=axis)

def _gelu(x):
    return jax.nn.gelu(x, approximate=True)

def _silu(x):
    return jax.nn.silu(x)

def _sigmoid(x):
    return jax.nn.sigmoid(x)

def _layernorm(x, axis=-1, eps=1e-05):
    m = jnp.mean(x, axis=axis, keepdims=True)
    v = jnp.var(x, axis=axis, keepdims=True)
    return (x - m) / jnp.sqrt(v + eps)

def _scatter_add(tgt, idx, src, axis=0):
    return tgt.at[idx].add(src)

def _segment_sum(src, seg, n):
    return jax.ops.segment_sum(src, seg, n)
kernel_name = 'mk_gnn_resnorm_d4_gnn_r32_541821'

def setup_inputs(seed: int=0):
    np.random.seed(seed)
    _w = jnp.asarray

    def _rec_inputs():
        import jax
        import jax.numpy as jnp
        _gk = jax.random.key(seed)
        x = -1.686e-05 + 1 * jax.random.normal(jax.random.fold_in(_gk, 1), (50000, 160), jnp.float32)
        src = jax.random.randint(jax.random.fold_in(_gk, 2), (50000,), 0, 50000, jnp.int32)
        dst = jax.random.randint(jax.random.fold_in(_gk, 3), (50000,), 0, 50000, jnp.int32)
        _o = jnp.argsort(dst, stable=True)
        src = src[_o]
        dst = dst[_o]
        edge_attr_12 = jax.random.uniform(jax.random.fold_in(_gk, 12), (50000, 12), jnp.float32, 0.0, 1)
        edge_attr_16 = jax.random.uniform(jax.random.fold_in(_gk, 13), (50000, 16), jnp.float32, 0.0, 1)
        edge_attr_32 = 0.000196303 + 1.00016 * jax.random.normal(jax.random.fold_in(_gk, 14), (50000, 32), jnp.float32)
        edge_attr_4 = 0.000486536 + 0.999406 * jax.random.normal(jax.random.fold_in(_gk, 15), (50000, 4), jnp.float32)
        node_vec1 = -0.00915711 + 0.999674 * jax.random.normal(jax.random.fold_in(_gk, 17), (50000, 1), jnp.float32)
        return (x, src, dst, edge_attr_12, edge_attr_16, edge_attr_32, edge_attr_4, node_vec1)
    x, src, dst, edge_attr_12, edge_attr_16, edge_attr_32, edge_attr_4, node_vec1 = _rec_inputs()

    def _L0_gnn_setup():
        import jax, jax.numpy as jnp
        import numpy as np
        MUL0_N, MUL1_N = (64, 32)
        MUL0_E, MUL1_E = (8, 8)
        MUL0_H, MUL1_H = (64, 32)
        N_NODES, N_EDGES = (50000, 25000)
        D_NODE = MUL0_N + 3 * MUL1_N
        D_EDGE = MUL0_E + 3 * MUL1_E
        D_HID = MUL0_H + 3 * MUL1_H

        def _split(x, mul0, mul1):
            s = x[..., :mul0]
            v = x[..., mul0:].reshape(x.shape[0], mul1, 3)
            return (s, v)

        def fctp_messages(x, e, W1, W2, W3, W4):
            xs, xv = _split(x, MUL0_N, MUL1_N)
            es, ev = _split(e, MUL0_E, MUL1_E)
            inv_sqrt2 = 1.0 / np.sqrt(2.0)
            s1 = jnp.einsum('ea,eb,abc->ec', xs, es, W1) * (1.0 / np.sqrt(MUL0_N * MUL0_E))
            s2 = jnp.einsum('eai,ebi,abc->ec', xv, ev, W2) * (1.0 / (np.sqrt(3.0) * np.sqrt(MUL1_N * MUL1_E)))
            out_s = (s1 + s2) * inv_sqrt2
            v1 = jnp.einsum('ea,ebi,abc->eci', xs, ev, W3) * (1.0 / np.sqrt(MUL0_N * MUL1_E))
            v2 = jnp.einsum('eai,eb,abc->eci', xv, es, W4) * (1.0 / np.sqrt(MUL1_N * MUL0_E))
            out_v = (v1 + v2) * inv_sqrt2
            return jnp.concatenate([out_s, out_v.reshape(out_v.shape[0], -1)], axis=-1)
        key = jax.random.key(seed)
        ks = jax.random.split(key, 12)
        node_features = jax.random.normal(ks[0], (N_NODES, D_NODE), dtype=jnp.float32)
        edge_index = jax.random.randint(ks[1], (2, N_EDGES), 0, N_NODES, dtype=jnp.int64)
        edge_attr_tensor = jax.random.normal(ks[2], (N_EDGES, D_EDGE), dtype=jnp.float32)
        node_attr_scalar_raw = jax.random.normal(ks[3], (N_NODES, 1), dtype=jnp.float32)
        W1 = jax.random.normal(ks[4], (MUL0_N, MUL0_E, MUL0_H), dtype=jnp.float32)
        W2 = jax.random.normal(ks[5], (MUL1_N, MUL1_E, MUL0_H), dtype=jnp.float32)
        W3 = jax.random.normal(ks[6], (MUL0_N, MUL1_E, MUL1_H), dtype=jnp.float32)
        W4 = jax.random.normal(ks[7], (MUL1_N, MUL0_E, MUL1_H), dtype=jnp.float32)
        Wm = jax.random.normal(ks[8], (D_HID, D_HID), dtype=jnp.float32) / np.sqrt(D_HID)
        bm = jnp.zeros((D_HID,), dtype=jnp.float32)
        Wu = jax.random.normal(ks[9], (D_NODE + D_HID, D_NODE), dtype=jnp.float32) / np.sqrt(D_NODE + D_HID)
        bu = jnp.zeros((D_NODE,), dtype=jnp.float32)
        return {'node_features': node_features, 'edge_index': edge_index, 'edge_attr_tensor': edge_attr_tensor, 'node_attr_scalar_raw': node_attr_scalar_raw, 'W1': W1, 'W2': W2, 'W3': W3, 'W4': W4, 'Wm': Wm, 'bm': bm, 'Wu': Wu, 'bu': bu}
    _L0_gnn_all = _L0_gnn_setup()
    _L0_gnn_in = {k: v for k, v in _L0_gnn_all.items() if k in ('W1', 'W2', 'W3', 'W4', 'Wm', 'bm', 'Wu', 'bu')}
    del _L0_gnn_all

    def _L1_gnn_setup():
        import jax, jax.numpy as jnp
        import numpy as np
        N = 50000
        E = 12500
        MUL0 = 64
        MUL1 = 32
        NEF = 12
        RN = 100
        NUM_NEIGHBORS = 8.0
        WNUM = MUL0 + MUL0 + MUL1 + MUL1

        def _split(x):
            return (x[:, :MUL0], x[:, MUL0:].reshape(-1, MUL1, 3))

        def _fctp_scalar_attr(x0, x1, z, Ws, Wv):
            s = x0 @ Ws * z / np.sqrt(Ws.shape[0])
            v = jnp.einsum('nuc,uw->nwc', x1, Wv) * z[:, :, None] / np.sqrt(Wv.shape[0])
            return (s, v)
        key = jax.random.key(seed)
        ks = jax.random.split(key, 16)
        return {'node_input': jax.random.normal(ks[0], (N, MUL0 + 3 * MUL1), jnp.float32), 'node_attr': jax.random.uniform(ks[1], (N, 1), dtype=jnp.float32), 'edge_src': jax.random.randint(ks[2], (E,), 0, N), 'edge_dst': jax.random.randint(ks[3], (E,), 0, N), 'edge_attr': jax.random.normal(ks[4], (E, 4), jnp.float32), 'edge_features': jax.random.uniform(ks[5], (E, NEF), dtype=jnp.float32), 'W_sc0': jax.random.normal(ks[6], (MUL0, MUL0), jnp.float32), 'W_sc1': jax.random.normal(ks[7], (MUL1, MUL1), jnp.float32), 'W_l1_0': jax.random.normal(ks[8], (MUL0, MUL0), jnp.float32), 'W_l1_1': jax.random.normal(ks[9], (MUL1, MUL1), jnp.float32), 'W_fc1': jax.random.normal(ks[10], (NEF, RN), jnp.float32), 'W_fc2': jax.random.normal(ks[11], (RN, WNUM), jnp.float32), 'W_l2_0': jax.random.normal(ks[12], (MUL0 + MUL1, MUL0), jnp.float32), 'W_l2_1': jax.random.normal(ks[13], (MUL0 + MUL1, MUL1), jnp.float32)}
    _L1_gnn_all = _L1_gnn_setup()
    _L1_gnn_in = {k: v for k, v in _L1_gnn_all.items() if k in ('W_sc0', 'W_sc1', 'W_l1_0', 'W_l1_1', 'W_fc1', 'W_fc2', 'W_l2_0', 'W_l2_1')}
    del _L1_gnn_all

    def _L2_gnn_setup():
        import jax, jax.numpy as jnp
        import numpy as np
        import math
        N = 50000
        E = 15625
        MUL0 = 64
        MUL1 = 32
        MID = MUL0 + MUL1
        FC_IN = 16
        FC_H = 64
        WEIGHT_NUMEL = 2 * MUL0 + 2 * MUL1
        NUM_NEIGH = 10.0
        C_S = math.sin(math.pi / 8.0)
        C_X = math.cos(math.pi / 8.0)
        key = jax.random.key(seed)
        ks = jax.random.split(key, 14)
        f32 = jnp.float32
        return {'node_input': jax.random.normal(ks[0], (N, MUL0 + 3 * MUL1), f32), 'node_attr': jnp.ones((N, 1), f32), 'edge_src': jax.random.randint(ks[1], (E,), 0, N), 'edge_dst': jax.random.randint(ks[2], (E,), 0, N), 'edge_attr': jax.random.normal(ks[3], (E, 4), f32), 'edge_length_embedded': jax.random.uniform(ks[4], (E, FC_IN), dtype=f32), 'W_sc0': jax.random.normal(ks[5], (MUL0, MUL0), f32), 'W_sc1': jax.random.normal(ks[6], (MUL1, MUL1), f32), 'W_l1_0': jax.random.normal(ks[7], (MUL0, MUL0), f32), 'W_l1_1': jax.random.normal(ks[8], (MUL1, MUL1), f32), 'fc_W1': jax.random.normal(ks[9], (FC_IN, FC_H), f32), 'fc_W2': jax.random.normal(ks[10], (FC_H, WEIGHT_NUMEL), f32), 'W_l2_0': jax.random.normal(ks[11], (MID, MUL0), f32), 'W_l2_1': jax.random.normal(ks[12], (MID, MUL1), f32)}
    _L2_gnn_all = _L2_gnn_setup()
    _L2_gnn_in = {k: v for k, v in _L2_gnn_all.items() if k in ('W_sc0', 'W_sc1', 'W_l1_0', 'W_l1_1', 'fc_W1', 'fc_W2', 'W_l2_0', 'W_l2_1')}
    del _L2_gnn_all

    def _L3_gnn_setup():
        import jax, jax.numpy as jnp
        import numpy as np
        N = 625
        E = 10000
        MUL0 = 64
        MUL1 = 32
        FC_IN = 16
        FC_H = 64
        WNUM = 192
        key = jax.random.key(seed)
        ks = jax.random.split(key, 16)
        return {'x': jax.random.normal(ks[0], (N, MUL0 + 3 * MUL1), jnp.float32), 'node_attr': jnp.ones((N, 1), jnp.float32), 'edge_scalars': jax.random.normal(ks[1], (E, FC_IN), jnp.float32), 'edge_attr_sh': jax.random.normal(ks[2], (E, 4), jnp.float32), 'edge_src': jax.random.randint(ks[3], (E,), 0, N), 'edge_dst': jax.random.randint(ks[4], (E,), 0, N), 'Wfc1': jax.random.normal(ks[5], (FC_IN, FC_H), jnp.float32), 'Wfc2': jax.random.normal(ks[6], (FC_H, WNUM), jnp.float32), 'Wsc0': jax.random.normal(ks[7], (MUL0, MUL0), jnp.float32), 'Wsc1': jax.random.normal(ks[8], (MUL1, MUL1), jnp.float32), 'Wl1_0': jax.random.normal(ks[9], (MUL0, MUL0), jnp.float32), 'Wl1_1': jax.random.normal(ks[10], (MUL1, MUL1), jnp.float32), 'Wl2_s': jax.random.normal(ks[11], (MUL0 + MUL1, MUL0), jnp.float32), 'Wl2_v': jax.random.normal(ks[12], (MUL0 + MUL1, MUL1), jnp.float32), 'Wa': 0.1 * jax.random.normal(ks[13], (MUL0 + MUL1, 1), jnp.float32)}
    _L3_gnn_all = _L3_gnn_setup()
    _L3_gnn_in = {k: v for k, v in _L3_gnn_all.items() if k in ('Wfc1', 'Wfc2', 'Wsc0', 'Wsc1', 'Wl1_0', 'Wl1_1', 'Wl2_s', 'Wl2_v', 'Wa')}
    del _L3_gnn_all
    return {'x': x, 'src': src, 'dst': dst, 'edge_attr_12': edge_attr_12, 'edge_attr_16': edge_attr_16, 'edge_attr_32': edge_attr_32, 'edge_attr_4': edge_attr_4, 'node_vec1': node_vec1, 'L0_gnn_W1': _L0_gnn_in['W1'], 'L0_gnn_W2': _L0_gnn_in['W2'], 'L0_gnn_W3': _L0_gnn_in['W3'], 'L0_gnn_W4': _L0_gnn_in['W4'], 'L0_gnn_Wm': _L0_gnn_in['Wm'], 'L0_gnn_bm': _L0_gnn_in['bm'], 'L0_gnn_Wu': _L0_gnn_in['Wu'], 'L0_gnn_bu': _L0_gnn_in['bu'], 'L1_gnn_W_sc0': _L1_gnn_in['W_sc0'], 'L1_gnn_W_sc1': _L1_gnn_in['W_sc1'], 'L1_gnn_W_l1_0': _L1_gnn_in['W_l1_0'], 'L1_gnn_W_l1_1': _L1_gnn_in['W_l1_1'], 'L1_gnn_W_fc1': _L1_gnn_in['W_fc1'], 'L1_gnn_W_fc2': _L1_gnn_in['W_fc2'], 'L1_gnn_W_l2_0': _L1_gnn_in['W_l2_0'], 'L1_gnn_W_l2_1': _L1_gnn_in['W_l2_1'], 'L2_gnn_W_sc0': _L2_gnn_in['W_sc0'], 'L2_gnn_W_sc1': _L2_gnn_in['W_sc1'], 'L2_gnn_W_l1_0': _L2_gnn_in['W_l1_0'], 'L2_gnn_W_l1_1': _L2_gnn_in['W_l1_1'], 'L2_gnn_fc_W1': _L2_gnn_in['fc_W1'], 'L2_gnn_fc_W2': _L2_gnn_in['fc_W2'], 'L2_gnn_W_l2_0': _L2_gnn_in['W_l2_0'], 'L2_gnn_W_l2_1': _L2_gnn_in['W_l2_1'], 'L3_gnn_Wfc1': _L3_gnn_in['Wfc1'], 'L3_gnn_Wfc2': _L3_gnn_in['Wfc2'], 'L3_gnn_Wsc0': _L3_gnn_in['Wsc0'], 'L3_gnn_Wsc1': _L3_gnn_in['Wsc1'], 'L3_gnn_Wl1_0': _L3_gnn_in['Wl1_0'], 'L3_gnn_Wl1_1': _L3_gnn_in['Wl1_1'], 'L3_gnn_Wl2_s': _L3_gnn_in['Wl2_s'], 'L3_gnn_Wl2_v': _L3_gnn_in['Wl2_v'], 'L3_gnn_Wa': _L3_gnn_in['Wa']}

def reference(x, src, dst, edge_attr_12, edge_attr_16, edge_attr_32, edge_attr_4, node_vec1, L0_gnn_W1, L0_gnn_W2, L0_gnn_W3, L0_gnn_W4, L0_gnn_Wm, L0_gnn_bm, L0_gnn_Wu, L0_gnn_bu, L1_gnn_W_sc0, L1_gnn_W_sc1, L1_gnn_W_l1_0, L1_gnn_W_l1_1, L1_gnn_W_fc1, L1_gnn_W_fc2, L1_gnn_W_l2_0, L1_gnn_W_l2_1, L2_gnn_W_sc0, L2_gnn_W_sc1, L2_gnn_W_l1_0, L2_gnn_W_l1_1, L2_gnn_fc_W1, L2_gnn_fc_W2, L2_gnn_W_l2_0, L2_gnn_W_l2_1, L3_gnn_Wfc1, L3_gnn_Wfc2, L3_gnn_Wsc0, L3_gnn_Wsc1, L3_gnn_Wl1_0, L3_gnn_Wl1_1, L3_gnn_Wl2_s, L3_gnn_Wl2_v, L3_gnn_Wa):
    import jax
    import jax.numpy as jnp

    def _L0_gnn_ref(node_features, edge_index, edge_attr_tensor, node_attr_scalar_raw, W1, W2, W3, W4, Wm, bm, Wu, bu):
        import jax, jax.numpy as jnp
        import numpy as np
        MUL0_N, MUL1_N = (64, 32)
        MUL0_E, MUL1_E = (8, 8)
        MUL0_H, MUL1_H = (64, 32)
        N_NODES, N_EDGES = (50000, 25000)
        D_NODE = MUL0_N + 3 * MUL1_N
        D_EDGE = MUL0_E + 3 * MUL1_E
        D_HID = MUL0_H + 3 * MUL1_H

        def _split(x, mul0, mul1):
            s = x[..., :mul0]
            v = x[..., mul0:].reshape(x.shape[0], mul1, 3)
            return (s, v)

        def fctp_messages(x, e, W1, W2, W3, W4):
            xs, xv = _split(x, MUL0_N, MUL1_N)
            es, ev = _split(e, MUL0_E, MUL1_E)
            inv_sqrt2 = 1.0 / np.sqrt(2.0)
            s1 = jnp.einsum('ea,eb,abc->ec', xs, es, W1) * (1.0 / np.sqrt(MUL0_N * MUL0_E))
            s2 = jnp.einsum('eai,ebi,abc->ec', xv, ev, W2) * (1.0 / (np.sqrt(3.0) * np.sqrt(MUL1_N * MUL1_E)))
            out_s = (s1 + s2) * inv_sqrt2
            v1 = jnp.einsum('ea,ebi,abc->eci', xs, ev, W3) * (1.0 / np.sqrt(MUL0_N * MUL1_E))
            v2 = jnp.einsum('eai,eb,abc->eci', xv, es, W4) * (1.0 / np.sqrt(MUL1_N * MUL0_E))
            out_v = (v1 + v2) * inv_sqrt2
            return jnp.concatenate([out_s, out_v.reshape(out_v.shape[0], -1)], axis=-1)
        row, col = (edge_index[0], edge_index[1])
        tp = fctp_messages(node_features[col], edge_attr_tensor, W1, W2, W3, W4)
        messages = tp @ Wm + bm
        agg = jax.ops.segment_sum(messages, row, num_segments=N_NODES)
        upd = jnp.concatenate([node_features, agg], axis=-1) @ Wu + bu
        return node_features + upd

    def _L1_gnn_ref(node_input, node_attr, edge_src, edge_dst, edge_attr, edge_features, W_sc0, W_sc1, W_l1_0, W_l1_1, W_fc1, W_fc2, W_l2_0, W_l2_1):
        import jax, jax.numpy as jnp
        import numpy as np
        N = 50000
        E = 12500
        MUL0 = 64
        MUL1 = 32
        NEF = 12
        RN = 100
        NUM_NEIGHBORS = 8.0
        WNUM = MUL0 + MUL0 + MUL1 + MUL1

        def _split(x):
            return (x[:, :MUL0], x[:, MUL0:].reshape(-1, MUL1, 3))

        def _fctp_scalar_attr(x0, x1, z, Ws, Wv):
            s = x0 @ Ws * z / np.sqrt(Ws.shape[0])
            v = jnp.einsum('nuc,uw->nwc', x1, Wv) * z[:, :, None] / np.sqrt(Wv.shape[0])
            return (s, v)
        x0, x1 = _split(node_input)
        z = node_attr
        s0, s1 = _fctp_scalar_attr(x0, x1, z, W_sc0, W_sc1)
        h0, h1 = _fctp_scalar_attr(x0, x1, z, W_l1_0, W_l1_1)
        h = jax.nn.silu(edge_features @ W_fc1 / np.sqrt(NEF))
        w = h @ W_fc2 / np.sqrt(RN)
        w0 = w[:, :MUL0]
        w1 = w[:, MUL0:2 * MUL0]
        w2 = w[:, 2 * MUL0:2 * MUL0 + MUL1]
        w3 = w[:, 2 * MUL0 + MUL1:]
        e0 = h0[edge_src]
        e1 = h1[edge_src]
        y0 = edge_attr[:, :1]
        y1 = edge_attr[:, 1:]
        m0a = w0 * e0 * y0
        m0b = w3 * jnp.einsum('eui,ei->eu', e1, y1) / np.sqrt(3.0)
        m1a = (w1 * e0)[:, :, None] * y1[:, None, :]
        m1b = w2[:, :, None] * (e1 * y0[:, :, None])
        mid_s = jnp.concatenate([m0a, m0b], axis=1)
        mid_v = jnp.concatenate([m1a, m1b], axis=1)
        inv = 1.0 / np.sqrt(NUM_NEIGHBORS)
        ns = jax.ops.segment_sum(mid_s, edge_dst, num_segments=N) * inv
        nv = jax.ops.segment_sum(mid_v, edge_dst, num_segments=N) * inv
        o0, o1 = _fctp_scalar_attr(ns, nv, z, W_l2_0, W_l2_1)
        c_s, c_x = (np.sin(np.pi / 8), np.cos(np.pi / 8))
        out0 = c_s * s0 + c_x * o0
        out1 = c_s * s1 + c_x * o1
        return jnp.concatenate([out0, out1.reshape(N, -1)], axis=1)

    def _L2_gnn_ref(node_input, node_attr, edge_src, edge_dst, edge_attr, edge_length_embedded, W_sc0, W_sc1, W_l1_0, W_l1_1, fc_W1, fc_W2, W_l2_0, W_l2_1):
        import jax, jax.numpy as jnp
        import numpy as np
        import math
        N = 50000
        E = 15625
        MUL0 = 64
        MUL1 = 32
        MID = MUL0 + MUL1
        FC_IN = 16
        FC_H = 64
        WEIGHT_NUMEL = 2 * MUL0 + 2 * MUL1
        NUM_NEIGH = 10.0
        C_S = math.sin(math.pi / 8.0)
        C_X = math.cos(math.pi / 8.0)
        n = node_input.shape[0]
        x0 = node_input[:, :MUL0]
        x1 = node_input[:, MUL0:].reshape(n, MUL1, 3)
        a = node_attr
        inv0 = 1.0 / math.sqrt(MUL0)
        inv1 = 1.0 / math.sqrt(MUL1)
        s0 = x0 @ W_sc0 * a * inv0
        s1 = jnp.einsum('nuc,uv->nvc', x1, W_sc1) * a[:, :, None] * inv1
        y0 = x0 @ W_l1_0 * a * inv0
        y1 = jnp.einsum('nuc,uv->nvc', x1, W_l1_1) * a[:, :, None] * inv1
        h = jax.nn.silu(edge_length_embedded @ fc_W1 * (1.0 / math.sqrt(FC_IN)))
        w = h @ fc_W2 * (1.0 / math.sqrt(FC_H))
        w_a = w[:, :MUL0]
        w_b = w[:, MUL0:2 * MUL0]
        w_c = w[:, 2 * MUL0:2 * MUL0 + MUL1]
        w_d = w[:, 2 * MUL0 + MUL1:]
        ys0 = y0[edge_src]
        ys1 = y1[edge_src]
        e0 = edge_attr[:, :1]
        e1 = edge_attr[:, 1:]
        mid_a = w_a * ys0 * e0
        mid_d = w_d * jnp.einsum('euc,ec->eu', ys1, e1) * (1.0 / math.sqrt(3.0))
        mid_b = (w_b * ys0)[:, :, None] * e1[:, None, :]
        mid_c = (w_c * e0)[:, :, None] * ys1
        mid0 = jnp.concatenate([mid_a, mid_d], axis=1)
        mid1 = jnp.concatenate([mid_b, mid_c], axis=1)
        inv_nb = 1.0 / math.sqrt(NUM_NEIGH)
        z0 = jnp.zeros((n, MID), mid0.dtype).at[edge_dst].add(mid0) * inv_nb
        z1 = jnp.zeros((n, MID, 3), mid1.dtype).at[edge_dst].add(mid1) * inv_nb
        inv_mid = 1.0 / math.sqrt(MID)
        o0 = z0 @ W_l2_0 * a * inv_mid
        o1 = jnp.einsum('nuc,uv->nvc', z1, W_l2_1) * a[:, :, None] * inv_mid
        out0 = C_S * s0 + C_X * o0
        out1 = C_S * s1 + C_X * o1
        return jnp.concatenate([out0, out1.reshape(n, MUL1 * 3)], axis=1)

    def _L3_gnn_ref(x, node_attr, edge_scalars, edge_attr_sh, edge_src, edge_dst, Wfc1, Wfc2, Wsc0, Wsc1, Wl1_0, Wl1_1, Wl2_s, Wl2_v, Wa):
        import jax, jax.numpy as jnp
        import numpy as np
        N = 625
        E = 10000
        MUL0 = 64
        MUL1 = 32
        FC_IN = 16
        FC_H = 64
        WNUM = 192
        n = x.shape[0]
        x0 = x[:, :MUL0]
        x1 = x[:, MUL0:].reshape(n, MUL1, 3)
        a = node_attr
        h = jax.nn.silu(edge_scalars @ (Wfc1 / jnp.sqrt(jnp.float32(FC_IN))))
        w = h @ (Wfc2 / jnp.sqrt(jnp.float32(FC_H)))
        w0 = w[:, :64]
        w1 = w[:, 64:128]
        w2 = w[:, 128:160]
        w3 = w[:, 160:192]
        inv8 = 1.0 / jnp.sqrt(jnp.float32(MUL0))
        inv32 = 1.0 / jnp.sqrt(jnp.float32(MUL1))
        sc = jnp.concatenate([x0 @ Wsc0 * a * inv8, (jnp.einsum('num,uv->nvm', x1, Wsc1) * a[..., None] * inv32).reshape(n, 3 * MUL1)], axis=1)
        f0 = x0 @ Wl1_0 * a * inv8
        f1 = jnp.einsum('num,uv->nvm', x1, Wl1_1) * a[..., None] * inv32
        e0 = f0[edge_src]
        e1 = f1[edge_src]
        sh0 = edge_attr_sh[:, :1]
        sh1 = edge_attr_sh[:, 1:4]
        mid0 = w0 * e0 * sh0
        mid1 = w3 * jnp.einsum('eum,em->eu', e1, sh1) / jnp.sqrt(3.0)
        mid2 = w1[:, :, None] * e0[:, :, None] * sh1[:, None, :]
        mid3 = w2[:, :, None] * e1 * sh0[:, :, None]
        cnt = jnp.clip(jax.ops.segment_sum(jnp.ones(edge_dst.shape, x.dtype), edge_dst, num_segments=n), 1.0)

        def smean(v):
            s = jax.ops.segment_sum(v, edge_dst, num_segments=n)
            return s / cnt.reshape((n,) + (1,) * (v.ndim - 1))
        n0, n1 = (smean(mid0), smean(mid1))
        n2, n3 = (smean(mid2), smean(mid3))
        scal = jnp.concatenate([n0, n1], axis=1)
        vec = jnp.concatenate([n2, n3], axis=1)
        inv96 = 1.0 / jnp.sqrt(jnp.float32(MUL0 + MUL1))
        alpha = scal @ Wa * a * inv96
        out_s = scal @ Wl2_s * a * inv96
        out_v = jnp.einsum('num,uv->nvm', vec, Wl2_v) * a[..., None] * inv96
        conv = jnp.concatenate([out_s, out_v.reshape(n, 3 * MUL1)], axis=1)
        return sc + alpha * conv
    edge_index = jnp.stack([src, dst])
    x = _layernorm(x + _L0_gnn_ref(x, edge_index, edge_attr_32, node_vec1, L0_gnn_W1, L0_gnn_W2, L0_gnn_W3, L0_gnn_W4, L0_gnn_Wm, L0_gnn_bm, L0_gnn_Wu, L0_gnn_bu), axis=-1)
    x = _layernorm(x + _L1_gnn_ref(x, node_vec1, src, dst, edge_attr_4, edge_attr_12, L1_gnn_W_sc0, L1_gnn_W_sc1, L1_gnn_W_l1_0, L1_gnn_W_l1_1, L1_gnn_W_fc1, L1_gnn_W_fc2, L1_gnn_W_l2_0, L1_gnn_W_l2_1), axis=-1)
    x = _layernorm(x + _L2_gnn_ref(x, node_vec1, src, dst, edge_attr_4, edge_attr_16, L2_gnn_W_sc0, L2_gnn_W_sc1, L2_gnn_W_l1_0, L2_gnn_W_l1_1, L2_gnn_fc_W1, L2_gnn_fc_W2, L2_gnn_W_l2_0, L2_gnn_W_l2_1), axis=-1)
    x = _layernorm(x + _L3_gnn_ref(x, node_vec1, edge_attr_16, edge_attr_4, src, dst, L3_gnn_Wfc1, L3_gnn_Wfc2, L3_gnn_Wsc0, L3_gnn_Wsc1, L3_gnn_Wl1_0, L3_gnn_Wl1_1, L3_gnn_Wl2_s, L3_gnn_Wl2_v, L3_gnn_Wa), axis=-1)
    return x

_drawn_inputs = setup_inputs


def setup_inputs(seed=0):
    import zlib

    import numpy as np

    out = dict(_drawn_inputs(seed))
    spreads = {'L0_gnn_bm': (0.0, 0.1), 'L0_gnn_bu': (0.0, 0.1)}
    factors = {'L3_gnn_Wfc1': 6.633,
     'L3_gnn_Wfc2': 6.326,
     'L3_gnn_Wl1_0': 6.378,
     'L3_gnn_Wl1_1': 8.0,
     'L3_gnn_Wl2_s': 8.0,
     'L3_gnn_Wl2_v': 8.0,
     'L3_gnn_Wa': 6.538}
    for name, (base, spread) in spreads.items():
        noise = np.random.default_rng([zlib.crc32(name.encode()), seed]).standard_normal(out[name].shape)
        drawn = base * np.exp(spread * noise) if base else spread * noise
        out[name] = jnp.asarray(drawn.astype(out[name].dtype))
    for name, factor in factors.items():
        out[name] = (out[name] * factor).astype(out[name].dtype)
    return out
```

```python
import math

import concourse.bass as bass
from concourse import mybir
from contextlib import ExitStack

F32 = mybir.dt.float32
I32 = mybir.dt.int32
ALU = mybir.AluOpType
ACT = mybir.ActivationFunctionType

ROWS = 50000
P = 128
QUAD = 4 * P
STEP = 2 * QUAD
TURNS = -(-ROWS // STEP)
PADDED = TURNS * STEP
QUADS = PADDED // QUAD
PAIRS = 4 * TURNS
NS, NV = 64, 32
D = NS + 3 * NV
EB = 8
SPARE = PADDED
ACC_ROWS = PADDED + 2 * P
REPEAT = 1024.0


def need(eng, sem, value):
    if isinstance(value, int) and value <= 0:
        return
    eng.wait_ge(sem, value)


def turns(eng, body):
    body(0)
    with eng.Fori(1, TURNS - 1) as i:
        body(i)
    body(TURNS - 1)


class Chain:

    def __init__(self, eng, sem, per_unit):
        self.eng, self.sem, self.per_unit = eng, sem, per_unit
        self.unit, self.count = 0, per_unit

    def start(self, unit):
        assert self.count == self.per_unit, self.count
        self.unit, self.count = unit, 0

    def did(self, instruction):
        instruction.then_inc(self.sem, 1)
        self.count += 1
        return self.count

    def wait(self, count):
        need(self.eng, self.sem, self.unit * self.per_unit + count)


def prepare_weights(nc, w, dram):
    with ExitStack() as ctx:
        sem = lambda name: ctx.enter_context(nc.semaphore(name))
        loaded, ready, folded, masks, mm = (sem(n) for n in ("w_loaded", "w_ready", "w_folded", "w_masks", "w_product"))
        prod = ctx.enter_context(nc.psum_tensor("prod", [P, 2, 512], F32))
        block = ctx.enter_context(nc.Block())
        loads = [(w[name], dram[name]) for name in w["loads"]]

        @block.sync
        def _(sp):
            for dst, src in loads:
                sp.dma_start(dst[:, :], src).then_inc(loaded, 16)

        @block.vector
        def _(dve):
            nc.vector.memset(w["ident"][:, :], 0.0)
            nc.vector.memset(w["zeros"][:, :], 0.0)
            nc.vector.memset(w["tp"][:, :, :, :], 1.0)
            nc.vector.memset(w["eps"][:, :], 1e-5)
            nc.vector.memset(w["mask"][:, :, :], 1.0).then_inc(ready, 1)
            dve.wait_ge(loaded, 16 * len(loads))
            for name, rows, cols, factor in w["factors"]:
                part = w[name][rows[0]:rows[1], cols[0]:cols[1]]
                nc.vector.tensor_scalar(part, part, factor, None, ALU.mult).then_inc(folded, 1)
            dve.wait_ge(mm, 1)
            nc.vector.tensor_copy(w["l0_out_a"][:, :], prod[:, 0, 0:D])
            nc.vector.tensor_copy(w["l0_out_b"][:, :], prod[0:NV + 1, 1, 0:D]).then_inc(folded, 1)

        @block.tensor
        def _(pe):
            pe.wait_ge(loaded, 16 * len(loads))
            for k, rows in ((0, P), (1, NV + 1)):
                cols = slice(k * P, k * P + rows)
                nc.tensor.matmul(prod[0:rows, k, 0:D], w["wm_t_a"][:, cols], w["wu2_a"][:, :], start=True, stop=False)
                last = nc.tensor.matmul(prod[0:rows, k, 0:D], w["wm_t_b"][:, cols], w["wu2_b"][:, :], start=False, stop=True)
            last.then_inc(mm, 1)

        @block.gpsimd
        def _(pool):
            pool.wait_ge(ready, 1)
            pool.affine_select(out=w["ident"][:, :], in_=w["ident"][:, :], compare_op=ALU.not_equal, fill=1.0,
                               base=0, pattern=[[-1, P]], channel_multiplier=1)
            pool.affine_select(out=w["mask"][:, 0, :], in_=w["mask"][:, 0, :], compare_op=ALU.is_ge, fill=REPEAT + 1,
                               base=0, pattern=[[1, 2 * P]], channel_multiplier=-1)
            pool.affine_select(out=w["mask"][:, 1, :], in_=w["mask"][:, 1, :], compare_op=ALU.is_ge, fill=REPEAT + 1,
                               base=-P, pattern=[[1, 2 * P]], channel_multiplier=-1)
            pool.iota(w["spare"][:, :], pattern=[[P, 2]], base=SPARE, channel_multiplier=1).then_inc(masks, 1)
            pool.wait_ge(masks, 1)
            pool.wait_ge(folded, len(w["factors"]) + 1)


def zero_accumulator(nc, w, acc, width):
    with ExitStack() as ctx:
        zeroed = ctx.enter_context(nc.semaphore("zeroed"))
        block = ctx.enter_context(nc.Block())

        @block.sync
        def _(sp):
            for n in range(TURNS):
                sp.dma_start(acc[n * STEP:(n + 1) * STEP, :].rearrange("(p r) c -> p (r c)", p=P),
                             w["zeros"][:, 0:8 * width]).then_inc(zeroed, 16)
            sp.dma_start(acc[PADDED:ACC_ROWS, :].rearrange("(p r) c -> p (r c)", p=P),
                         w["zeros"][:, 0:2 * width]).then_inc(zeroed, 16)
            sp.wait_ge(zeroed, 16 * (TURNS + 1))


def edge_layer0(nc, w, dram, x, acc, next_acc, next_width):
    with ExitStack() as ctx:
        sem = lambda name: ctx.enter_context(nc.semaphore("a_" + name))
        sb = lambda name, shape, dt=F32: ctx.enter_context(nc.sbuf_tensor("a_" + name, shape, dt))
        pb = lambda name: ctx.enter_context(nc.psum_tensor("a_" + name, [P, 512], F32))
        target_row = sb("target_row", [P, 2, QUAD], I32)
        index = sb("index", [P, 2, 8], I32)
        attr = sb("attr", [P, 2, 4, 4 * EB])
        rows = sb("rows", [P, 4, 2, D])
        xt = sb("xt", [P, 2, 2, 2 * P])
        dp = sb("dp", [P, 3, EB, NV])
        dot = sb("dot", [P, 2, EB * NV])
        dsum = sb("dsum", [P, EB * NV])
        dott = sb("dott", [P, 2, 2, P])
        mac = sb("mac", [P, 2, 2, D])
        vprod = sb("vprod", [P, 2, 3, EB, NV])
        vsum = sb("vsum", [P, 2, 3 * NV])
        tp = w["tp"]
        same_a = sb("same_a", [P, 2, P])
        same_b = sb("same_b", [P, 2, 2 * P])
        hits = sb("hits", [P, 2, 2 * P])
        seen = sb("seen", [P, 2, 2])
        away = sb("away", [P, 2, 2])
        move = sb("move", [P, 2, 2])
        slot = sb("slot", [P, 2, 2], I32)
        zt = sb("zt", [P, 2, 2, 2 * P])
        out = sb("out", [P, 2, 2, D])
        tb = [pb(f"t{k}") for k in range(4)]
        p_xt, p_dt, p_z, p_out = pb("p_xt"), pb("p_dt"), pb("p_z"), pb("p_out")

        loaded = [sem(f"loaded{c}") for c in range(2)]
        gathered = [sem(f"gathered{j}") for j in range(4)]
        zeroed = sem("zeroed")
        xt_ready, xt_copied = sem("xt_ready"), sem("xt_copied")
        dot_steps, dot_ready = sem("dot_steps"), sem("dot_ready")
        dt_ready, dt_copied = sem("dt_ready"), sem("dt_copied")
        bank_ready = [sem(f"bank_ready{k}") for k in range(4)]
        bank_read = [sem(f"bank_read{k}") for k in range(4)]
        s2_ready, s2_read = sem("s2_ready"), sem("s2_read")
        steps = sem("steps")
        pair_done = sem("pair_done")
        z_ready, z_copied = sem("z_ready"), sem("z_copied")
        out_ready, rows_ready = sem("out_ready"), sem("rows_ready")
        scattered = sem("scattered")
        block = ctx.enter_context(nc.Block())

        @block.sync
        def _(sp):
            def turn(i):
                for c in range(2):
                    q = 2 * i + c
                    need(sp, pair_done, 2 * q - 2)
                    sp.nop(nofuse=True)
                    sp.dma_start(target_row[:, c, :], dram["src_row"][bass.ds(q, 1), :].to_broadcast([P, QUAD])).then_inc(loaded[c], 16)
                    sp.dma_start(index[:, c, :], dram["index0"][bass.ds(q * P, P), :]).then_inc(loaded[c], 16)
                    sp.dma_start(attr[:, c, :, :].rearrange("p t k -> p (t k)"), dram["attr32"][bass.ds(q * P, P), :]).then_inc(loaded[c], 16)
                sp.dma_start(next_acc[bass.ds(i * STEP, STEP), :].rearrange("(p r) c -> p (r c)", p=P),
                             w["zeros"][:, 0:8 * next_width]).then_inc(zeroed, 16)
            turns(sp, turn)
            sp.dma_start(next_acc[PADDED:ACC_ROWS, :].rearrange("(p r) c -> p (r c)", p=P),
                         w["zeros"][:, 0:2 * next_width]).then_inc(zeroed, 16)
            sp.wait_ge(zeroed, 16 * (TURNS + 1))

        @block.gpsimd
        def _(pool):
            chain = Chain(pool, dot_steps, 3)

            def gather(i, j):
                if isinstance(i, int) and 4 * i + j >= PAIRS:
                    return
                j, i = j % 4, i + j // 4
                c, r = j // 2, j % 2
                need(pool, dt_ready, 2 * (4 * i + j) - 6)
                pool.wait_ge(loaded[c], 48 * (i + 1))
                for t in range(2):
                    pool.nop(nofuse=True)
                    pool.indirect_dma_start(rows[:, j, t, :], None, x,
                                            bass.IndirectOffsetOnAxis(ap=index[:, c, 2 * r + t:2 * r + t + 1], axis=0)
                                            ).then_inc(gathered[j], 16)

            def scatter(i, j):
                if isinstance(i, int) and 4 * i + j < 0:
                    return
                need(pool, scattered, 32 * (4 * i + j))
                pool.wait_ge(rows_ready, 4 * i + j + 1)
                for t in range(2):
                    pool.nop(nofuse=True)
                    pool.indirect_dma_start(acc, bass.IndirectOffsetOnAxis(ap=slot[:, j % 2, t:t + 1], axis=0),
                                            out[:, j % 2, t, :], None, compute_op=ALU.add).then_inc(scattered, 16)

            def dots(i, j):
                c, r = j // 2, j % 2
                pool.wait_ge(gathered[j], 32 * (i + 1))
                for t in range(2):
                    m = 8 * i + 2 * j + t
                    chain.start(m)
                    need(pool, dt_ready, m - 1)
                    chain.wait(0)
                    ev = attr[:, c, 2 * r + t, EB:].rearrange("p (k b) -> p k b", k=3)
                    xv = rows[:, j, t, NS:].rearrange("p (k a) -> p k a", k=3)
                    n = chain.did(nc.gpsimd.tensor_tensor(dp[:, :, :, :], xv.unsqueeze(2).to_broadcast([P, 3, EB, NV]),
                                                          ev.unsqueeze(3).to_broadcast([P, 3, EB, NV]), ALU.mult))
                    chain.wait(n)
                    flat = dp[:, :, :, :].rearrange("p k b a -> p k (b a)")
                    n = chain.did(nc.gpsimd.tensor_tensor(dsum[:, :], flat[:, 0, :], flat[:, 1, :], ALU.add))
                    chain.wait(n)
                    last = nc.gpsimd.tensor_tensor(dot[:, t, :], dsum[:, :], flat[:, 2, :], ALU.add)
                    chain.did(last)

            def turn(i):
                for j in range(4):
                    gather(i, j + 2)
                    dots(i, j)
                    scatter(i, j - 1)
            gather(0, 0)
            gather(0, 1)
            turns(pool, turn)
            scatter(TURNS - 1, 3)
            pool.wait_ge(scattered, 32 * PAIRS)

        @block.scalar
        def _(act):
            def copy_xt(i, j):
                if isinstance(i, int) and 4 * i + j >= PAIRS:
                    return
                j, i = j % 4, i + j // 4
                need(act, bank_ready[2], 2 * (4 * i + j) - 2)
                act.wait_ge(xt_ready, 4 * i + j + 1)
                nc.scalar.copy(xt[:, j % 2, 0, :], p_xt[:, 0:2 * P])
                nc.scalar.copy(xt[0:NV, j % 2, 1, :], p_xt[0:NV, 2 * P:]).then_inc(xt_copied, 1)

            def copy_dott(i, j, t):
                n = 8 * i + 2 * j + t
                need(act, s2_ready, n - 1)
                act.wait_ge(dt_ready, n + 1)
                nc.scalar.copy(dott[:, t, :, :].rearrange("p k e -> p (k e)"), p_dt[:, 0:2 * P]).then_inc(dt_copied, 1)

            def copy_z(i, j):
                n = 4 * i + j
                if isinstance(i, int) and n < 0:
                    return
                need(act, out_ready, n - 1)
                act.wait_ge(z_ready, n + 1)
                nc.scalar.copy(zt[:, j % 2, 0, :], p_z[:, 0:2 * P])
                nc.scalar.copy(zt[0:NV + 1, j % 2, 1, :], p_z[0:NV + 1, 2 * P:]).then_inc(z_copied, 1)

            def copy_out(i, j):
                n = 4 * i + j
                if isinstance(i, int) and n < 0:
                    return
                need(act, scattered, 32 * (n - 1))
                act.wait_ge(out_ready, n + 1)
                nc.scalar.copy(out[:, j % 2, :, :].rearrange("p t c -> p (t c)"), p_out[:, 0:2 * D]).then_inc(rows_ready, 1)

            def turn(i):
                for j in range(4):
                    copy_dott(i, j, 0)
                    copy_xt(i, j + 1)
                    copy_z(i, j - 1)
                    copy_dott(i, j, 1)
                    copy_out(i, j - 1)
            copy_xt(0, 0)
            turns(act, turn)
            copy_z(TURNS - 1, 3)
            copy_out(TURNS - 1, 3)

        @block.vector
        def _(dve):
            chain = Chain(dve, steps, 16)

            def pair(i, j):
                c, r, s = j // 2, j % 2, j % 2
                n = 4 * i + j
                chain.start(n)
                dve.wait_ge(loaded[c], 48 * (i + 1))
                need(dve, pair_done, n)
                need(dve, z_ready, n - 1)
                need(dve, scattered, 32 * (n - 1))
                mine = index[:, c, 4 + 2 * r:6 + 2 * r]
                pair_row = target_row[:, c, 2 * P * r:2 * P * (r + 1)]
                for t in range(2):
                    ins = nc.vector.scalar_tensor_tensor(hits[:, t, :], pair_row, mine[:, t:t + 1], w["mask"][:, t, :],
                                                         ALU.is_equal, ALU.mult, accum_out=seen[:, s, t:t + 1])
                chain.did(ins)
                k = chain.did(nc.vector.tensor_tensor(away[:, s, :], w["spare"][:, :], mine, ALU.subtract))
                nc.vector.tensor_scalar(same_a[:, s, :], pair_row[:, 0:P], mine[:, 0:1], None, ALU.is_equal)
                nc.vector.tensor_scalar(same_b[:, s, :], pair_row, mine[:, 1:2], None, ALU.is_equal)
                chain.wait(k)
                k_move = chain.did(nc.vector.scalar_tensor_tensor(move[:, s, :], seen[:, s, :], REPEAT, away[:, s, :],
                                                                  ALU.is_ge, ALU.mult))
                for t in range(2):
                    m = 2 * n + t
                    a = attr[:, c, 2 * r + t, :]

                    def scaled(b):
                        bank, at = tb[b // 3], D * (b % 3)
                        if b == 0:
                            return nc.vector.tensor_scalar(mac[:, t, 0, :], bank[:, at:at + D], a[:, 0:1], None, ALU.mult)
                        return nc.vector.scalar_tensor_tensor(mac[:, t, b % 2, :], bank[:, at:at + D], a[:, b:b + 1],
                                                              mac[:, t, (b + 1) % 2, :], ALU.mult, ALU.add)
                    dve.wait_ge(bank_ready[0], m + 1)
                    k = chain.did(scaled(0))
                    dve.wait_ge(bank_ready[3], m + 1)
                    t3 = tb[3][:, 0:EB * NV].rearrange("p (b c) -> p b c", b=EB)
                    ev = a[:, EB:].rearrange("p (k b) -> p k b", k=3)
                    nc.vector.tensor_tensor(vprod[:, t, :, :, :], t3.unsqueeze(1).to_broadcast([P, 3, EB, NV]),
                                            ev.unsqueeze(3).to_broadcast([P, 3, EB, NV]), ALU.mult).then_inc(bank_read[3], 1)
                    chain.wait(k)
                    k = chain.did(scaled(1))
                    if t == 0:
                        chain.wait(k_move)
                        nc.vector.tensor_tensor(slot[:, s, :], move[:, s, :], mine, ALU.add)
                    chain.wait(k)
                    scaled(2).then_inc(bank_read[0], 1)
                    dve.wait_ge(bank_read[3], m + 1)
                    k_sum = chain.did(nc.vector.tensor_reduce(vsum[:, t, :].rearrange("p (k c) -> p k c", k=3),
                                                              vprod[:, t, :, :, :].rearrange("p k b c -> p k c b"),
                                                              mybir.AxisListType.X, ALU.add))
                    dve.wait_ge(bank_ready[1], m + 1)
                    dve.wait_ge(bank_read[0], m + 1)
                    k = chain.did(scaled(3))
                    chain.wait(k)
                    k = chain.did(scaled(4))
                    chain.wait(k)
                    scaled(5).then_inc(bank_read[1], 1)
                    dve.wait_ge(bank_ready[2], m + 1)
                    dve.wait_ge(bank_read[1], m + 1)
                    k = chain.did(scaled(6))
                    chain.wait(k)
                    scaled(7).then_inc(bank_read[2], 1)
                    dve.wait_ge(s2_ready, m + 1)
                    dve.wait_ge(bank_read[2], m + 1)
                    nc.vector.tensor_tensor(tp[:, s, t, 0:NS], mac[:, t, 1, 0:NS], tb[3][:, 256:256 + NS], ALU.add
                                            ).then_inc(s2_read, 1)
                    chain.wait(k_sum)
                    ins = nc.vector.tensor_tensor(tp[:, s, t, NS:D], mac[:, t, 1, NS:D], vsum[:, t, :], ALU.add)
                    if t == 0:
                        chain.did(ins)
                    else:
                        ins.then_inc(pair_done, 1)

            def turn(i):
                for j in range(4):
                    pair(i, j)
            turns(dve, turn)

        @block.tensor
        def _(pe):
            def transpose_x(i, j):
                if isinstance(i, int) and 4 * i + j >= PAIRS:
                    return
                j, i = j % 4, i + j // 4
                need(pe, xt_copied, 4 * i + j)
                pe.wait_ge(gathered[j], 32 * (i + 1))
                for t in range(2):
                    nc.tensor.transpose(p_xt[:, t * P:(t + 1) * P], rows[:, j, t, 0:P], w["ident"][:, :])
                    last = nc.tensor.transpose(p_xt[0:NV, (2 + t) * P:(3 + t) * P], rows[:, j, t, P:D], w["ident"][:, :])
                last.then_inc(xt_ready, 1)

            def transpose_dot(i, j, t):
                n = 8 * i + 2 * j + t
                need(pe, dt_copied, n)
                pe.wait_ge(dot_steps, 3 * (n + 1))
                for k in range(2):
                    last = nc.tensor.transpose(p_dt[:, k * P:(k + 1) * P], dot[:, t, k * P:(k + 1) * P], w["ident"][:, :])
                last.then_inc(dt_ready, 1)

            def products(i, j, t):
                n = 8 * i + 2 * j + t
                s = j % 2
                pe.wait_ge(xt_copied, 4 * i + j + 1)
                xa = xt[:, s, 0, t * P:(t + 1) * P]
                xb = xt[0:NV, s, 1, t * P:(t + 1) * P]
                for k, nb in ((0, 3), (3, 0), (1, 3), (2, 2)):
                    need(pe, s2_read if k == 3 else bank_read[k], n)
                    if k == 3:
                        last = nc.tensor.matmul(tb[3][:, 0:EB * NV], xa[0:NS, :], w["l0_w3"][:, :], start=True, stop=True)
                    else:
                        view = tb[k][:, 0:nb * D].rearrange("p (b c) -> p b c", b=nb)
                        nc.tensor.matmul(view[:, :, 0:P], xa, w["l0_w14"][:, 3 * P * k:3 * P * k + nb * P], start=True, stop=True)
                        last = nc.tensor.matmul(view[:, :, P:D], xb, w["l0_w4"][:, 3 * NV * k:3 * NV * k + nb * NV], start=True, stop=True)
                    last.then_inc(bank_ready[k], 1)

            def scalars(i, j, t):
                n = 8 * i + 2 * j + t
                pe.wait_ge(dt_copied, n + 1)
                pe.wait_ge(bank_read[3], n + 1)
                for k in range(2):
                    last = nc.tensor.matmul(tb[3][:, 256:256 + NS], dott[:, t, k, :], w["l0_w2"][:, k * NS:(k + 1) * NS],
                                            start=(k == 0), stop=(k == 1))
                last.then_inc(s2_ready, 1)

            def sums(i, j):
                n = 4 * i + j
                if isinstance(i, int) and n < 0:
                    return
                s = j % 2
                need(pe, z_copied, n)
                pe.wait_ge(pair_done, n + 1)
                for k, (lo, hi) in enumerate(((0, P), (P, D + 1))):
                    z = p_z[0:hi - lo, 2 * P * k:2 * P * (k + 1)]
                    nc.tensor.matmul(z, tp[:, s, 1, lo:hi], same_b[:, s, :], start=True, stop=False)
                    last = nc.tensor.matmul(z[:, 0:P], tp[:, s, 0, lo:hi], same_a[:, s, :], start=False, stop=True)
                last.then_inc(z_ready, 1)

            def outputs(i, j):
                n = 4 * i + j
                if isinstance(i, int) and n < 0:
                    return
                need(pe, rows_ready, n)
                pe.wait_ge(z_copied, n + 1)
                for t in range(2):
                    o = p_out[:, t * D:(t + 1) * D]
                    nc.tensor.matmul(o, zt[:, j % 2, 0, t * P:(t + 1) * P], w["l0_out_a"][:, :], start=True, stop=False)
                    last = nc.tensor.matmul(o, zt[0:NV + 1, j % 2, 1, t * P:(t + 1) * P], w["l0_out_b"][:, :], start=False, stop=True)
                last.then_inc(out_ready, 1)

            def turn(i):
                for j in range(4):
                    products(i, j, 0)
                    transpose_dot(i, j, 0)
                    transpose_x(i, j + 1)
                    sums(i, j - 1)
                    scalars(i, j, 0)
                    products(i, j, 1)
                    transpose_dot(i, j, 1)
                    outputs(i, j - 1)
                    scalars(i, j, 1)
            transpose_x(0, 0)
            turns(pe, turn)
            sums(TURNS - 1, 3)
            outputs(TURNS - 1, 3)


def edge_conv(nc, w, dram, layer, table, acc, width, next_acc, next_width):
    conv = CONVS[layer]
    nf, hidden = conv["features"], conv["hidden"]
    find = layer == 1
    with ExitStack() as ctx:
        pre = f"c{layer}_"
        sem = lambda name: ctx.enter_context(nc.semaphore(pre + name))
        sb = lambda name, shape, dt=F32: ctx.enter_context(nc.sbuf_tensor("s_" + pre + name, shape, dt))
        pb = lambda name: ctx.enter_context(nc.psum_tensor(pre + name, [P, 512], F32))
        features = sb("features", [nf, 2, QUAD])
        target_row = sb("target_row", [P, 2, QUAD], I32)
        index = sb("index", [P, 2, 8], I32)
        attr = sb("attr", [P, 2, 4, 4])
        rows = sb("rows", [P, 4, 2, D])
        hid = sb("hid", [hidden, 2, QUAD])
        pw = sb("pw", [P, 2, 2, 2, NS])
        vw = sb("vw", [P, 2, 2, 3, NV])
        dv = sb("dv", [P, 2, 2, 3, NV])
        ds = sb("ds", [P, 2, 2, 2, NV])
        mid = sb("mid", [P, 2, 2, 3, P])
        same_a = sb("same_a", [P, 2, P])
        same_b = sb("same_b", [P, 2, 2 * P])
        hits = sb("hits", [P, 2, 2 * P])
        away = sb("away", [P, 2, 2])
        move = sb("move", [P, 2, 2])
        slot = sb("slot", [P, 2, 2], I32)
        zt = sb("zt", [P, 2, 3, 2 * P])
        out = sb("out", [P, 2, 2, width])
        p_hid = pb("p_hid")
        p_w = [pb(f"p_w{r}") for r in range(2)]
        p_z = [ctx.enter_context(nc.psum_tensor(pre + f"p_z{r}", [P, 1024], F32)) for r in range(2)]
        p_out = pb("p_out")
        off = 1 if layer == 3 else 0
        ow = off + D

        loaded = [sem(f"loaded{c}") for c in range(2)]
        gathered = [sem(f"gathered{j}") for j in range(4)]
        zeroed = sem("zeroed")
        hid_ready, silu_done = sem("hid_ready"), sem("silu_done")
        w_ready = sem("w_ready")
        steps, pair_done = sem("steps"), sem("pair_done")
        z_ready, z_copied = sem("z_ready"), sem("z_copied")
        out_ready, rows_ready = sem("out_ready"), sem("rows_ready")
        scattered = sem("scattered")
        block = ctx.enter_context(nc.Block())

        @block.sync
        def _(sp):
            def turn(i):
                for c in range(2):
                    q = 2 * i + c
                    need(sp, pair_done, 2 * q - 2)
                    sp.nop(nofuse=True)
                    need(sp, hid_ready, q - 1)
                    sp.nop(nofuse=True)
                    sp.dma_start(target_row[:, c, :], dram["dst_row"][bass.ds(q, 1), :].to_broadcast([P, QUAD])).then_inc(loaded[c], 16)
                    sp.dma_start(index[:, c, :], dram["index1"][bass.ds(q * P, P), :]).then_inc(loaded[c], 16)
                    sp.dma_start(attr[:, c, :, :].rearrange("p t k -> p (t k)"), dram["attr4"][bass.ds(q * P, P), :]).then_inc(loaded[c], 16)
                    sp.dma_start(features[:, c, :], dram[f"features{nf}"][:, bass.ds(q * QUAD, QUAD)]).then_inc(loaded[c], 16)
                if next_acc is not None:
                    sp.dma_start(next_acc[bass.ds(i * STEP, STEP), :].rearrange("(p r) c -> p (r c)", p=P),
                                 w["zeros"][:, 0:8 * next_width]).then_inc(zeroed, 16)
            turns(sp, turn)
            if next_acc is not None:
                sp.dma_start(next_acc[PADDED:ACC_ROWS, :].rearrange("(p r) c -> p (r c)", p=P),
                             w["zeros"][:, 0:2 * next_width]).then_inc(zeroed, 16)
                sp.wait_ge(zeroed, 16 * (TURNS + 1))

        @block.gpsimd
        def _(pool):
            def gather(i, j):
                if isinstance(i, int) and 4 * i + j >= PAIRS:
                    return
                j, i = j % 4, i + j // 4
                c, r = j // 2, j % 2
                need(pool, pair_done, 4 * i + j - 3)
                pool.wait_ge(loaded[c], 64 * (i + 1))
                for t in range(2):
                    pool.nop(nofuse=True)
                    pool.indirect_dma_start(rows[:, j, t, :], None, table,
                                            bass.IndirectOffsetOnAxis(ap=index[:, c, 2 * r + t:2 * r + t + 1], axis=0)
                                            ).then_inc(gathered[j], 16)

            def scatter(i, j):
                if isinstance(i, int) and 4 * i + j < 0:
                    return
                need(pool, scattered, 32 * (4 * i + j))
                pool.wait_ge(rows_ready, 4 * i + j + 1)
                for t in range(2):
                    pool.nop(nofuse=True)
                    pool.indirect_dma_start(acc, bass.IndirectOffsetOnAxis(ap=slot[:, j % 2, t:t + 1], axis=0),
                                            out[:, j % 2, t, :], None, compute_op=ALU.add).then_inc(scattered, 16)

            def turn(i):
                for j in range(4):
                    gather(i, j + 2)
                    scatter(i, j - 1)
            gather(0, 0)
            gather(0, 1)
            turns(pool, turn)
            scatter(TURNS - 1, 3)
            pool.wait_ge(scattered, 32 * PAIRS)

        @block.scalar
        def _(act):
            def silu(i, c):
                if isinstance(i, int) and 2 * i + c >= QUADS:
                    return
                c, i = c % 2, i + c // 2
                q = 2 * i + c
                need(act, w_ready, 2 * q - 2)
                act.wait_ge(hid_ready, q + 1)
                nc.scalar.activation(hid[:, c, :], p_hid[0:hidden, :], ACT.Silu, scale=1.0 / math.sqrt(nf)).then_inc(silu_done, 1)

            def copy_z(i, j):
                n = 4 * i + j
                need(act, out_ready, n - 1)
                act.wait_ge(z_ready, n + 1)
                nc.scalar.copy(zt[:, j % 2, :, :].rearrange("p k e -> p (k e)"), p_z[j % 2][:, 0:6 * P]).then_inc(z_copied, 1)

            def copy_out(i, j):
                n = 4 * i + j
                if isinstance(i, int) and n < 0:
                    return
                need(act, scattered, 32 * (n - 1))
                act.wait_ge(out_ready, n + 1)
                src = p_out[:, 0:2 * ow].rearrange("p (t c) -> p t c", t=2)
                last = nc.scalar.copy(out[:, j % 2, :, 0:ow], src)
                if layer == 3:
                    last = nc.scalar.copy(out[:, j % 2, :, D + 1:D + 2], w["seen"][:, bass.ds(2 * n, 2)].unsqueeze(2))
                last.then_inc(rows_ready, 1)

            def turn(i):
                for j in range(4):
                    if j % 2 == 0:
                        silu(i, j // 2 + 1)
                    copy_z(i, j)
                    copy_out(i, j - 1)
            silu(0, 0)
            turns(act, turn)
            copy_out(TURNS - 1, 3)

        @block.vector
        def _(dve):
            chain = Chain(dve, steps, 9 if find else 5)

            def pair(i, j):
                c, r, s = j // 2, j % 2, j % 2
                n = 4 * i + j
                chain.start(n)
                dve.wait_ge(loaded[c], 64 * (i + 1))
                need(dve, pair_done, n)
                need(dve, z_ready, n - 1)
                need(dve, scattered, 32 * (n - 1))
                mine = index[:, c, 4 + 2 * r:6 + 2 * r]
                pair_row = target_row[:, c, 2 * P * r:2 * P * (r + 1)]
                nc.vector.tensor_scalar(same_a[:, s, :], pair_row[:, 0:P], mine[:, 0:1], None, ALU.is_equal)
                nc.vector.tensor_scalar(same_b[:, s, :], pair_row, mine[:, 1:2], None, ALU.is_equal)
                if find:
                    for t in range(2):
                        last = nc.vector.scalar_tensor_tensor(hits[:, t, :], pair_row, mine[:, t:t + 1], w["mask"][:, t, :],
                                                              ALU.is_equal, ALU.mult, accum_out=w["seen"][:, bass.ds(2 * n + t, 1)])
                    chain.did(last)
                    k = chain.did(nc.vector.tensor_tensor(away[:, s, :], w["spare"][:, :], mine, ALU.subtract))
                    chain.wait(k)
                    k = chain.did(nc.vector.scalar_tensor_tensor(move[:, s, :], w["seen"][:, bass.ds(2 * n, 2)], REPEAT, away[:, s, :],
                                                                 ALU.is_ge, ALU.mult))
                    chain.wait(k)
                    k = chain.did(nc.vector.tensor_tensor(slot[:, s, :], move[:, s, :], mine, ALU.add))
                    chain.wait(k)
                    nc.vector.tensor_copy(w["slots"][:, bass.ds(2 * n, 2)], slot[:, s, :])
                else:
                    nc.vector.tensor_copy(slot[:, s, :], w["slots"][:, bass.ds(2 * n, 2)])
                dve.wait_ge(gathered[j], 32 * (i + 1))
                y = attr[:, c, 2 * r:2 * r + 2, :]
                e0 = rows[:, j, :, 0:NS]
                e1 = rows[:, j, :, NS:D].rearrange("p t (k u) -> p t k u", k=3)
                y1 = y[:, :, 1:4].unsqueeze(3)
                k_dv = chain.did(nc.vector.tensor_tensor(dv[:, s], e1, y1.to_broadcast([P, 2, 3, NV]), ALU.mult))
                dve.wait_ge(w_ready, n + 1)
                pwv = p_w[r][:, 0:384].rearrange("p (t m) -> p t m", t=2)
                k_pw = chain.did(nc.vector.tensor_tensor(
                    pw[:, s], pwv[:, :, 0:2 * NS].rearrange("p t (k u) -> p t k u", k=2),
                    e0.unsqueeze(2).to_broadcast([P, 2, 2, NS]), ALU.mult))
                k_vw = chain.did(nc.vector.tensor_tensor(
                    vw[:, s], pwv[:, :, 2 * NS:2 * NS + NV].unsqueeze(2).to_broadcast([P, 2, 3, NV]), e1, ALU.mult))
                chain.wait(k_dv)
                k_ds = chain.did(nc.vector.tensor_tensor(ds[:, s, :, 0, :], dv[:, s, :, 0, :], dv[:, s, :, 1, :], ALU.add))
                chain.wait(k_pw)
                nc.vector.tensor_tensor(mid[:, s, :, :, 0:NS], pw[:, s, :, 1, :].unsqueeze(2).to_broadcast([P, 2, 3, NS]),
                                        y1.to_broadcast([P, 2, 3, NS]), ALU.mult)
                chain.wait(k_ds)
                k_ds = chain.did(nc.vector.tensor_tensor(ds[:, s, :, 1, :], ds[:, s, :, 0, :], dv[:, s, :, 2, :], ALU.add))
                nc.vector.tensor_tensor(mid[:, s, :, :, NS:NS + NV], vw[:, s], y[:, :, 0:1].unsqueeze(3).to_broadcast([P, 2, 3, NV]), ALU.mult)
                nc.vector.tensor_tensor(mid[:, s, :, 1:3, NS + NV:], pw[:, s, :, 0, :].rearrange("p t (k u) -> p t k u", k=2),
                                        y[:, :, 0:1].unsqueeze(3).to_broadcast([P, 2, 2, NV]), ALU.mult)
                chain.wait(k_ds)
                nc.vector.tensor_tensor(mid[:, s, :, 0, NS + NV:], pwv[:, :, 2 * NS + NV:], ds[:, s, :, 1, :], ALU.mult).then_inc(pair_done, 1)

            def turn(i):
                for j in range(4):
                    pair(i, j)
            turns(dve, turn)

        @block.tensor
        def _(pe):
            def hidden_layer(i, c):
                if isinstance(i, int) and 2 * i + c >= QUADS:
                    return
                c, i = c % 2, i + c // 2
                q = 2 * i + c
                need(pe, silu_done, q)
                pe.wait_ge(loaded[c], 64 * (i + 1))
                nc.tensor.matmul(p_hid[0:hidden, :], w[pre + "fc1"][:, :], features[:, c, :], start=True, stop=True).then_inc(hid_ready, 1)

            def edge_weights(i, j):
                if isinstance(i, int) and 4 * i + j >= PAIRS:
                    return
                j, i = j % 4, i + j // 4
                c, r = j // 2, j % 2
                need(pe, pair_done, 4 * i + j - 1)
                pe.wait_ge(silu_done, 2 * i + c + 1)
                for t in range(2):
                    last = nc.tensor.matmul(p_w[r][:, t * 192:(t + 1) * 192], hid[:, c, (2 * r + t) * P:(2 * r + t + 1) * P],
                                            w[pre + "fc2"][:, :], start=True, stop=True)
                last.then_inc(w_ready, 1)

            def sums(i, j):
                n, s = 4 * i + j, j % 2
                need(pe, z_copied, n - 1)
                pe.wait_ge(pair_done, n + 1)
                for k in range(3):
                    z = p_z[s][:, 2 * P * k:2 * P * (k + 1)]
                    nc.tensor.matmul(z, mid[:, s, 1, k, :], same_b[:, s, :], start=True, stop=False)
                    last = nc.tensor.matmul(z[:, 0:P], mid[:, s, 0, k, :], same_a[:, s, :], start=False, stop=True)
                last.then_inc(z_ready, 1)

            def outputs(i, j):
                n = 4 * i + j
                if isinstance(i, int) and n < 0:
                    return
                need(pe, rows_ready, n)
                pe.wait_ge(z_copied, n + 1)
                for t in range(2):
                    for a, k in enumerate((2, 0, 1)):
                        cols = off + NS + NV * (k + 1)
                        last = nc.tensor.matmul(p_out[:, t * ow:t * ow + cols], zt[:, j % 2, k, t * P:(t + 1) * P],
                                                w[pre + "out"][:, k * ow:k * ow + cols], start=(a == 0), stop=(a == 2))
                last.then_inc(out_ready, 1)

            def turn(i):
                for j in range(4):
                    if j % 2 == 0:
                        hidden_layer(i, j // 2 + 1)
                    edge_weights(i, j + 1)
                    sums(i, j)
                    outputs(i, j - 1)
            hidden_layer(0, 0)
            edge_weights(0, 0)
            turns(pe, turn)
            outputs(TURNS - 1, 3)


def node_pass(nc, w, dram, after, source, acc, width, table, base, result):
    first, final = after == 0, after == 3
    off = 1 if final else 0
    with ExitStack() as ctx:
        pre = f"n{after}_"
        sem = lambda name: ctx.enter_context(nc.semaphore(pre + name))
        sb = lambda name, shape, dt=F32: ctx.enter_context(nc.sbuf_tensor("s_" + pre + name, shape, dt))
        pb = lambda name: ctx.enter_context(nc.psum_tensor(pre + name, [P, 512], F32))
        src = sb("src", [P, 2, 4, D])
        agg = sb("agg", [P, 2, 4, width])
        coef = sb("coef", [P, 2, 5, 4])
        xr = sb("xr", [P, 2, 4, D])
        part = sb("part", [P, 2, 4, D])
        total = sb("total", [P, 2, 4])
        nmean = sb("nmean", [P, 2, 4])
        square = sb("square", [P, 2, 4, D])
        ssq = sb("ssq", [P, 2, 4])
        std = sb("std", [P, 2, 4])
        rstd = sb("rstd", [P, 2, 4])
        xn = sb("xn", [P, 2, 4, D])
        xta = sb("xta", [P, 2, 4 * P])
        xtb = sb("xtb", [NV + 1, 2, 4 * P])
        fta = sb("fta", [P, 2, 4 * P])
        ftb = sb("ftb", [NV + 1, 2, 4 * P])
        bout = sb("bout", [P, 2, 4, D])
        tout = sb("tout", [P, 2, 4, D])
        p_ta, p_tb = pb("p_ta"), pb("p_tb")
        p_o = [pb(f"p_o{t}") for t in range(4)]
        p_u = [pb(f"p_u{t}") for t in range(2)]

        loaded = [sem(f"loaded{c}") for c in range(2)]
        if first:
            ones = sem("ones")
            f_ready, f_copied, u_ready = sem("f_ready"), sem("f_copied"), sem("u_ready")
        steps, norm_steps, square_steps = sem("steps"), sem("norm_steps"), sem("square_steps")
        sum_done, std_done, xn_done = sem("sum_done"), sem("std_done"), sem("xn_done")
        if not final:
            t_ready, t_copied, o_ready = sem("t_ready"), sem("t_copied"), sem("o_ready")
            base_done, table_done = sem("base_done"), sem("table_done")
        stored = [sem(f"stored{c}") for c in range(2)]
        block = ctx.enter_context(nc.Block())
        view = lambda a, q: a[bass.ds(q * QUAD, QUAD), :].rearrange("(p r) c -> p (r c)", p=P)
        flat = lambda a, c: a[:, c].rearrange("p t k -> p (t k)")
        z_of = lambda q, t: w["z_node"][:, bass.ds(4 * q + t, 1)]
        per_store = 16 if final else 32

        def quad(i, c):
            i, c = i + c // 2, c % 2
            q = 2 * i + c
            if isinstance(q, int) and not 0 <= q < QUADS:
                return None
            return i, c, q

        @block.sync
        def _(sp):
            def turn(i):
                for c in range(2):
                    q = 2 * i + c
                    need(sp, sum_done, q - 1)
                    sp.nop(nofuse=True)
                    sp.dma_start(flat(src, c), view(source, q)).then_inc(loaded[c], 16)
                    sp.dma_start(flat(agg, c), view(acc, q)).then_inc(loaded[c], 16)
            turns(sp, turn)
            for c in range(2):
                sp.wait_ge(stored[c], per_store * TURNS)

        @block.gpsimd
        def _(pool):
            def turn(i):
                for c in range(2):
                    q = 2 * i + c
                    if final:
                        pool.wait_ge(xn_done, q + 1)
                        pool.nop(nofuse=True)
                        pool.dma_start(view(result, q), flat(xn, c)).then_inc(stored[c], 16)
                    else:
                        pool.wait_ge(base_done, 4 * q + 4)
                        pool.nop(nofuse=True)
                        pool.dma_start(view(base, q), flat(bout, c)).then_inc(stored[c], 16)
                        pool.wait_ge(table_done, q + 1)
                        pool.nop(nofuse=True)
                        pool.dma_start(view(table, q), flat(tout, c)).then_inc(stored[c], 16)
            turns(pool, turn)

        @block.scalar
        def _(act):
            def copy_front(at):
                if at is None:
                    return
                i, c, q = at
                need(act, u_ready, q - 1)
                act.wait_ge(f_ready, q + 1)
                nc.scalar.copy(fta[:, c, :], p_ta[:, :])
                nc.scalar.copy(ftb[0:NV, c, :], p_tb[0:NV, :]).then_inc(f_copied, 1)

            def squares(at):
                if at is None:
                    return
                i, c, q = at
                need(act, std_done, q - 1)
                need(act, xn_done, q - 1)
                act.wait_ge(sum_done, q + 1)
                for t in range(4):
                    last = nc.scalar.activation(square[:, c, t, :], xr[:, c, t, :], ACT.Square, bias=nmean[:, c, t:t + 1],
                                                accum_out=ssq[:, c, t:t + 1])
                last.then_inc(square_steps, 1)
                act.wait_ge(square_steps, q + 1)
                nc.scalar.activation(std[:, c, :], ssq[:, c, :], ACT.Sqrt, scale=1.0 / D, bias=w["eps"][:, :]).then_inc(std_done, 1)

            def copy_t(at):
                i, c, q = at
                need(act, o_ready, q - 1)
                act.wait_ge(t_ready, q + 1)
                nc.scalar.copy(xta[:, c, :], p_ta[:, :])
                nc.scalar.copy(xtb[0:NV, c, :], p_tb[0:NV, :]).then_inc(t_copied, 1)

            def messages(at):
                if at is None:
                    return
                i, c, q = at
                need(act, stored[c], per_store * i)
                act.wait_ge(o_ready, q + 1)
                for t in range(4):
                    act.wait_ge(base_done, 4 * q + t + 1)
                    last = nc.scalar.activation(tout[:, c, t, :], p_o[t][:, D:2 * D], ACT.Copy, scale=z_of(q, t))
                last.then_inc(table_done, 1)

            def turn(i):
                for c in range(2):
                    if not final:
                        messages(quad(i, c - 1))
                    if first:
                        copy_front(quad(i, c + 1))
                    squares(quad(i, c + 1))
                    if not final:
                        copy_t(quad(i, c))
            if first:
                copy_front(quad(0, 0))
            squares(quad(0, 0))
            turns(act, turn)
            if not final:
                messages(quad(TURNS - 1, 1))

        @block.vector
        def _(dve):
            chain = Chain(dve, steps, 6 if final else 2 if first else 1)

            def sums(at):
                if at is None:
                    return
                i, c, q = at
                chain.start(q)
                dve.wait_ge(loaded[c], 32 * (i + 1))
                need(dve, xn_done, q - 1)
                if first:
                    dve.wait_ge(u_ready, q + 1)
                    for t in range(4):
                        ins = nc.vector.scalar_tensor_tensor(part[:, c, t, :], src[:, c, t, :], 2.0,
                                                             p_u[t // 2][:, (t % 2) * D:(t % 2 + 1) * D], ALU.mult, ALU.add)
                    chain.wait(chain.did(ins))
                    ins = [nc.vector.scalar_tensor_tensor(xr[:, c, t, :], part[:, c, t, :], 1.0, agg[:, c, t, :], ALU.mult,
                                                          ALU.add, accum_out=total[:, c, t:t + 1]) for t in range(4)][-1]
                elif final:
                    cf = lambda k: coef[:, c, k, :].unsqueeze(2)
                    chain.wait(chain.did(nc.vector.tensor_scalar(cf(0), agg[:, c, :, D + 1:D + 2], 1.0, None, ALU.max)))
                    chain.wait(chain.did(nc.vector.reciprocal(cf(1), cf(0))))
                    chain.wait(chain.did(nc.vector.tensor_tensor(coef[:, c, 2, :], coef[:, c, 1, :],
                                                                 w["z_node"][:, bass.ds(4 * q, 4)], ALU.mult)))
                    chain.wait(chain.did(nc.vector.tensor_tensor(cf(3), cf(2), cf(2), ALU.mult)))
                    chain.wait(chain.did(nc.vector.tensor_tensor(cf(4), cf(3), agg[:, c, :, 0:1], ALU.mult)))
                    ins = [nc.vector.scalar_tensor_tensor(xr[:, c, t, :], agg[:, c, t, 1:1 + D], coef[:, c, 4, t:t + 1],
                                                          src[:, c, t, :], ALU.mult, ALU.add,
                                                          accum_out=total[:, c, t:t + 1]) for t in range(4)][-1]
                else:
                    ins = [nc.vector.scalar_tensor_tensor(xr[:, c, t, :], agg[:, c, t, :], z_of(q, t), src[:, c, t, :],
                                                          ALU.mult, ALU.add,
                                                          accum_out=total[:, c, t:t + 1]) for t in range(4)][-1]
                chain.wait(chain.did(ins))
                nc.vector.tensor_scalar(nmean[:, c, :], total[:, c, :], -1.0 / D, None, ALU.mult).then_inc(sum_done, 1)

            def norm(at):
                i, c, q = at
                dve.wait_ge(std_done, q + 1)
                nc.vector.reciprocal(rstd[:, c, :], std[:, c, :]).then_inc(norm_steps, 1)
                if final:
                    need(dve, stored[c], per_store * i)
                else:
                    need(dve, t_ready, q - 1)
                    need(dve, base_done, 4 * q - 4)
                dve.wait_ge(norm_steps, q + 1)
                for t in range(4):
                    ins = nc.vector.tensor_scalar(xn[:, c, t, :], xr[:, c, t, :], nmean[:, c, t:t + 1], rstd[:, c, t:t + 1],
                                                  ALU.add, ALU.mult)
                ins.then_inc(xn_done, 1)

            def self_term(at):
                if at is None:
                    return
                i, c, q = at
                need(dve, stored[c], per_store * i)
                dve.wait_ge(o_ready, q + 1)
                for t in range(4):
                    nc.vector.scalar_tensor_tensor(bout[:, c, t, :], p_o[t][:, 0:D], z_of(q, t), xn[:, c, t, :],
                                                   ALU.mult, ALU.add).then_inc(base_done, 1)

            def turn(i):
                for c in range(2):
                    if not final:
                        self_term(quad(i, c - 1))
                    sums(quad(i, c + 1))
                    norm(quad(i, c))
            if first:
                nc.vector.memset(ftb[:, :, :], 1.0).then_inc(ones, 1)
            sums(quad(0, 0))
            turns(dve, turn)
            if not final:
                self_term(quad(TURNS - 1, 1))

        if final:
            return

        @block.tensor
        def _(pe):
            def transpose(src_slot):
                for t in range(4):
                    nc.tensor.transpose(p_ta[:, t * P:(t + 1) * P], src_slot[:, t, 0:P], w["ident"][:, :])
                    last = nc.tensor.transpose(p_tb[0:NV, t * P:(t + 1) * P], src_slot[:, t, P:D], w["ident"][:, :])
                return last

            def front(at):
                if at is None:
                    return
                i, c, q = at
                need(pe, t_copied, q - 1)
                pe.wait_ge(loaded[c], 32 * (i + 1))
                transpose(src[:, c]).then_inc(f_ready, 1)
                need(pe, sum_done, q)
                pe.wait_ge(f_copied, q + 1)
                for t in range(4):
                    o = p_u[t // 2][:, (t % 2) * D:(t % 2 + 1) * D]
                    nc.tensor.matmul(o, fta[:, c, t * P:(t + 1) * P], w["u_a"][:, :], start=True, stop=False)
                    last = nc.tensor.matmul(o, ftb[:, c, t * P:(t + 1) * P], w["u_b"][:, :], start=False, stop=True)
                last.then_inc(u_ready, 1)

            def products(at):
                i, c, q = at
                need(pe, t_copied, q)
                pe.wait_ge(xn_done, q + 1)
                transpose(xn[:, c]).then_inc(t_ready, 1)
                need(pe, base_done, 4 * q)
                need(pe, table_done, q)
                pe.wait_ge(t_copied, q + 1)
                for t in range(4):
                    o = p_o[t][:, 0:2 * D].rearrange("p (k c) -> p k c", k=2)
                    nc.tensor.matmul(o[:, :, 0:P], xta[:, c, t * P:(t + 1) * P], w[f"node{after + 1}_a"][:, :], start=True, stop=True)
                    last = nc.tensor.matmul(o[:, :, P:D], xtb[0:NV, c, t * P:(t + 1) * P], w[f"node{after + 1}_b"][:, :],
                                            start=True, stop=True)
                last.then_inc(o_ready, 1)

            def turn(i):
                for c in range(2):
                    if first:
                        front(quad(i, c + 1))
                    products(quad(i, c))
            if first:
                pe.wait_ge(ones, 1)
                front(quad(0, 0))
            turns(pe, turn)


CONVS = {
    1: dict(features=12, hidden=100, self_factor=math.sin(math.pi / 8), factor=math.cos(math.pi / 8) / math.sqrt(8.0 * 96 * 100)),
    2: dict(features=16, hidden=64, self_factor=math.sin(math.pi / 8), factor=math.cos(math.pi / 8) / math.sqrt(10.0 * 96 * 64)),
    3: dict(features=16, hidden=64, self_factor=1.0, factor=1.0 / math.sqrt(96.0 * 64)),
}

FACTORS = [
    ("l0_w14", (0, NS), (0, EB * P), 1 / math.sqrt(2.0 * NS * EB)),
    ("l0_w14", (NS, P), (0, EB * P), 1 / math.sqrt(2.0 * NV * EB)),
    ("l0_w4", (0, NV), (0, EB * NV), 1 / math.sqrt(2.0 * NV * EB)),
    ("l0_w3", (0, NS), (0, EB * NV), 1 / math.sqrt(2.0 * NS * EB)),
    ("l0_w2", (0, P), (0, 2 * NS), 1 / math.sqrt(3.0 * 2.0 * NV * EB)),
]
for _l, _c in CONVS.items():
    _ow = D + (_l == 3)
    FACTORS += [
        (f"c{_l}_out", (0, P - NV), (0, 3 * _ow), _c["factor"]),
        (f"c{_l}_out", (P - NV, P), (0, _ow), _c["factor"] / math.sqrt(3.0)),
        (f"c{_l}_out", (P - NV, P), (_ow, 3 * _ow), _c["factor"]),
        (f"node{_l}_a", (0, P), (0, NS), _c["self_factor"] / math.sqrt(NS)),
        (f"node{_l}_a", (0, P), (NS, P), _c["self_factor"] / math.sqrt(NV)),
        (f"node{_l}_a", (0, P), (P, P + NS), 1 / math.sqrt(NS)),
        (f"node{_l}_a", (0, P), (P + NS, 2 * P), 1 / math.sqrt(NV)),
        (f"node{_l}_b", (0, NV), (0, NV), _c["self_factor"] / math.sqrt(NV)),
        (f"node{_l}_b", (0, NV), (NV, 2 * NV), 1 / math.sqrt(NV)),
    ]


def build(nc, dram, result):
    scratch = lambda name, rows, cols: nc.dram_tensor(name, [rows, cols], F32).ap()
    table = scratch("table", PADDED, D)
    bases = [scratch(f"base{k}", PADDED, D) for k in range(2)]
    accs = [scratch(f"acc{k}", ACC_ROWS, D) for k in range(2)]
    acc3 = scratch("acc3", ACC_ROWS, D + 2)
    with ExitStack() as ctx:
        w = {}
        for name in WEIGHTS:
            w[name] = ctx.enter_context(nc.sbuf_tensor("w_" + name, list(dram[name].shape), F32))
        w["loads"], w["factors"] = WEIGHTS, FACTORS
        for name, shape, dt in (("ident", [P, P], F32), ("zeros", [P, 8 * (D + 2)], F32), ("tp", [P, 2, 2, D + 1], F32),
                                ("mask", [P, 2, 2 * P], F32), ("spare", [P, 2], I32), ("eps", [P, 1], F32),
                                ("l0_out_a", [P, D], F32), ("l0_out_b", [NV + 1, D], F32),
                                ("seen", [P, 2 * PAIRS], F32), ("slots", [P, 2 * PAIRS], I32)):
            w[name] = ctx.enter_context(nc.sbuf_tensor("w_" + name, shape, dt))
        prepare_weights(nc, w, dram)
        zero_accumulator(nc, w, accs[0], D)
        edge_layer0(nc, w, dram, dram["x"], accs[0], accs[1], D)
        node_pass(nc, w, dram, 0, dram["x"], accs[0], D, table, bases[0], None)
        edge_conv(nc, w, dram, 1, table, accs[1], D, accs[0], D)
        node_pass(nc, w, dram, 1, bases[0], accs[1], D, table, bases[1], None)
        edge_conv(nc, w, dram, 2, table, accs[0], D, acc3, D + 2)
        node_pass(nc, w, dram, 2, bases[1], accs[0], D, table, bases[0], None)
        edge_conv(nc, w, dram, 3, table, acc3, D + 2, None, 0)
        node_pass(nc, w, dram, 3, bases[0], acc3, D + 2, None, None, result)


WEIGHTS = (["z_node", "l0_w14", "l0_w4", "l0_w3", "l0_w2", "wm_t_a", "wm_t_b", "wu2_a", "wu2_b", "u_a", "u_b"]
           + [f"c{l}_{m}" for l in (1, 2, 3) for m in ("fc1", "fc2", "out")]
           + [f"node{l}_{m}" for l in (1, 2, 3) for m in ("a", "b")])


def lay_out(inputs):
    import numpy as np
    a = {k: np.asarray(v) for k, v in inputs.items()}
    extra = PADDED - ROWS

    def by_component(m, axis):
        m = np.moveaxis(m, axis, 0)
        v = m[NS:].reshape((NV, 3) + m.shape[1:])
        v = np.swapaxes(v, 0, 1).reshape((3 * NV,) + m.shape[1:])
        return np.moveaxis(np.concatenate([m[:NS], v]), 0, axis)

    def pad(m, value=0):
        return np.concatenate([m, np.full((extra,) + m.shape[1:], value, m.dtype)])

    d = {}
    d["x"] = pad(by_component(a["x"], 1))
    src, dst = pad(a["src"], ROWS), pad(a["dst"], ROWS)
    by_partition = lambda m: m.reshape(QUADS, 4, P, -1).transpose(0, 2, 1, 3).reshape(QUADS * P, -1)
    d["src_row"], d["dst_row"] = src.reshape(QUADS, QUAD), dst.reshape(QUADS, QUAD)
    d["index0"] = np.concatenate([by_partition(dst), by_partition(src)], axis=1)
    d["index1"] = np.concatenate([by_partition(src), by_partition(dst)], axis=1)
    e = a["edge_attr_32"]
    ev = e[:, EB:].reshape(ROWS, EB, 3).transpose(0, 2, 1).reshape(ROWS, 3 * EB)
    d["attr32"] = by_partition(pad(np.concatenate([e[:, :EB], ev], axis=1)))
    d["attr4"] = by_partition(pad(a["edge_attr_4"]))
    d["features12"], d["features16"] = pad(a["edge_attr_12"]).T, pad(a["edge_attr_16"]).T
    d["z_node"] = pad(a["node_vec1"]).reshape(QUADS, P, 4).transpose(1, 0, 2).reshape(P, 4 * QUADS)

    w1, w2, w3, w4 = (a[f"L0_gnn_W{k}"] for k in (1, 2, 3, 4))
    w14 = np.zeros((P, EB, P), np.float32)
    w14[:NS, :, :NS] = w1
    w14[NS:NS + NV, :, NS:NS + NV] = w4
    w14[NS + NV:, :, NS + NV:] = w4
    d["l0_w14"], d["l0_w4"], d["l0_w3"] = w14.reshape(P, EB * P), w4.reshape(NV, EB * NV), w3.reshape(NS, EB * NV)
    d["l0_w2"] = w2.transpose(1, 0, 2).reshape(2, P, NS).transpose(1, 0, 2).reshape(P, 2 * NS)
    wm = np.concatenate([by_component(a["L0_gnn_Wm"], 0), a["L0_gnn_bm"][None]]).T
    d["wm_t_a"], d["wm_t_b"] = wm[:P], wm[P:]
    wu = by_component(a["L0_gnn_Wu"], 1)
    d["wu2_a"], d["wu2_b"] = wu[D:D + P], wu[D + P:]
    u = np.concatenate([by_component(wu[:D], 0), by_component(a["L0_gnn_bu"], 0)[None]])
    d["u_a"], d["u_b"] = u[:P], u[P:]

    names = {1: ("L1_gnn_W_fc1", "L1_gnn_W_fc2", "L1_gnn_W_sc0", "L1_gnn_W_sc1", "L1_gnn_W_l1_0", "L1_gnn_W_l1_1", "L1_gnn_W_l2_0", "L1_gnn_W_l2_1"),
             2: ("L2_gnn_fc_W1", "L2_gnn_fc_W2", "L2_gnn_W_sc0", "L2_gnn_W_sc1", "L2_gnn_W_l1_0", "L2_gnn_W_l1_1", "L2_gnn_W_l2_0", "L2_gnn_W_l2_1"),
             3: ("L3_gnn_Wfc1", "L3_gnn_Wfc2", "L3_gnn_Wsc0", "L3_gnn_Wsc1", "L3_gnn_Wl1_0", "L3_gnn_Wl1_1", "L3_gnn_Wl2_s", "L3_gnn_Wl2_v")}
    for l, keys in names.items():
        fc1, fc2, sc0, sc1, l10, l11, l20, l21 = (a[k] for k in keys)
        d[f"c{l}_fc1"], d[f"c{l}_fc2"] = fc1, fc2
        if l == 3:
            l20 = np.concatenate([a["L3_gnn_Wa"], l20], axis=1)
        ow = l20.shape[1] + 3 * NV
        out = np.zeros((P, 3, ow), np.float32)
        for k in range(3):
            at = l20.shape[1] + k * NV
            out[:NS + NV, k, at:at + NV] = l21
        out[P - NV:, 0, :l20.shape[1]] = l20[NS:]
        out[P - NV:, 1, :l20.shape[1]] = l20[:NV]
        out[P - NV:, 2, :l20.shape[1]] = l20[NV:NS]
        d[f"c{l}_out"] = out.reshape(P, 3 * ow)
        na = np.zeros((P, 2, P), np.float32)
        for k, (ws, wv) in enumerate(((sc0, sc1), (l10, l11))):
            na[:NS, k, :NS] = ws
            na[NS:NS + NV, k, NS:NS + NV] = wv
            na[NS + NV:, k, NS + NV:] = wv
        d[f"node{l}_a"] = na.reshape(P, 2 * P)
        d[f"node{l}_b"] = np.concatenate([sc1, l11], axis=1)
    return {k: np.ascontiguousarray(v) for k, v in d.items()}


def kernel(**inputs):
    import numpy as np
    import concourse.bacc as bacc
    from concourse.bass_utils import run_bass_kernel_spmd

    arrays = lay_out(inputs)
    nc = bacc.Bacc("TRN2", target_bir_lowering=False, num_devices=1)
    dram = {name: nc.dram_tensor(name, a.shape, mybir.dt.from_np(a.dtype), kind="ExternalInput").ap()
            for name, a in arrays.items()}
    result = nc.dram_tensor("result", (PADDED, D), F32, kind="ExternalOutput").ap()
    build(nc, dram, result)
    out = run_bass_kernel_spmd(nc, [arrays], core_ids=[0]).results[0]["result"][:ROWS]
    v = out[:, NS:].reshape(ROWS, 3, NV).transpose(0, 2, 1).reshape(ROWS, 3 * NV)
    return np.concatenate([out[:, :NS], v], axis=1)
```

```python
import math

import concourse.bass as bass
from concourse import mybir
from contextlib import ExitStack

F32 = mybir.dt.float32
I32 = mybir.dt.int32
ALU = mybir.AluOpType
ACT = mybir.ActivationFunctionType

ROWS = 50000
P = 128
QUAD = 4 * P
STEP = 2 * QUAD
TURNS = -(-ROWS // STEP)
PADDED = TURNS * STEP
QUADS = PADDED // QUAD
RING = 4
NODE_TURNS = -(-QUADS // RING)
PAIRS = 4 * TURNS
NS, NV = 64, 32
D = NS + 3 * NV
EB = 8
SPARE = PADDED
ACC_ROWS = PADDED + 2 * P
REPEAT = 1024.0


def need(eng, sem, value):
    if isinstance(value, int) and value <= 0:
        return
    eng.wait_ge(sem, value)


def turns(eng, body):
    body(0)
    with eng.Fori(1, TURNS - 1) as i:
        body(i)
    body(TURNS - 1)


class Chain:

    def __init__(self, eng, sem, per_unit):
        self.eng, self.sem, self.per_unit = eng, sem, per_unit
        self.unit, self.count = 0, per_unit

    def start(self, unit):
        assert self.count == self.per_unit, self.count
        self.unit, self.count = unit, 0

    def did(self, instruction):
        instruction.then_inc(self.sem, 1)
        self.count += 1
        return self.count

    def wait(self, count):
        need(self.eng, self.sem, self.unit * self.per_unit + count)


def prepare_weights(nc, w, dram):
    with ExitStack() as ctx:
        sem = lambda name: ctx.enter_context(nc.semaphore(name))
        loaded, ready, folded, masks, mm = (sem(n) for n in ("w_loaded", "w_ready", "w_folded", "w_masks", "w_product"))
        prod = ctx.enter_context(nc.psum_tensor("prod", [P, 2, 512], F32))
        block = ctx.enter_context(nc.Block())
        loads = [(w[name], dram[name]) for name in w["loads"]]

        @block.sync
        def _(sp):
            for dst, src in loads:
                sp.dma_start(dst[:, :], src).then_inc(loaded, 16)

        @block.vector
        def _(dve):
            nc.vector.memset(w["ident"][:, :], 0.0)
            nc.vector.memset(w["zeros"][:, :], 0.0)
            nc.vector.memset(w["tp"][:, :, :, :], 1.0)
            nc.vector.memset(w["eps"][:, :], 1e-5)
            nc.vector.memset(w["mask"][:, :, :], 1.0).then_inc(ready, 1)
            dve.wait_ge(loaded, 16 * len(loads))
            for name, rows, cols, factor in w["factors"]:
                part = w[name][rows[0]:rows[1], cols[0]:cols[1]]
                nc.vector.tensor_scalar(part, part, factor, None, ALU.mult).then_inc(folded, 1)
            dve.wait_ge(mm, 1)
            nc.vector.tensor_copy(w["l0_out_a"][:, :], prod[:, 0, 0:D])
            nc.vector.tensor_copy(w["l0_out_b"][:, :], prod[0:NV + 1, 1, 0:D]).then_inc(folded, 1)

        @block.tensor
        def _(pe):
            pe.wait_ge(loaded, 16 * len(loads))
            for k, rows in ((0, P), (1, NV + 1)):
                cols = slice(k * P, k * P + rows)
                nc.tensor.matmul(prod[0:rows, k, 0:D], w["wm_t_a"][:, cols], w["wu2_a"][:, :], start=True, stop=False)
                last = nc.tensor.matmul(prod[0:rows, k, 0:D], w["wm_t_b"][:, cols], w["wu2_b"][:, :], start=False, stop=True)
            last.then_inc(mm, 1)

        @block.gpsimd
        def _(pool):
            pool.wait_ge(ready, 1)
            pool.affine_select(out=w["ident"][:, :], in_=w["ident"][:, :], compare_op=ALU.not_equal, fill=1.0,
                               base=0, pattern=[[-1, P]], channel_multiplier=1)
            pool.affine_select(out=w["mask"][:, 0, :], in_=w["mask"][:, 0, :], compare_op=ALU.is_ge, fill=REPEAT + 1,
                               base=0, pattern=[[1, 2 * P]], channel_multiplier=-1)
            pool.affine_select(out=w["mask"][:, 1, :], in_=w["mask"][:, 1, :], compare_op=ALU.is_ge, fill=REPEAT + 1,
                               base=-P, pattern=[[1, 2 * P]], channel_multiplier=-1)
            pool.iota(w["spare"][:, :], pattern=[[P, 2]], base=SPARE, channel_multiplier=1).then_inc(masks, 1)
            pool.wait_ge(masks, 1)
            pool.wait_ge(folded, len(w["factors"]) + 1)


def zero_accumulator(nc, w, acc, width):
    with ExitStack() as ctx:
        zeroed = ctx.enter_context(nc.semaphore("zeroed"))
        block = ctx.enter_context(nc.Block())

        @block.sync
        def _(sp):
            for n in range(TURNS):
                sp.dma_start(acc[n * STEP:(n + 1) * STEP, :].rearrange("(p r) c -> p (r c)", p=P),
                             w["zeros"][:, 0:8 * width]).then_inc(zeroed, 16)
            sp.dma_start(acc[PADDED:ACC_ROWS, :].rearrange("(p r) c -> p (r c)", p=P),
                         w["zeros"][:, 0:2 * width]).then_inc(zeroed, 16)
            sp.wait_ge(zeroed, 16 * (TURNS + 1))


def edge_layer0(nc, w, dram, x, acc, next_acc, next_width):
    with ExitStack() as ctx:
        sem = lambda name: ctx.enter_context(nc.semaphore("a_" + name))
        sb = lambda name, shape, dt=F32: ctx.enter_context(nc.sbuf_tensor("a_" + name, shape, dt))
        pb = lambda name: ctx.enter_context(nc.psum_tensor("a_" + name, [P, 512], F32))
        target_row = sb("target_row", [P, 2, QUAD], I32)
        index = sb("index", [P, 2, 8], I32)
        attr = sb("attr", [P, 2, 4, 4 * EB])
        rows = sb("rows", [P, 4, 2, D])
        xt = sb("xt", [P, 2, 2, 2 * P])
        dp = sb("dp", [P, 3, EB, NV])
        dot = sb("dot", [P, 4, EB * NV])
        dsum = sb("dsum", [P, EB * NV])
        dott = sb("dott", [P, 2, 2, P])
        mac = sb("mac", [P, 2, 2, D])
        vprod = sb("vprod", [P, 2, 3, EB, NV])
        init = sb("init", [P, 2, D])
        tp = w["tp"]
        same_a = sb("same_a", [P, 2, P])
        same_b = sb("same_b", [P, 2, 2 * P])
        hits = sb("hits", [P, 2, 2 * P])
        seen = sb("seen", [P, 2, 2])
        away = sb("away", [P, 2, 2])
        move = sb("move", [P, 2, 2])
        slot = sb("slot", [P, 4, 2], I32)
        zt = sb("zt", [P, 2, 2, 2 * P])
        out = sb("out", [P, 2, 2, D])
        tb = [pb(f"t{k}") for k in range(4)]
        p_xt, p_dt, p_z, p_out = pb("p_xt"), pb("p_dt"), pb("p_z"), pb("p_out")

        loaded = [sem(f"loaded{c}") for c in range(2)]
        gathered = [sem(f"gathered{j}") for j in range(4)]
        zeroed = sem("zeroed")
        xt_ready, xt_copied = sem("xt_ready"), sem("xt_copied")
        dot_steps = sem("dot_steps")
        dt_ready, dt_copied = sem("dt_ready"), sem("dt_copied")
        bank_ready = [sem(f"bank_ready{k}") for k in range(4)]
        bank_read = [sem(f"bank_read{k}") for k in range(4)]
        s2_ready, s2_copied = sem("s2_ready"), sem("s2_copied")
        steps = sem("steps")
        pair_done = sem("pair_done")
        z_ready, z_copied = sem("z_ready"), sem("z_copied")
        out_ready, rows_ready = sem("out_ready"), sem("rows_ready")
        scattered = sem("scattered")
        block = ctx.enter_context(nc.Block())

        @block.sync
        def _(sp):
            def turn(i):
                for c in range(2):
                    q = 2 * i + c
                    need(sp, pair_done, 2 * q - 2)
                    sp.nop(nofuse=True)
                    sp.dma_start(target_row[:, c, :], dram["src_row"][bass.ds(q, 1), :].to_broadcast([P, QUAD])).then_inc(loaded[c], 16)
                    sp.dma_start(index[:, c, :], dram["index0"][bass.ds(q * P, P), :]).then_inc(loaded[c], 16)
                    sp.dma_start(attr[:, c, :, :].rearrange("p t k -> p (t k)"), dram["attr32"][bass.ds(q * P, P), :]).then_inc(loaded[c], 16)
                sp.dma_start(next_acc[bass.ds(i * STEP, STEP), :].rearrange("(p r) c -> p (r c)", p=P),
                             w["zeros"][:, 0:8 * next_width]).then_inc(zeroed, 16)
            turns(sp, turn)
            sp.dma_start(next_acc[PADDED:ACC_ROWS, :].rearrange("(p r) c -> p (r c)", p=P),
                         w["zeros"][:, 0:2 * next_width]).then_inc(zeroed, 16)
            sp.wait_ge(zeroed, 16 * (TURNS + 1))

        @block.gpsimd
        def _(pool):
            chain = Chain(pool, dot_steps, 3)

            def gather(i, j):
                if isinstance(i, int) and 4 * i + j >= PAIRS:
                    return
                j, i = j % 4, i + j // 4
                c, r = j // 2, j % 2
                need(pool, dt_ready, 2 * (4 * i + j) - 6)
                pool.wait_ge(loaded[c], 48 * (i + 1))
                for t in range(2):
                    pool.nop(nofuse=True)
                    pool.indirect_dma_start(rows[:, j, t, :], None, x,
                                            bass.IndirectOffsetOnAxis(ap=index[:, c, 2 * r + t:2 * r + t + 1], axis=0)
                                            ).then_inc(gathered[j], 16)

            def scatter(i, j):
                if isinstance(i, int) and 4 * i + j < 0:
                    return
                need(pool, scattered, 32 * (4 * i + j))
                pool.wait_ge(rows_ready, 4 * i + j + 1)
                for t in range(2):
                    pool.nop(nofuse=True)
                    pool.indirect_dma_start(acc, bass.IndirectOffsetOnAxis(ap=slot[:, j % 4, t:t + 1], axis=0),
                                            out[:, j % 2, t, :], None, compute_op=ALU.add).then_inc(scattered, 16)

            def dots(i, j):
                if isinstance(i, int) and 4 * i + j >= PAIRS:
                    return
                j, i = j % 4, i + j // 4
                c, r = j // 2, j % 2
                pool.wait_ge(gathered[j], 32 * (i + 1))
                for t in range(2):
                    m = 8 * i + 2 * j + t
                    chain.start(m)
                    need(pool, dt_ready, m - 3)
                    chain.wait(0)
                    ev = attr[:, c, 2 * r + t, EB:].rearrange("p (k b) -> p k b", k=3)
                    xv = rows[:, j, t, NS:].rearrange("p (k a) -> p k a", k=3)
                    n = chain.did(nc.gpsimd.tensor_tensor(dp[:, :, :, :], xv.unsqueeze(2).to_broadcast([P, 3, EB, NV]),
                                                          ev.unsqueeze(3).to_broadcast([P, 3, EB, NV]), ALU.mult))
                    chain.wait(n)
                    flat = dp[:, :, :, :].rearrange("p k b a -> p k (b a)")
                    n = chain.did(nc.gpsimd.tensor_tensor(dsum[:, :], flat[:, 0, :], flat[:, 1, :], ALU.add))
                    chain.wait(n)
                    last = nc.gpsimd.tensor_tensor(dot[:, 2 * r + t, :], dsum[:, :], flat[:, 2, :], ALU.add)
                    chain.did(last)

            def turn(i):
                for j in range(4):
                    dots(i, j + 1)
                    gather(i, j + 2)
                    scatter(i, j - 1)
            gather(0, 0)
            gather(0, 1)
            dots(0, 0)
            turns(pool, turn)
            scatter(TURNS - 1, 3)
            pool.wait_ge(scattered, 32 * PAIRS)

        @block.scalar
        def _(act):
            def copy_xt(i, j):
                if isinstance(i, int) and 4 * i + j >= PAIRS:
                    return
                j, i = j % 4, i + j // 4
                need(act, bank_ready[2], 2 * (4 * i + j) - 2)
                act.wait_ge(xt_ready, 4 * i + j + 1)
                nc.scalar.copy(xt[:, j % 2, 0, :], p_xt[:, 0:2 * P])
                nc.scalar.copy(xt[0:NV, j % 2, 1, :], p_xt[0:NV, 2 * P:]).then_inc(xt_copied, 1)

            def copy_dott(i, j, t):
                n = 8 * i + 2 * j + t
                need(act, s2_ready, n - 1)
                act.wait_ge(dt_ready, n + 1)
                nc.scalar.copy(dott[:, t, :, :].rearrange("p k e -> p (k e)"), p_dt[:, 0:2 * P]).then_inc(dt_copied, 1)

            def copy_s2(i, j, t):
                n = 8 * i + 2 * j + t
                need(act, bank_read[1], n - 1)
                act.wait_ge(s2_ready, n + 1)
                nc.scalar.copy(init[:, t, 0:NS], p_dt[:, 2 * P:2 * P + NS]).then_inc(s2_copied, 1)

            def copy_z(i, j):
                n = 4 * i + j
                if isinstance(i, int) and n < 0:
                    return
                need(act, out_ready, n - 1)
                act.wait_ge(z_ready, n + 1)
                nc.scalar.copy(zt[:, j % 2, 0, :], p_z[:, 0:2 * P])
                nc.scalar.copy(zt[0:NV + 1, j % 2, 1, :], p_z[0:NV + 1, 2 * P:]).then_inc(z_copied, 1)

            def copy_out(i, j):
                n = 4 * i + j
                if isinstance(i, int) and n < 0:
                    return
                need(act, scattered, 32 * (n - 1))
                act.wait_ge(out_ready, n + 1)
                nc.scalar.copy(out[:, j % 2, :, :].rearrange("p t c -> p (t c)"), p_out[:, 0:2 * D]).then_inc(rows_ready, 1)

            def turn(i):
                for j in range(4):
                    copy_dott(i, j, 0)
                    copy_s2(i, j, 0)
                    copy_xt(i, j + 1)
                    copy_z(i, j - 1)
                    copy_dott(i, j, 1)
                    copy_s2(i, j, 1)
                    copy_out(i, j - 1)
            copy_xt(0, 0)
            turns(act, turn)
            copy_z(TURNS - 1, 3)
            copy_out(TURNS - 1, 3)

        @block.vector
        def _(dve):
            chain = Chain(dve, steps, 13)

            def pair(i, j):
                c, r, s = j // 2, j % 2, j % 2
                n = 4 * i + j
                chain.start(n)
                dve.wait_ge(loaded[c], 48 * (i + 1))
                need(dve, pair_done, n)
                need(dve, z_ready, n - 1)
                need(dve, scattered, 32 * (n - 3))
                mine = index[:, c, 4 + 2 * r:6 + 2 * r]
                pair_row = target_row[:, c, 2 * P * r:2 * P * (r + 1)]
                for t in range(2):
                    ins = nc.vector.scalar_tensor_tensor(hits[:, t, :], pair_row, mine[:, t:t + 1], w["mask"][:, t, :],
                                                         ALU.is_equal, ALU.mult, accum_out=seen[:, s, t:t + 1])
                chain.did(ins)
                k = chain.did(nc.vector.tensor_tensor(away[:, s, :], w["spare"][:, :], mine, ALU.subtract))
                nc.vector.tensor_scalar(same_a[:, s, :], pair_row[:, 0:P], mine[:, 0:1], None, ALU.is_equal)
                nc.vector.tensor_scalar(same_b[:, s, :], pair_row, mine[:, 1:2], None, ALU.is_equal)
                chain.wait(k)
                moved = chain.did(nc.vector.scalar_tensor_tensor(move[:, s, :], seen[:, s, :], REPEAT, away[:, s, :],
                                                                  ALU.is_ge, ALU.mult))
                for t in range(2):
                    m = 2 * n + t
                    a = attr[:, c, 2 * r + t, :]

                    def scaled(b, chain_of, start=None):
                        bank, at, total = tb[b // 3], D * (b % 3), mac[:, t, chain_of, :]
                        return nc.vector.scalar_tensor_tensor(total, bank[:, at:at + D], a[:, b:b + 1],
                                                              total if start is None else start, ALU.mult, ALU.add)
                    dve.wait_ge(bank_ready[3], m + 1)
                    t3 = tb[3][:, 0:EB * NV].rearrange("p (b c) -> p b c", b=EB)
                    ev = a[:, EB:].rearrange("p (k b) -> p k b", k=3)
                    nc.vector.tensor_tensor(vprod[:, t, :, :, :], t3.unsqueeze(1).to_broadcast([P, 3, EB, NV]),
                                            ev.unsqueeze(3).to_broadcast([P, 3, EB, NV]), ALU.mult).then_inc(bank_read[3], 1)
                    dve.wait_ge(bank_ready[0], m + 1)
                    first_0 = chain.did(nc.vector.tensor_scalar(mac[:, t, 0, :], tb[0][:, 0:D], a[:, 0:1], None, ALU.mult))
                    need(dve, bank_read[1], m - 1)
                    dve.wait_ge(bank_read[3], m + 1)
                    vectors = chain.did(nc.vector.tensor_reduce(init[:, t, NS:].rearrange("p (k c) -> p k c", k=3),
                                                                vprod[:, t, :, :, :].rearrange("p k b c -> p k c b"),
                                                                mybir.AxisListType.X, ALU.add))
                    chain.wait(first_0)
                    first_2 = chain.did(scaled(2, 0))
                    if t == 0:
                        chain.wait(moved)
                        nc.vector.tensor_tensor(slot[:, j, :], move[:, s, :], mine, ALU.add)
                    chain.wait(vectors)
                    dve.wait_ge(s2_copied, m + 1)
                    scaled(1, 1, init[:, t, :]).then_inc(bank_read[0], 1)
                    dve.wait_ge(bank_ready[1], m + 1)
                    chain.wait(first_2)
                    first_3 = chain.did(scaled(3, 0))
                    dve.wait_ge(bank_read[0], m + 1)
                    second_4 = chain.did(scaled(4, 1))
                    chain.wait(first_3)
                    scaled(5, 0).then_inc(bank_read[1], 1)
                    dve.wait_ge(bank_ready[2], m + 1)
                    chain.wait(second_4)
                    scaled(6, 1)
                    dve.wait_ge(bank_read[1], m + 1)
                    scaled(7, 0).then_inc(bank_read[2], 1)
                    dve.wait_ge(bank_read[2], m + 1)
                    ins = nc.vector.tensor_tensor(tp[:, s, t, 0:D], mac[:, t, 0, :], mac[:, t, 1, :], ALU.add)
                ins.then_inc(pair_done, 1)

            def turn(i):
                for j in range(4):
                    pair(i, j)
            turns(dve, turn)

        @block.tensor
        def _(pe):
            def transpose_x(i, j):
                if isinstance(i, int) and 4 * i + j >= PAIRS:
                    return
                j, i = j % 4, i + j // 4
                need(pe, xt_copied, 4 * i + j)
                pe.wait_ge(gathered[j], 32 * (i + 1))
                for t in range(2):
                    nc.tensor.transpose(p_xt[:, t * P:(t + 1) * P], rows[:, j, t, 0:P], w["ident"][:, :])
                    last = nc.tensor.transpose(p_xt[0:NV, (2 + t) * P:(3 + t) * P], rows[:, j, t, P:D], w["ident"][:, :])
                last.then_inc(xt_ready, 1)

            def transpose_dot(i, j, t):
                n = 8 * i + 2 * j + t
                need(pe, s2_copied, n)
                pe.wait_ge(dot_steps, 3 * (n + 1))
                for k in range(2):
                    last = nc.tensor.transpose(p_dt[:, k * P:(k + 1) * P], dot[:, (2 * j + t) % 4, k * P:(k + 1) * P], w["ident"][:, :])
                last.then_inc(dt_ready, 1)

            def products(i, j, t):
                n = 8 * i + 2 * j + t
                s = j % 2
                pe.wait_ge(xt_copied, 4 * i + j + 1)
                xa = xt[:, s, 0, t * P:(t + 1) * P]
                xb = xt[0:NV, s, 1, t * P:(t + 1) * P]
                for k, nb in ((3, 0), (0, 3), (1, 3), (2, 2)):
                    need(pe, bank_read[k], n)
                    if k == 1:
                        scalars(i, j, t)
                    if k == 3:
                        last = nc.tensor.matmul(tb[3][:, 0:EB * NV], xa[0:NS, :], w["l0_w3"][:, :], start=True, stop=True)
                    else:
                        view = tb[k][:, 0:nb * D].rearrange("p (b c) -> p b c", b=nb)
                        nc.tensor.matmul(view[:, :, 0:P], xa, w["l0_w14"][:, 3 * P * k:3 * P * k + nb * P], start=True, stop=True)
                        last = nc.tensor.matmul(view[:, :, P:D], xb, w["l0_w4"][:, 3 * NV * k:3 * NV * k + nb * NV], start=True, stop=True)
                    last.then_inc(bank_ready[k], 1)

            def scalars(i, j, t):
                n = 8 * i + 2 * j + t
                pe.wait_ge(dt_copied, n + 1)
                for k in range(2):
                    last = nc.tensor.matmul(p_dt[:, 2 * P:2 * P + NS], dott[:, t, k, :], w["l0_w2"][:, k * NS:(k + 1) * NS],
                                            start=(k == 0), stop=(k == 1))
                last.then_inc(s2_ready, 1)

            def sums(i, j):
                n = 4 * i + j
                if isinstance(i, int) and n < 0:
                    return
                s = j % 2
                need(pe, z_copied, n)
                pe.wait_ge(pair_done, n + 1)
                for k, (lo, hi) in enumerate(((0, P), (P, D + 1))):
                    z = p_z[0:hi - lo, 2 * P * k:2 * P * (k + 1)]
                    nc.tensor.matmul(z, tp[:, s, 1, lo:hi], same_b[:, s, :], start=True, stop=False)
                    last = nc.tensor.matmul(z[:, 0:P], tp[:, s, 0, lo:hi], same_a[:, s, :], start=False, stop=True)
                last.then_inc(z_ready, 1)

            def outputs(i, j):
                n = 4 * i + j
                if isinstance(i, int) and n < 0:
                    return
                need(pe, rows_ready, n)
                pe.wait_ge(z_copied, n + 1)
                for t in range(2):
                    o = p_out[:, t * D:(t + 1) * D]
                    nc.tensor.matmul(o, zt[:, j % 2, 0, t * P:(t + 1) * P], w["l0_out_a"][:, :], start=True, stop=False)
                    last = nc.tensor.matmul(o, zt[0:NV + 1, j % 2, 1, t * P:(t + 1) * P], w["l0_out_b"][:, :], start=False, stop=True)
                last.then_inc(out_ready, 1)

            def turn(i):
                for j in range(4):
                    transpose_dot(i, j, 0)
                    products(i, j, 0)
                    transpose_x(i, j + 1)
                    sums(i, j - 1)
                    transpose_dot(i, j, 1)
                    products(i, j, 1)
                    outputs(i, j - 1)
            transpose_x(0, 0)
            turns(pe, turn)
            sums(TURNS - 1, 3)
            outputs(TURNS - 1, 3)


def edge_conv(nc, w, dram, layer, table, acc, width, next_acc, next_width):
    conv = CONVS[layer]
    nf, hidden = conv["features"], conv["hidden"]
    find = layer == 1
    with ExitStack() as ctx:
        pre = f"c{layer}_"
        sem = lambda name: ctx.enter_context(nc.semaphore(pre + name))
        sb = lambda name, shape, dt=F32: ctx.enter_context(nc.sbuf_tensor("s_" + pre + name, shape, dt))
        pb = lambda name: ctx.enter_context(nc.psum_tensor(pre + name, [P, 512], F32))
        features = sb("features", [nf, 2, QUAD])
        target_row = sb("target_row", [P, 2, QUAD], I32)
        index = sb("index", [P, 2, 8], I32)
        attr = sb("attr", [P, 2, 4, 4])
        rows = sb("rows", [P, 4, 2, D])
        hid = sb("hid", [hidden, 2, QUAD])
        pw = sb("pw", [P, 2, 2, 2, NS])
        vw = sb("vw", [P, 2, 2, 3, NV])
        dv = sb("dv", [P, 2, 2, 3, NV])
        ds = sb("ds", [P, 2, 2, 2, NV])
        mid = sb("mid", [P, 2, 2, 3, P])
        same_a = sb("same_a", [P, 2, P])
        same_b = sb("same_b", [P, 2, 2 * P])
        hits = sb("hits", [P, 2, 2 * P])
        away = sb("away", [P, 2, 2])
        move = sb("move", [P, 2, 2])
        slot = sb("slot", [P, 4, 2], I32)
        zt = sb("zt", [P, 2, 3, 2 * P])
        out = sb("out", [P, 2, 2, width])
        p_hid = pb("p_hid")
        p_w = [pb(f"p_w{r}") for r in range(2)]
        p_z = [ctx.enter_context(nc.psum_tensor(pre + f"p_z{r}", [P, 1024], F32)) for r in range(2)]
        p_out = pb("p_out")
        off = 1 if layer == 3 else 0
        ow = off + D

        loaded = [sem(f"loaded{c}") for c in range(2)]
        gathered = [sem(f"gathered{j}") for j in range(4)]
        zeroed = sem("zeroed")
        hid_ready, silu_done = sem("hid_ready"), sem("silu_done")
        w_ready = sem("w_ready")
        steps, pair_done = sem("steps"), sem("pair_done")
        z_ready, z_copied = sem("z_ready"), sem("z_copied")
        out_ready, rows_ready = sem("out_ready"), sem("rows_ready")
        scattered = sem("scattered")
        block = ctx.enter_context(nc.Block())

        @block.sync
        def _(sp):
            def turn(i):
                for c in range(2):
                    q = 2 * i + c
                    need(sp, pair_done, 2 * q - 2)
                    sp.nop(nofuse=True)
                    need(sp, hid_ready, q - 1)
                    sp.nop(nofuse=True)
                    sp.dma_start(target_row[:, c, :], dram["dst_row"][bass.ds(q, 1), :].to_broadcast([P, QUAD])).then_inc(loaded[c], 16)
                    sp.dma_start(index[:, c, :], dram["index1"][bass.ds(q * P, P), :]).then_inc(loaded[c], 16)
                    sp.dma_start(attr[:, c, :, :].rearrange("p t k -> p (t k)"), dram["attr4"][bass.ds(q * P, P), :]).then_inc(loaded[c], 16)
                    sp.dma_start(features[:, c, :], dram[f"features{nf}"][:, bass.ds(q * QUAD, QUAD)]).then_inc(loaded[c], 16)
                if next_acc is not None:
                    sp.dma_start(next_acc[bass.ds(i * STEP, STEP), :].rearrange("(p r) c -> p (r c)", p=P),
                                 w["zeros"][:, 0:8 * next_width]).then_inc(zeroed, 16)
            turns(sp, turn)
            if next_acc is not None:
                sp.dma_start(next_acc[PADDED:ACC_ROWS, :].rearrange("(p r) c -> p (r c)", p=P),
                             w["zeros"][:, 0:2 * next_width]).then_inc(zeroed, 16)
                sp.wait_ge(zeroed, 16 * (TURNS + 1))

        @block.gpsimd
        def _(pool):
            def gather(i, j):
                if isinstance(i, int) and 4 * i + j >= PAIRS:
                    return
                j, i = j % 4, i + j // 4
                c, r = j // 2, j % 2
                need(pool, pair_done, 4 * i + j - 3)
                pool.wait_ge(loaded[c], 64 * (i + 1))
                for t in range(2):
                    pool.nop(nofuse=True)
                    pool.indirect_dma_start(rows[:, j, t, :], None, table,
                                            bass.IndirectOffsetOnAxis(ap=index[:, c, 2 * r + t:2 * r + t + 1], axis=0)
                                            ).then_inc(gathered[j], 16)

            def scatter(i, j):
                if isinstance(i, int) and 4 * i + j < 0:
                    return
                need(pool, scattered, 32 * (4 * i + j))
                pool.wait_ge(rows_ready, 4 * i + j + 1)
                for t in range(2):
                    pool.nop(nofuse=True)
                    pool.indirect_dma_start(acc, bass.IndirectOffsetOnAxis(ap=slot[:, j % 4, t:t + 1], axis=0),
                                            out[:, j % 2, t, :], None, compute_op=ALU.add).then_inc(scattered, 16)

            def turn(i):
                for j in range(4):
                    gather(i, j + 2)
                    scatter(i, j - 1)
            gather(0, 0)
            gather(0, 1)
            turns(pool, turn)
            scatter(TURNS - 1, 3)
            pool.wait_ge(scattered, 32 * PAIRS)

        @block.scalar
        def _(act):
            def silu(i, c):
                if isinstance(i, int) and 2 * i + c >= QUADS:
                    return
                c, i = c % 2, i + c // 2
                q = 2 * i + c
                need(act, w_ready, 2 * q - 2)
                act.wait_ge(hid_ready, q + 1)
                nc.scalar.activation(hid[:, c, :], p_hid[0:hidden, :], ACT.Silu, scale=1.0 / math.sqrt(nf)).then_inc(silu_done, 1)

            def copy_z(i, j):
                n = 4 * i + j
                need(act, out_ready, n - 1)
                act.wait_ge(z_ready, n + 1)
                nc.scalar.copy(zt[:, j % 2, :, :].rearrange("p k e -> p (k e)"), p_z[j % 2][:, 0:6 * P]).then_inc(z_copied, 1)

            def copy_out(i, j):
                n = 4 * i + j
                if isinstance(i, int) and n < 0:
                    return
                need(act, scattered, 32 * (n - 1))
                act.wait_ge(out_ready, n + 1)
                src = p_out[:, 0:2 * ow].rearrange("p (t c) -> p t c", t=2)
                last = nc.scalar.copy(out[:, j % 2, :, 0:ow], src)
                if layer == 3:
                    last = nc.scalar.copy(out[:, j % 2, :, D + 1:D + 2], w["seen"][:, bass.ds(2 * n, 2)].unsqueeze(2))
                last.then_inc(rows_ready, 1)

            def turn(i):
                for j in range(4):
                    if j % 2 == 0:
                        silu(i, j // 2 + 1)
                    copy_z(i, j)
                    copy_out(i, j - 1)
            silu(0, 0)
            turns(act, turn)
            copy_out(TURNS - 1, 3)

        @block.vector
        def _(dve):
            chain = Chain(dve, steps, 9 if find else 5)

            def pair(i, j):
                c, r, s = j // 2, j % 2, j % 2
                n = 4 * i + j
                chain.start(n)
                dve.wait_ge(loaded[c], 64 * (i + 1))
                need(dve, pair_done, n)
                need(dve, z_ready, n - 1)
                need(dve, scattered, 32 * (n - 3))
                mine = index[:, c, 4 + 2 * r:6 + 2 * r]
                pair_row = target_row[:, c, 2 * P * r:2 * P * (r + 1)]
                nc.vector.tensor_scalar(same_a[:, s, :], pair_row[:, 0:P], mine[:, 0:1], None, ALU.is_equal)
                nc.vector.tensor_scalar(same_b[:, s, :], pair_row, mine[:, 1:2], None, ALU.is_equal)
                if find:
                    for t in range(2):
                        last = nc.vector.scalar_tensor_tensor(hits[:, t, :], pair_row, mine[:, t:t + 1], w["mask"][:, t, :],
                                                              ALU.is_equal, ALU.mult, accum_out=w["seen"][:, bass.ds(2 * n + t, 1)])
                    chain.did(last)
                    k = chain.did(nc.vector.tensor_tensor(away[:, s, :], w["spare"][:, :], mine, ALU.subtract))
                    chain.wait(k)
                    k = chain.did(nc.vector.scalar_tensor_tensor(move[:, s, :], w["seen"][:, bass.ds(2 * n, 2)], REPEAT, away[:, s, :],
                                                                 ALU.is_ge, ALU.mult))
                    chain.wait(k)
                    k = chain.did(nc.vector.tensor_tensor(slot[:, j, :], move[:, s, :], mine, ALU.add))
                    chain.wait(k)
                    nc.vector.tensor_copy(w["slots"][:, bass.ds(2 * n, 2)], slot[:, j, :])
                else:
                    nc.vector.tensor_copy(slot[:, j, :], w["slots"][:, bass.ds(2 * n, 2)])
                dve.wait_ge(gathered[j], 32 * (i + 1))
                y = attr[:, c, 2 * r:2 * r + 2, :]
                e0 = rows[:, j, :, 0:NS]
                e1 = rows[:, j, :, NS:D].rearrange("p t (k u) -> p t k u", k=3)
                y1 = y[:, :, 1:4].unsqueeze(3)
                k_dv = chain.did(nc.vector.tensor_tensor(dv[:, s], e1, y1.to_broadcast([P, 2, 3, NV]), ALU.mult))
                dve.wait_ge(w_ready, n + 1)
                pwv = p_w[r][:, 0:384].rearrange("p (t m) -> p t m", t=2)
                k_pw = chain.did(nc.vector.tensor_tensor(
                    pw[:, s], pwv[:, :, 0:2 * NS].rearrange("p t (k u) -> p t k u", k=2),
                    e0.unsqueeze(2).to_broadcast([P, 2, 2, NS]), ALU.mult))
                k_vw = chain.did(nc.vector.tensor_tensor(
                    vw[:, s], pwv[:, :, 2 * NS:2 * NS + NV].unsqueeze(2).to_broadcast([P, 2, 3, NV]), e1, ALU.mult))
                chain.wait(k_dv)
                k_ds = chain.did(nc.vector.tensor_tensor(ds[:, s, :, 0, :], dv[:, s, :, 0, :], dv[:, s, :, 1, :], ALU.add))
                chain.wait(k_pw)
                nc.vector.tensor_tensor(mid[:, s, :, :, 0:NS], pw[:, s, :, 1, :].unsqueeze(2).to_broadcast([P, 2, 3, NS]),
                                        y1.to_broadcast([P, 2, 3, NS]), ALU.mult)
                chain.wait(k_ds)
                k_ds = chain.did(nc.vector.tensor_tensor(ds[:, s, :, 1, :], ds[:, s, :, 0, :], dv[:, s, :, 2, :], ALU.add))
                nc.vector.tensor_tensor(mid[:, s, :, :, NS:NS + NV], vw[:, s], y[:, :, 0:1].unsqueeze(3).to_broadcast([P, 2, 3, NV]), ALU.mult)
                nc.vector.tensor_tensor(mid[:, s, :, 1:3, NS + NV:], pw[:, s, :, 0, :].rearrange("p t (k u) -> p t k u", k=2),
                                        y[:, :, 0:1].unsqueeze(3).to_broadcast([P, 2, 2, NV]), ALU.mult)
                chain.wait(k_ds)
                nc.vector.tensor_tensor(mid[:, s, :, 0, NS + NV:], pwv[:, :, 2 * NS + NV:], ds[:, s, :, 1, :], ALU.mult).then_inc(pair_done, 1)

            def turn(i):
                for j in range(4):
                    pair(i, j)
            turns(dve, turn)

        @block.tensor
        def _(pe):
            def hidden_layer(i, c):
                if isinstance(i, int) and 2 * i + c >= QUADS:
                    return
                c, i = c % 2, i + c // 2
                q = 2 * i + c
                need(pe, silu_done, q)
                pe.wait_ge(loaded[c], 64 * (i + 1))
                nc.tensor.matmul(p_hid[0:hidden, :], w[pre + "fc1"][:, :], features[:, c, :], start=True, stop=True).then_inc(hid_ready, 1)

            def edge_weights(i, j):
                if isinstance(i, int) and 4 * i + j >= PAIRS:
                    return
                j, i = j % 4, i + j // 4
                c, r = j // 2, j % 2
                need(pe, pair_done, 4 * i + j - 1)
                pe.wait_ge(silu_done, 2 * i + c + 1)
                for t in range(2):
                    last = nc.tensor.matmul(p_w[r][:, t * 192:(t + 1) * 192], hid[:, c, (2 * r + t) * P:(2 * r + t + 1) * P],
                                            w[pre + "fc2"][:, :], start=True, stop=True)
                last.then_inc(w_ready, 1)

            def sums(i, j):
                n, s = 4 * i + j, j % 2
                need(pe, z_copied, n - 1)
                pe.wait_ge(pair_done, n + 1)
                for k in range(3):
                    z = p_z[s][:, 2 * P * k:2 * P * (k + 1)]
                    nc.tensor.matmul(z, mid[:, s, 1, k, :], same_b[:, s, :], start=True, stop=False)
                    last = nc.tensor.matmul(z[:, 0:P], mid[:, s, 0, k, :], same_a[:, s, :], start=False, stop=True)
                last.then_inc(z_ready, 1)

            def outputs(i, j):
                n = 4 * i + j
                if isinstance(i, int) and n < 0:
                    return
                need(pe, rows_ready, n)
                pe.wait_ge(z_copied, n + 1)
                for t in range(2):
                    for a, k in enumerate((2, 0, 1)):
                        cols = off + NS + NV * (k + 1)
                        last = nc.tensor.matmul(p_out[:, t * ow:t * ow + cols], zt[:, j % 2, k, t * P:(t + 1) * P],
                                                w[pre + "out"][:, k * ow:k * ow + cols], start=(a == 0), stop=(a == 2))
                last.then_inc(out_ready, 1)

            def turn(i):
                for j in range(4):
                    if j % 2 == 0:
                        hidden_layer(i, j // 2 + 1)
                    edge_weights(i, j + 1)
                    sums(i, j)
                    outputs(i, j - 1)
            hidden_layer(0, 0)
            edge_weights(0, 0)
            turns(pe, turn)
            outputs(TURNS - 1, 3)


def node_pass(nc, w, dram, after, source, acc, width, table, base, result):
    first, final = after == 0, after == 3
    off = 1 if final else 0
    with ExitStack() as ctx:
        pre = f"n{after}_"
        sem = lambda name: ctx.enter_context(nc.semaphore(pre + name))
        sb = lambda name, shape, dt=F32: ctx.enter_context(nc.sbuf_tensor("s_" + pre + name, shape, dt))
        pb = lambda name: ctx.enter_context(nc.psum_tensor(pre + name, [P, 512], F32))
        src = sb("src", [P, RING, 4, D])
        agg = sb("agg", [P, RING, 4, width])
        coef = sb("coef", [P, RING, 5, 4])
        xr = sb("xr", [P, RING, 4, D])
        part = sb("part", [P, RING, 4, D])
        total = sb("total", [P, RING, 4])
        nmean = sb("nmean", [P, RING, 4])
        square = sb("square", [P, RING, 4, D])
        ssq = sb("ssq", [P, RING, 4])
        std = sb("std", [P, RING, 4])
        rstd = sb("rstd", [P, RING, 4])
        xn = sb("xn", [P, RING, 4, D])
        xta = sb("xta", [P, 2, 4 * P])
        xtb = sb("xtb", [NV + 1, 2, 4 * P])
        fta = sb("fta", [P, 2, 4 * P])
        ftb = sb("ftb", [NV + 1, 2, 4 * P])
        bout = sb("bout", [P, 2, 4, D])
        tout = sb("tout", [P, 2, 4, D])
        p_ta, p_tb = pb("p_ta"), pb("p_tb")
        p_o = [pb(f"p_o{t}") for t in range(4)]
        p_u = [pb(f"p_u{t}") for t in range(2)]

        stores = RING if final else 2
        loaded = [sem(f"loaded{c}") for c in range(RING)]
        if first:
            ones = sem("ones")
            f_ready, f_copied, u_ready = sem("f_ready"), sem("f_copied"), sem("u_ready")
        steps, norm_steps, square_steps = sem("steps"), sem("norm_steps"), sem("square_steps")
        sum_done, std_done, xn_done = sem("sum_done"), sem("std_done"), sem("xn_done")
        if not final:
            t_ready, t_copied, o_ready = sem("t_ready"), sem("t_copied"), sem("o_ready")
            base_done, table_done = sem("base_done"), sem("table_done")
        stored = [sem(f"stored{c}") for c in range(stores)]
        block = ctx.enter_context(nc.Block())
        view = lambda a, q: a[bass.ds(q * QUAD, QUAD), :].rearrange("(p r) c -> p (r c)", p=P)
        flat = lambda a, c: a[:, c].rearrange("p t k -> p (t k)")
        z_of = lambda q, t: w["z_node"][:, bass.ds(4 * q + t, 1)]
        per_store = 16 if final else 32

        def quad(i, c):
            i, c = i + c // RING, c % RING
            q = RING * i + c
            if isinstance(q, int) and not 0 <= q < QUADS:
                return None
            return i, c, q

        def steps_of(eng, step):
            def turn(i):
                for c in range(RING):
                    step(i, c)
            turn(-1)
            turn(0)
            with eng.Fori(1, NODE_TURNS - 2) as i:
                turn(i)
            turn(NODE_TURNS - 2)
            turn(NODE_TURNS - 1)

        def wait_stored(eng, i, c):
            if final:
                need(eng, stored[c], per_store * i)
            else:
                need(eng, stored[c % 2], per_store * (2 * i + c // 2))

        @block.sync
        def _(sp):
            def step(i, c):
                at = quad(i, c + 4)
                if at is None:
                    return
                i, c, q = at
                need(sp, sum_done, q - 3)
                sp.nop(nofuse=True)
                sp.dma_start(flat(src, c), view(source, q)).then_inc(loaded[c], 16)
                sp.dma_start(flat(agg, c), view(acc, q)).then_inc(loaded[c], 16)
            steps_of(sp, step)
            for c in range(stores):
                sp.wait_ge(stored[c], per_store * len(range(c, QUADS, stores)))

        @block.gpsimd
        def _(pool):
            def step(i, c):
                at = quad(i, c)
                if at is None:
                    return
                i, c, q = at
                if final:
                    pool.wait_ge(xn_done, q + 1)
                    pool.nop(nofuse=True)
                    pool.dma_start(view(result, q), flat(xn, c)).then_inc(stored[c], 16)
                else:
                    pool.wait_ge(base_done, 4 * q + 4)
                    pool.nop(nofuse=True)
                    pool.dma_start(view(base, q), flat(bout, c % 2)).then_inc(stored[c % 2], 16)
                    pool.wait_ge(table_done, 4 * q + 4)
                    pool.nop(nofuse=True)
                    pool.dma_start(view(table, q), flat(tout, c % 2)).then_inc(stored[c % 2], 16)
            steps_of(pool, step)

        @block.scalar
        def _(act):
            def copy_front(at):
                if at is None:
                    return
                i, c, q = at
                need(act, u_ready, q - 1)
                act.wait_ge(f_ready, q + 1)
                nc.scalar.copy(fta[:, c % 2, :], p_ta[:, :])
                nc.scalar.copy(ftb[0:NV, c % 2, :], p_tb[0:NV, :]).then_inc(f_copied, 1)

            def squares(at):
                if at is None:
                    return
                i, c, q = at
                need(act, std_done, q - 3)
                need(act, xn_done, q - 3)
                act.wait_ge(sum_done, q + 1)
                for t in range(4):
                    last = nc.scalar.activation(square[:, c, t, :], xr[:, c, t, :], ACT.Square, bias=nmean[:, c, t:t + 1],
                                                accum_out=ssq[:, c, t:t + 1])
                last.then_inc(square_steps, 1)
                act.wait_ge(square_steps, q + 1)
                nc.scalar.activation(std[:, c, :], ssq[:, c, :], ACT.Sqrt, scale=1.0 / D, bias=w["eps"][:, :]).then_inc(std_done, 1)

            def copy_t(at):
                if at is None:
                    return
                i, c, q = at
                need(act, o_ready, 4 * q - 4)
                act.wait_ge(t_ready, q + 1)
                nc.scalar.copy(xta[:, c % 2, :], p_ta[:, :])
                nc.scalar.copy(xtb[0:NV, c % 2, :], p_tb[0:NV, :]).then_inc(t_copied, 1)

            def messages(at):
                if at is None:
                    return
                i, c, q = at
                wait_stored(act, i, c)
                for t in range(4):
                    act.wait_ge(base_done, 4 * q + t + 1)
                    nc.scalar.activation(tout[:, c % 2, t, :], p_o[t][:, D:2 * D], ACT.Copy, scale=z_of(q, t)).then_inc(table_done, 1)

            def step(i, c):
                if first:
                    copy_front(quad(i, c + 4))
                squares(quad(i, c + 2))
                if not final:
                    copy_t(quad(i, c))
                    messages(quad(i, c - 1))
            steps_of(act, step)

        @block.vector
        def _(dve):
            chain = Chain(dve, steps, 6 if final else 2 if first else 1)

            def sums(at):
                if at is None:
                    return
                i, c, q = at
                if not final:
                    chain.start(q)
                dve.wait_ge(loaded[c], 32 * (i + 1))
                need(dve, xn_done, q - 3)
                if first:
                    dve.wait_ge(u_ready, q + 1)
                    for t in range(4):
                        ins = nc.vector.scalar_tensor_tensor(part[:, c, t, :], src[:, c, t, :], 2.0,
                                                             p_u[t // 2][:, (t % 2) * D:(t % 2 + 1) * D], ALU.mult, ALU.add)
                    chain.wait(chain.did(ins))
                    ins = [nc.vector.scalar_tensor_tensor(xr[:, c, t, :], part[:, c, t, :], 1.0, agg[:, c, t, :], ALU.mult,
                                                          ALU.add, accum_out=total[:, c, t:t + 1]) for t in range(4)][-1]
                elif final:
                    chain.wait(5)
                    ins = [nc.vector.scalar_tensor_tensor(xr[:, c, t, :], agg[:, c, t, 1:1 + D], coef[:, c, 4, t:t + 1],
                                                          src[:, c, t, :], ALU.mult, ALU.add,
                                                          accum_out=total[:, c, t:t + 1]) for t in range(4)][-1]
                else:
                    ins = [nc.vector.scalar_tensor_tensor(xr[:, c, t, :], agg[:, c, t, :], z_of(q, t), src[:, c, t, :],
                                                          ALU.mult, ALU.add,
                                                          accum_out=total[:, c, t:t + 1]) for t in range(4)][-1]
                chain.wait(chain.did(ins))
                nc.vector.tensor_scalar(nmean[:, c, :], total[:, c, :], -1.0 / D, None, ALU.mult).then_inc(sum_done, 1)

            def factor_step(at, k):
                if not final or at is None:
                    return
                i, c, q = at
                cf = lambda k: coef[:, c, k, :].unsqueeze(2)
                if k == 0:
                    chain.start(q)
                    dve.wait_ge(loaded[c], 32 * (i + 1))
                    need(dve, xn_done, q - 3)
                    chain.did(nc.vector.tensor_scalar(cf(0), agg[:, c, :, D + 1:D + 2], 1.0, None, ALU.max))
                    return
                chain.wait(k)
                if k == 1:
                    chain.did(nc.vector.reciprocal(cf(1), cf(0)))
                elif k == 2:
                    chain.did(nc.vector.tensor_tensor(coef[:, c, 2, :], coef[:, c, 1, :], w["z_node"][:, bass.ds(4 * q, 4)], ALU.mult))
                elif k == 3:
                    chain.did(nc.vector.tensor_tensor(cf(3), cf(2), cf(2), ALU.mult))
                else:
                    chain.did(nc.vector.tensor_tensor(cf(4), cf(3), agg[:, c, :, 0:1], ALU.mult))

            def norm(at, ahead):
                if at is None:
                    for k in range(5):
                        factor_step(ahead, k)
                    return
                i, c, q = at
                dve.wait_ge(std_done, q + 1)
                nc.vector.reciprocal(rstd[:, c, :], std[:, c, :]).then_inc(norm_steps, 1)
                if final:
                    wait_stored(dve, i, c)
                else:
                    need(dve, t_ready, q - 3)
                    need(dve, base_done, 4 * q - 12)
                factor_step(ahead, 0)
                dve.wait_ge(norm_steps, q + 1)
                for t in range(4):
                    ins = nc.vector.tensor_scalar(xn[:, c, t, :], xr[:, c, t, :], nmean[:, c, t:t + 1], rstd[:, c, t:t + 1],
                                                  ALU.add, ALU.mult)
                    if t == 3:
                        ins.then_inc(xn_done, 1)
                    factor_step(ahead, t + 1)

            def self_term(at):
                if at is None:
                    return
                i, c, q = at
                wait_stored(dve, i, c)
                for t in range(4):
                    dve.wait_ge(o_ready, 4 * q + t + 1)
                    nc.vector.scalar_tensor_tensor(bout[:, c % 2, t, :], p_o[t][:, 0:D], z_of(q, t), xn[:, c, t, :],
                                                   ALU.mult, ALU.add).then_inc(base_done, 1)

            def step(i, c):
                norm(quad(i, c + 1), quad(i, c + 3))
                sums(quad(i, c + 3))
                if not final:
                    self_term(quad(i, c - 1))
            if first:
                nc.vector.memset(ftb[:, :, :], 1.0).then_inc(ones, 1)
            steps_of(dve, step)

        if final:
            return

        @block.tensor
        def _(pe):
            def transpose(src_slot):
                for t in range(4):
                    nc.tensor.transpose(p_ta[:, t * P:(t + 1) * P], src_slot[:, t, 0:P], w["ident"][:, :])
                    last = nc.tensor.transpose(p_tb[0:NV, t * P:(t + 1) * P], src_slot[:, t, P:D], w["ident"][:, :])
                return last

            def front_transposes(at):
                if at is None:
                    return
                i, c, q = at
                need(pe, t_copied, q - 4)
                pe.wait_ge(loaded[c], 32 * (i + 1))
                transpose(src[:, c]).then_inc(f_ready, 1)

            def front_products(at):
                if at is None:
                    return
                i, c, q = at
                need(pe, sum_done, q)
                pe.wait_ge(f_copied, q + 1)
                for t in range(4):
                    o = p_u[t // 2][:, (t % 2) * D:(t % 2 + 1) * D]
                    nc.tensor.matmul(o, fta[:, c % 2, t * P:(t + 1) * P], w["u_a"][:, :], start=True, stop=False)
                    last = nc.tensor.matmul(o, ftb[:, c % 2, t * P:(t + 1) * P], w["u_b"][:, :], start=False, stop=True)
                last.then_inc(u_ready, 1)

            def transposes(at):
                if at is None:
                    return
                i, c, q = at
                need(pe, t_copied, q)
                if first:
                    pe.wait_ge(f_copied, min(q + 5, QUADS) if isinstance(q, int) else q + 5)
                pe.wait_ge(xn_done, q + 1)
                transpose(xn[:, c]).then_inc(t_ready, 1)

            def products(at):
                if at is None:
                    return
                i, c, q = at
                pe.wait_ge(t_copied, q + 1)
                for t in range(4):
                    need(pe, table_done, 4 * (q - 1) + t + 1)
                    o = p_o[t][:, 0:2 * D].rearrange("p (k c) -> p k c", k=2)
                    nc.tensor.matmul(o[:, :, 0:P], xta[:, c % 2, t * P:(t + 1) * P], w[f"node{after + 1}_a"][:, :], start=True, stop=True)
                    nc.tensor.matmul(o[:, :, P:D], xtb[0:NV, c % 2, t * P:(t + 1) * P], w[f"node{after + 1}_b"][:, :],
                                     start=True, stop=True).then_inc(o_ready, 1)

            def step(i, c):
                if first:
                    front_transposes(quad(i, c + 4))
                    products(quad(i, c - 1))
                    transposes(quad(i, c))
                    front_products(quad(i, c + 4))
                else:
                    transposes(quad(i, c))
                    products(quad(i, c - 1))
            if first:
                pe.wait_ge(ones, 1)
            steps_of(pe, step)


CONVS = {
    1: dict(features=12, hidden=100, self_factor=math.sin(math.pi / 8), factor=math.cos(math.pi / 8) / math.sqrt(8.0 * 96 * 100)),
    2: dict(features=16, hidden=64, self_factor=math.sin(math.pi / 8), factor=math.cos(math.pi / 8) / math.sqrt(10.0 * 96 * 64)),
    3: dict(features=16, hidden=64, self_factor=1.0, factor=1.0 / math.sqrt(96.0 * 64)),
}

FACTORS = [
    ("l0_w14", (0, NS), (0, EB * P), 1 / math.sqrt(2.0 * NS * EB)),
    ("l0_w14", (NS, P), (0, EB * P), 1 / math.sqrt(2.0 * NV * EB)),
    ("l0_w4", (0, NV), (0, EB * NV), 1 / math.sqrt(2.0 * NV * EB)),
    ("l0_w3", (0, NS), (0, EB * NV), 1 / math.sqrt(2.0 * NS * EB)),
    ("l0_w2", (0, P), (0, 2 * NS), 1 / math.sqrt(3.0 * 2.0 * NV * EB)),
]
for _l, _c in CONVS.items():
    _ow = D + (_l == 3)
    FACTORS += [
        (f"c{_l}_out", (0, P - NV), (0, 3 * _ow), _c["factor"]),
        (f"c{_l}_out", (P - NV, P), (0, _ow), _c["factor"] / math.sqrt(3.0)),
        (f"c{_l}_out", (P - NV, P), (_ow, 3 * _ow), _c["factor"]),
        (f"node{_l}_a", (0, P), (0, NS), _c["self_factor"] / math.sqrt(NS)),
        (f"node{_l}_a", (0, P), (NS, P), _c["self_factor"] / math.sqrt(NV)),
        (f"node{_l}_a", (0, P), (P, P + NS), 1 / math.sqrt(NS)),
        (f"node{_l}_a", (0, P), (P + NS, 2 * P), 1 / math.sqrt(NV)),
        (f"node{_l}_b", (0, NV), (0, NV), _c["self_factor"] / math.sqrt(NV)),
        (f"node{_l}_b", (0, NV), (NV, 2 * NV), 1 / math.sqrt(NV)),
    ]


def build(nc, dram, result):
    scratch = lambda name, rows, cols: nc.dram_tensor(name, [rows, cols], F32).ap()
    table = scratch("table", PADDED, D)
    bases = [scratch(f"base{k}", PADDED, D) for k in range(2)]
    accs = [scratch(f"acc{k}", ACC_ROWS, D) for k in range(2)]
    acc3 = scratch("acc3", ACC_ROWS, D + 2)
    with ExitStack() as ctx:
        w = {}
        for name in WEIGHTS:
            w[name] = ctx.enter_context(nc.sbuf_tensor("w_" + name, list(dram[name].shape), F32))
        w["loads"], w["factors"] = WEIGHTS, FACTORS
        for name, shape, dt in (("ident", [P, P], F32), ("zeros", [P, 8 * (D + 2)], F32), ("tp", [P, 2, 2, D + 1], F32),
                                ("mask", [P, 2, 2 * P], F32), ("spare", [P, 2], I32), ("eps", [P, 1], F32),
                                ("l0_out_a", [P, D], F32), ("l0_out_b", [NV + 1, D], F32),
                                ("seen", [P, 2 * PAIRS], F32), ("slots", [P, 2 * PAIRS], I32)):
            w[name] = ctx.enter_context(nc.sbuf_tensor("w_" + name, shape, dt))
        prepare_weights(nc, w, dram)
        zero_accumulator(nc, w, accs[0], D)
        edge_layer0(nc, w, dram, dram["x"], accs[0], accs[1], D)
        node_pass(nc, w, dram, 0, dram["x"], accs[0], D, table, bases[0], None)
        edge_conv(nc, w, dram, 1, table, accs[1], D, accs[0], D)
        node_pass(nc, w, dram, 1, bases[0], accs[1], D, table, bases[1], None)
        edge_conv(nc, w, dram, 2, table, accs[0], D, acc3, D + 2)
        node_pass(nc, w, dram, 2, bases[1], accs[0], D, table, bases[0], None)
        edge_conv(nc, w, dram, 3, table, acc3, D + 2, None, 0)
        node_pass(nc, w, dram, 3, bases[0], acc3, D + 2, None, None, result)


WEIGHTS = (["z_node", "l0_w14", "l0_w4", "l0_w3", "l0_w2", "wm_t_a", "wm_t_b", "wu2_a", "wu2_b", "u_a", "u_b"]
           + [f"c{l}_{m}" for l in (1, 2, 3) for m in ("fc1", "fc2", "out")]
           + [f"node{l}_{m}" for l in (1, 2, 3) for m in ("a", "b")])


def lay_out(inputs):
    import numpy as np
    a = {k: np.asarray(v) for k, v in inputs.items()}
    extra = PADDED - ROWS

    def by_component(m, axis):
        m = np.moveaxis(m, axis, 0)
        v = m[NS:].reshape((NV, 3) + m.shape[1:])
        v = np.swapaxes(v, 0, 1).reshape((3 * NV,) + m.shape[1:])
        return np.moveaxis(np.concatenate([m[:NS], v]), 0, axis)

    def pad(m, value=0):
        return np.concatenate([m, np.full((extra,) + m.shape[1:], value, m.dtype)])

    d = {}
    d["x"] = pad(by_component(a["x"], 1))
    src, dst = pad(a["src"], ROWS), pad(a["dst"], ROWS)
    by_partition = lambda m: m.reshape(QUADS, 4, P, -1).transpose(0, 2, 1, 3).reshape(QUADS * P, -1)
    d["src_row"], d["dst_row"] = src.reshape(QUADS, QUAD), dst.reshape(QUADS, QUAD)
    d["index0"] = np.concatenate([by_partition(dst), by_partition(src)], axis=1)
    d["index1"] = np.concatenate([by_partition(src), by_partition(dst)], axis=1)
    e = a["edge_attr_32"]
    ev = e[:, EB:].reshape(ROWS, EB, 3).transpose(0, 2, 1).reshape(ROWS, 3 * EB)
    d["attr32"] = by_partition(pad(np.concatenate([e[:, :EB], ev], axis=1)))
    d["attr4"] = by_partition(pad(a["edge_attr_4"]))
    d["features12"], d["features16"] = pad(a["edge_attr_12"]).T, pad(a["edge_attr_16"]).T
    d["z_node"] = pad(a["node_vec1"]).reshape(QUADS, P, 4).transpose(1, 0, 2).reshape(P, 4 * QUADS)

    w1, w2, w3, w4 = (a[f"L0_gnn_W{k}"] for k in (1, 2, 3, 4))
    w14 = np.zeros((P, EB, P), np.float32)
    w14[:NS, :, :NS] = w1
    w14[NS:NS + NV, :, NS:NS + NV] = w4
    w14[NS + NV:, :, NS + NV:] = w4
    d["l0_w14"], d["l0_w4"], d["l0_w3"] = w14.reshape(P, EB * P), w4.reshape(NV, EB * NV), w3.reshape(NS, EB * NV)
    d["l0_w2"] = w2.transpose(1, 0, 2).reshape(2, P, NS).transpose(1, 0, 2).reshape(P, 2 * NS)
    wm = np.concatenate([by_component(a["L0_gnn_Wm"], 0), a["L0_gnn_bm"][None]]).T
    d["wm_t_a"], d["wm_t_b"] = wm[:P], wm[P:]
    wu = by_component(a["L0_gnn_Wu"], 1)
    d["wu2_a"], d["wu2_b"] = wu[D:D + P], wu[D + P:]
    u = np.concatenate([by_component(wu[:D], 0), by_component(a["L0_gnn_bu"], 0)[None]])
    d["u_a"], d["u_b"] = u[:P], u[P:]

    names = {1: ("L1_gnn_W_fc1", "L1_gnn_W_fc2", "L1_gnn_W_sc0", "L1_gnn_W_sc1", "L1_gnn_W_l1_0", "L1_gnn_W_l1_1", "L1_gnn_W_l2_0", "L1_gnn_W_l2_1"),
             2: ("L2_gnn_fc_W1", "L2_gnn_fc_W2", "L2_gnn_W_sc0", "L2_gnn_W_sc1", "L2_gnn_W_l1_0", "L2_gnn_W_l1_1", "L2_gnn_W_l2_0", "L2_gnn_W_l2_1"),
             3: ("L3_gnn_Wfc1", "L3_gnn_Wfc2", "L3_gnn_Wsc0", "L3_gnn_Wsc1", "L3_gnn_Wl1_0", "L3_gnn_Wl1_1", "L3_gnn_Wl2_s", "L3_gnn_Wl2_v")}
    for l, keys in names.items():
        fc1, fc2, sc0, sc1, l10, l11, l20, l21 = (a[k] for k in keys)
        d[f"c{l}_fc1"], d[f"c{l}_fc2"] = fc1, fc2
        if l == 3:
            l20 = np.concatenate([a["L3_gnn_Wa"], l20], axis=1)
        ow = l20.shape[1] + 3 * NV
        out = np.zeros((P, 3, ow), np.float32)
        for k in range(3):
            at = l20.shape[1] + k * NV
            out[:NS + NV, k, at:at + NV] = l21
        out[P - NV:, 0, :l20.shape[1]] = l20[NS:]
        out[P - NV:, 1, :l20.shape[1]] = l20[:NV]
        out[P - NV:, 2, :l20.shape[1]] = l20[NV:NS]
        d[f"c{l}_out"] = out.reshape(P, 3 * ow)
        na = np.zeros((P, 2, P), np.float32)
        for k, (ws, wv) in enumerate(((sc0, sc1), (l10, l11))):
            na[:NS, k, :NS] = ws
            na[NS:NS + NV, k, NS:NS + NV] = wv
            na[NS + NV:, k, NS + NV:] = wv
        d[f"node{l}_a"] = na.reshape(P, 2 * P)
        d[f"node{l}_b"] = np.concatenate([sc1, l11], axis=1)
    return {k: np.ascontiguousarray(v) for k, v in d.items()}


def kernel(**inputs):
    import numpy as np
    import concourse.bacc as bacc
    from concourse.bass_utils import run_bass_kernel_spmd

    arrays = lay_out(inputs)
    nc = bacc.Bacc("TRN2", target_bir_lowering=False, num_devices=1)
    dram = {name: nc.dram_tensor(name, a.shape, mybir.dt.from_np(a.dtype), kind="ExternalInput").ap()
            for name, a in arrays.items()}
    result = nc.dram_tensor("result", (PADDED, D), F32, kind="ExternalOutput").ap()
    build(nc, dram, result)
    out = run_bass_kernel_spmd(nc, [arrays], core_ids=[0]).results[0]["result"][:ROWS]
    v = out[:, NS:].reshape(ROWS, 3, NV).transpose(0, 2, 1).reshape(ROWS, 3 * NV)
    return np.concatenate([out[:, :NS], v], axis=1)
```

```python
import math

import concourse.bass as bass
from concourse import mybir
from contextlib import ExitStack

F32 = mybir.dt.float32
I32 = mybir.dt.int32
ALU = mybir.AluOpType
ACT = mybir.ActivationFunctionType

ROWS = 50000
P = 128
QUAD = 4 * P
STEP = 2 * QUAD
TURNS = -(-ROWS // STEP)
PADDED = TURNS * STEP
QUADS = PADDED // QUAD
RING = 4
NODE_TURNS = -(-QUADS // RING)
PAIRS = 4 * TURNS
NS, NV = 64, 32
D = NS + 3 * NV
EB = 8
SPARE = PADDED
ACC_ROWS = PADDED + 2 * P
REPEAT = 1024.0


def need(eng, sem, value):
    if isinstance(value, int) and value <= 0:
        return
    eng.wait_ge(sem, value)


def turns(eng, body):
    body(0)
    with eng.Fori(1, TURNS - 1) as i:
        body(i)
    body(TURNS - 1)


class Chain:

    def __init__(self, eng, sem, per_unit):
        self.eng, self.sem, self.per_unit = eng, sem, per_unit
        self.unit, self.count = 0, per_unit

    def start(self, unit):
        assert self.count == self.per_unit, self.count
        self.unit, self.count = unit, 0

    def did(self, instruction):
        instruction.then_inc(self.sem, 1)
        self.count += 1
        return self.count

    def wait(self, count):
        need(self.eng, self.sem, self.unit * self.per_unit + count)


def prepare(nc, w, dram, acc, width):
    with ExitStack() as ctx:
        sem = lambda name: ctx.enter_context(nc.semaphore(name))
        loaded, ready, folded, masks, mm = (sem(n) for n in ("w_loaded", "w_ready", "w_folded", "w_masks", "w_product"))
        zeros_ready, zeroed = sem("zeros_ready"), sem("zeroed")
        prod = ctx.enter_context(nc.psum_tensor("prod", [P, 2, 512], F32))
        block = ctx.enter_context(nc.Block())
        loads = [(w[name], dram[name]) for name in w["loads"]]

        @block.sync
        def _(sp):
            for dst, src in loads:
                sp.dma_start(dst[:, :], src).then_inc(loaded, 16)

        @block.scalar
        def _(act):
            act.wait_ge(zeros_ready, 1)
            for n in range(TURNS):
                act.dma_start(acc[n * STEP:(n + 1) * STEP, :].rearrange("(p r) c -> p (r c)", p=P),
                              w["zeros"][:, 0:8 * width]).then_inc(zeroed, 16)
            act.dma_start(acc[PADDED:ACC_ROWS, :].rearrange("(p r) c -> p (r c)", p=P),
                          w["zeros"][:, 0:2 * width]).then_inc(zeroed, 16)
            act.wait_ge(zeroed, 16 * (TURNS + 1))

        @block.vector
        def _(dve):
            nc.vector.memset(w["zeros"][:, :], 0.0).then_inc(zeros_ready, 1)
            nc.vector.memset(w["ident"][:, :], 0.0)
            nc.vector.memset(w["tp"][:, :, :, :], 1.0)
            nc.vector.memset(w["eps"][:, :], 1e-5)
            nc.vector.memset(w["mask"][:, :, :], 1.0).then_inc(ready, 1)
            dve.wait_ge(loaded, 16 * len(loads))
            for name, rows, cols, factor in w["factors"]:
                part = w[name][rows[0]:rows[1], cols[0]:cols[1]]
                nc.vector.tensor_scalar(part, part, factor, None, ALU.mult).then_inc(folded, 1)
            dve.wait_ge(mm, 1)
            nc.vector.tensor_copy(w["l0_out_a"][:, :], prod[:, 0, 0:D])
            nc.vector.tensor_copy(w["l0_out_b"][:, :], prod[0:NV + 1, 1, 0:D]).then_inc(folded, 1)

        @block.tensor
        def _(pe):
            pe.wait_ge(loaded, 16 * len(loads))
            for k, rows in ((0, P), (1, NV + 1)):
                cols = slice(k * P, k * P + rows)
                nc.tensor.matmul(prod[0:rows, k, 0:D], w["wm_t_a"][:, cols], w["wu2_a"][:, :], start=True, stop=False)
                last = nc.tensor.matmul(prod[0:rows, k, 0:D], w["wm_t_b"][:, cols], w["wu2_b"][:, :], start=False, stop=True)
            last.then_inc(mm, 1)

        @block.gpsimd
        def _(pool):
            pool.wait_ge(ready, 1)
            pool.affine_select(out=w["ident"][:, :], in_=w["ident"][:, :], compare_op=ALU.not_equal, fill=1.0,
                               base=0, pattern=[[-1, P]], channel_multiplier=1)
            pool.affine_select(out=w["mask"][:, 0, :], in_=w["mask"][:, 0, :], compare_op=ALU.is_ge, fill=REPEAT + 1,
                               base=0, pattern=[[1, 2 * P]], channel_multiplier=-1)
            pool.affine_select(out=w["mask"][:, 1, :], in_=w["mask"][:, 1, :], compare_op=ALU.is_ge, fill=REPEAT + 1,
                               base=-P, pattern=[[1, 2 * P]], channel_multiplier=-1)
            pool.iota(w["spare"][:, :], pattern=[[P, 2]], base=SPARE, channel_multiplier=1).then_inc(masks, 1)
            pool.wait_ge(masks, 1)
            pool.wait_ge(folded, len(w["factors"]) + 1)


def edge_layer0(nc, w, dram, x, acc, next_acc, next_width):
    with ExitStack() as ctx:
        sem = lambda name: ctx.enter_context(nc.semaphore("a_" + name))
        sb = lambda name, shape, dt=F32: ctx.enter_context(nc.sbuf_tensor("a_" + name, shape, dt))
        pb = lambda name: ctx.enter_context(nc.psum_tensor("a_" + name, [P, 512], F32))
        target_row = sb("target_row", [P, 2, QUAD], I32)
        index = sb("index", [P, 2, 8], I32)
        attr = sb("attr", [P, 2, 4, 4 * EB])
        rows = sb("rows", [P, 4, 2, D])
        xt = sb("xt", [P, 2, 2, 2 * P])
        dp = sb("dp", [P, 2, 3, EB, NV])
        dots = sb("dots", [P, 4, EB * NV])
        dsum = sb("dsum", [P, 2, EB * NV])
        dott = sb("dott", [P, 2, 2, P])
        prod = sb("prod", [P, 2, EB, D])
        sum4 = sb("sum4", [P, 2, 4, D])
        sum2 = sb("sum2", [P, 2, 2, D])
        sum1 = sb("sum1", [P, 2, D])
        vprod = sb("vprod", [P, 2, 3, EB, NV])
        vecs = sb("vecs", [P, 4, D])
        tp = w["tp"]
        same_a = sb("same_a", [P, 2, P])
        same_b = sb("same_b", [P, 2, 2 * P])
        hits = sb("hits", [P, 2, 2 * P])
        seen = sb("seen", [P, 2, 2])
        away = sb("away", [P, 2, 2])
        move = sb("move", [P, 2, 2])
        slot = sb("slot", [P, 4, 2], I32)
        zt = sb("zt", [P, 2, 2, 2 * P])
        out = sb("out", [P, 2, 2, D])
        tb = [pb(f"t{k}") for k in range(4)]
        p_xt, p_dt, p_z, p_out = pb("p_xt"), pb("p_dt"), pb("p_z"), pb("p_out")

        loaded = [sem(f"loaded{c}") for c in range(2)]
        gathered = [sem(f"gathered{j}") for j in range(4)]
        zeroed = sem("zeroed")
        xt_ready, xt_copied = sem("xt_ready"), sem("xt_copied")
        dot_steps, dot_done = sem("dot_steps"), sem("dot_done")
        dt_ready, dt_copied = sem("dt_ready"), sem("dt_copied")
        bank_ready = [sem(f"bank_ready{k}") for k in range(4)]
        bank_read = [sem(f"bank_read{k}") for k in range(4)]
        s2_ready, s2_copied = sem("s2_ready"), sem("s2_copied")
        steps, prod_read = sem("steps"), sem("prod_read")
        pair_done = sem("pair_done")
        z_ready, z_copied = sem("z_ready"), sem("z_copied")
        out_ready, rows_ready = sem("out_ready"), sem("rows_ready")
        scattered = sem("scattered")
        block = ctx.enter_context(nc.Block())

        @block.sync
        def _(sp):
            def turn(i):
                for c in range(2):
                    q = 2 * i + c
                    need(sp, pair_done, 2 * q - 2)
                    sp.nop(nofuse=True)
                    sp.dma_start(target_row[:, c, :], dram["src_row"][bass.ds(q, 1), :].to_broadcast([P, QUAD])).then_inc(loaded[c], 16)
                    sp.dma_start(index[:, c, :], dram["index0"][bass.ds(q * P, P), :]).then_inc(loaded[c], 16)
                    sp.dma_start(attr[:, c, :, :].rearrange("p t k -> p (t k)"), dram["attr32"][bass.ds(q * P, P), :]).then_inc(loaded[c], 16)
                sp.dma_start(next_acc[bass.ds(i * STEP, STEP), :].rearrange("(p r) c -> p (r c)", p=P),
                             w["zeros"][:, 0:8 * next_width]).then_inc(zeroed, 16)
            turns(sp, turn)
            sp.dma_start(next_acc[PADDED:ACC_ROWS, :].rearrange("(p r) c -> p (r c)", p=P),
                         w["zeros"][:, 0:2 * next_width]).then_inc(zeroed, 16)
            sp.wait_ge(zeroed, 16 * (TURNS + 1))

        @block.gpsimd
        def _(pool):
            chain = Chain(pool, dot_steps, 2)

            def gather(i, j):
                if isinstance(i, int) and 4 * i + j >= PAIRS:
                    return
                j, i = j % 4, i + j // 4
                c, r = j // 2, j % 2
                need(pool, dt_ready, 2 * (4 * i + j) - 6)
                pool.wait_ge(loaded[c], 48 * (i + 1))
                for t in range(2):
                    pool.nop(nofuse=True)
                    pool.indirect_dma_start(rows[:, j, t, :], None, x,
                                            bass.IndirectOffsetOnAxis(ap=index[:, c, 2 * r + t:2 * r + t + 1], axis=0)
                                            ).then_inc(gathered[j], 16)

            def scatter(i, j):
                if isinstance(i, int) and 4 * i + j < 0:
                    return
                need(pool, scattered, 32 * (4 * i + j))
                pool.wait_ge(rows_ready, 4 * i + j + 1)
                for t in range(2):
                    pool.nop(nofuse=True)
                    pool.indirect_dma_start(acc, bass.IndirectOffsetOnAxis(ap=slot[:, j % 4, t:t + 1], axis=0),
                                            out[:, j % 2, t, :], None, compute_op=ALU.add).then_inc(scattered, 16)

            def dot_products(i, j):
                if isinstance(i, int) and 4 * i + j >= PAIRS:
                    return
                j, i = j % 4, i + j // 4
                c, r = j // 2, j % 2
                pool.wait_ge(gathered[j], 32 * (i + 1))
                for t in range(2):
                    m = 8 * i + 2 * j + t
                    chain.start(m)
                    need(pool, dot_done, m - 1)
                    ev = attr[:, c, 2 * r + t, EB:].rearrange("p (k b) -> p k b", k=3)
                    xv = rows[:, j, t, NS:].rearrange("p (k a) -> p k a", k=3)
                    n = chain.did(nc.gpsimd.tensor_tensor(dp[:, t, :, :, :], xv.unsqueeze(2).to_broadcast([P, 3, EB, NV]),
                                                          ev.unsqueeze(3).to_broadcast([P, 3, EB, NV]), ALU.mult))
                    chain.wait(n)
                    chain.did(nc.gpsimd.tensor_tensor(dsum[:, t, :], dp[:, t, 0, :, :].rearrange("p b a -> p (b a)"),
                                                      dp[:, t, 1, :, :].rearrange("p b a -> p (b a)"), ALU.add))

            def turn(i):
                for j in range(4):
                    dot_products(i, j + 1)
                    gather(i, j + 2)
                    scatter(i, j - 1)
            gather(0, 0)
            gather(0, 1)
            dot_products(0, 0)
            turns(pool, turn)
            scatter(TURNS - 1, 3)
            pool.wait_ge(scattered, 32 * PAIRS)

        @block.scalar
        def _(act):
            def copy_xt(i, j):
                if isinstance(i, int) and 4 * i + j >= PAIRS:
                    return
                j, i = j % 4, i + j // 4
                need(act, bank_ready[2], 2 * (4 * i + j) - 2)
                act.wait_ge(xt_ready, 4 * i + j + 1)
                nc.scalar.copy(xt[:, j % 2, 0, :], p_xt[:, 0:2 * P])
                nc.scalar.copy(xt[0:NV, j % 2, 1, :], p_xt[0:NV, 2 * P:]).then_inc(xt_copied, 1)

            def copy_dott(i, j, t):
                n = 8 * i + 2 * j + t
                need(act, s2_ready, n - 1)
                act.wait_ge(dt_ready, n + 1)
                nc.scalar.copy(dott[:, t, :, :].rearrange("p k e -> p (k e)"), p_dt[:, 0:2 * P]).then_inc(dt_copied, 1)

            def copy_s2(i, j, t):
                n = 8 * i + 2 * j + t
                need(act, pair_done, 4 * i + j - 1)
                act.wait_ge(s2_ready, n + 1)
                nc.scalar.copy(vecs[:, (2 * j + t) % 4, 0:NS], p_dt[:, 2 * P:2 * P + NS]).then_inc(s2_copied, 1)

            def scale(i, j, t, k):
                n = 8 * i + 2 * j + t
                if k == 0:
                    need(act, prod_read, n - 1)
                    act.wait_ge(loaded[j // 2], 48 * (i + 1))
                act.wait_ge(bank_ready[k], n + 1)
                for b in range(3 * k, min(3 * k + 3, EB)):
                    last = nc.scalar.activation(prod[:, t, b, :], tb[k][:, D * (b % 3):D * (b % 3) + D], ACT.Copy,
                                                scale=attr[:, j // 2, 2 * (j % 2) + t, b:b + 1])
                last.then_inc(bank_read[k], 1)

            def copy_z(i, j):
                n = 4 * i + j
                if isinstance(i, int) and n < 0:
                    return
                need(act, out_ready, n - 1)
                act.wait_ge(z_ready, n + 1)
                nc.scalar.copy(zt[:, j % 2, 0, :], p_z[:, 0:2 * P])
                nc.scalar.copy(zt[0:NV + 1, j % 2, 1, :], p_z[0:NV + 1, 2 * P:]).then_inc(z_copied, 1)

            def copy_out(i, j):
                n = 4 * i + j
                if isinstance(i, int) and n < 0:
                    return
                need(act, scattered, 32 * (n - 1))
                act.wait_ge(out_ready, n + 1)
                nc.scalar.copy(out[:, j % 2, :, :].rearrange("p t c -> p (t c)"), p_out[:, 0:2 * D]).then_inc(rows_ready, 1)

            def turn(i):
                for j in range(4):
                    for t in range(2):
                        copy_dott(i, j, t)
                        scale(i, j, t, 0)
                        copy_s2(i, j, t)
                        scale(i, j, t, 1)
                        scale(i, j, t, 2)
                        if t == 0:
                            copy_xt(i, j + 1)
                            copy_z(i, j - 1)
                        else:
                            copy_out(i, j - 1)
            copy_xt(0, 0)
            turns(act, turn)
            copy_z(TURNS - 1, 3)
            copy_out(TURNS - 1, 3)

        @block.vector
        def _(dve):
            chain = Chain(dve, steps, 10)

            def dot(i, j, t):
                if isinstance(i, int) and 4 * i + j >= PAIRS:
                    return
                m = 8 * i + 2 * j + t
                need(dve, dt_ready, m - 3)
                dve.wait_ge(dot_steps, 2 * (m + 1))
                nc.vector.tensor_tensor(dots[:, (2 * j + t) % 4, :], dsum[:, t, :],
                                        dp[:, t, 2, :, :].rearrange("p b a -> p (b a)"), ALU.add).then_inc(dot_done, 1)

            def pair(i, j):
                c, r, s = j // 2, j % 2, j % 2
                n = 4 * i + j
                chain.start(n)
                dve.wait_ge(loaded[c], 48 * (i + 1))
                need(dve, pair_done, n)
                need(dve, z_ready, n - 1)
                need(dve, scattered, 32 * (n - 3))
                mine = index[:, c, 4 + 2 * r:6 + 2 * r]
                pair_row = target_row[:, c, 2 * P * r:2 * P * (r + 1)]

                def find_hits(t):
                    return nc.vector.scalar_tensor_tensor(hits[:, t, :], pair_row, mine[:, t:t + 1], w["mask"][:, t, :],
                                                          ALU.is_equal, ALU.mult, accum_out=seen[:, s, t:t + 1])

                def vector_products(t):
                    dve.wait_ge(bank_ready[3], 2 * n + t + 1)
                    t3 = tb[3][:, 0:EB * NV].rearrange("p (b c) -> p b c", b=EB)
                    ev = attr[:, c, 2 * r + t, EB:].rearrange("p (k b) -> p k b", k=3)
                    nc.vector.tensor_tensor(vprod[:, t, :, :, :], t3.unsqueeze(1).to_broadcast([P, 3, EB, NV]),
                                            ev.unsqueeze(3).to_broadcast([P, 3, EB, NV]), ALU.mult).then_inc(bank_read[3], 1)

                def vector_sum(t):
                    dve.wait_ge(bank_read[3], 2 * n + t + 1)
                    return chain.did(nc.vector.tensor_reduce(
                        vecs[:, (2 * j + t) % 4, NS:].rearrange("p (k c) -> p k c", k=3),
                        vprod[:, t, :, :, :].rearrange("p k b c -> p k c b"), mybir.AxisListType.X, ALU.add))

                def add4(t):
                    dve.wait_ge(bank_read[2], 2 * n + t + 1)
                    nc.vector.tensor_tensor(sum4[:, t, :, :], prod[:, t, 0:4, :], prod[:, t, 4:8, :], ALU.add).then_inc(prod_read, 1)

                def add2(t):
                    dve.wait_ge(prod_read, 2 * n + t + 1)
                    return chain.did(nc.vector.tensor_tensor(sum2[:, t, :, :], sum4[:, t, 0:2, :], sum4[:, t, 2:4, :], ALU.add))

                def add1(t, sum2_written):
                    chain.wait(sum2_written)
                    return chain.did(nc.vector.tensor_tensor(sum1[:, t, :], sum2[:, t, 0, :], sum2[:, t, 1, :], ALU.add))

                def add_vectors(t, written):
                    chain.wait(written)
                    dve.wait_ge(s2_copied, 2 * n + t + 1)
                    return nc.vector.tensor_tensor(tp[:, s, t, 0:D], sum1[:, t, :], vecs[:, (2 * j + t) % 4, :], ALU.add)

                vector_products(0)
                find_hits(0)
                vector_sum(0)
                add4(0)
                hits_found = chain.did(find_hits(1))
                add2_0 = add2(0)
                dot(*ahead(i, j + 1), 0)
                add1_0 = add1(0, add2_0)
                vector_products(1)
                add_vectors(0, add1_0)
                vector_sum(1)
                away_written = chain.did(nc.vector.tensor_tensor(away[:, s, :], w["spare"][:, :], mine, ALU.subtract))
                add4(1)
                chain.wait(max(hits_found, away_written))
                moved = chain.did(nc.vector.scalar_tensor_tensor(move[:, s, :], seen[:, s, :], REPEAT, away[:, s, :],
                                                                 ALU.is_ge, ALU.mult))
                nc.vector.tensor_scalar(same_a[:, s, :], pair_row[:, 0:P], mine[:, 0:1], None, ALU.is_equal)
                add2_1 = add2(1)
                dot(*ahead(i, j + 1), 1)
                add1_1 = add1(1, add2_1)
                nc.vector.tensor_scalar(same_b[:, s, :], pair_row, mine[:, 1:2], None, ALU.is_equal)
                chain.wait(moved)
                chain.did(nc.vector.tensor_tensor(slot[:, j, :], move[:, s, :], mine, ALU.add))
                add_vectors(1, add1_1).then_inc(pair_done, 1)

            def ahead(i, j):
                return i + j // 4, j % 4

            def turn(i):
                for j in range(4):
                    pair(i, j)
            for t in range(2):
                dot(0, 0, t)
            turns(dve, turn)

        @block.tensor
        def _(pe):
            def transpose_x(i, j):
                if isinstance(i, int) and 4 * i + j >= PAIRS:
                    return
                j, i = j % 4, i + j // 4
                need(pe, xt_copied, 4 * i + j)
                pe.wait_ge(gathered[j], 32 * (i + 1))
                for t in range(2):
                    nc.tensor.transpose(p_xt[:, t * P:(t + 1) * P], rows[:, j, t, 0:P], w["ident"][:, :])
                    last = nc.tensor.transpose(p_xt[0:NV, (2 + t) * P:(3 + t) * P], rows[:, j, t, P:D], w["ident"][:, :])
                last.then_inc(xt_ready, 1)

            def transpose_dot(i, j, t):
                n = 8 * i + 2 * j + t
                need(pe, s2_copied, n)
                pe.wait_ge(dot_done, n + 1)
                for k in range(2):
                    last = nc.tensor.transpose(p_dt[:, k * P:(k + 1) * P], dots[:, (2 * j + t) % 4, k * P:(k + 1) * P], w["ident"][:, :])
                last.then_inc(dt_ready, 1)

            def products(i, j, t):
                n = 8 * i + 2 * j + t
                s = j % 2
                pe.wait_ge(xt_copied, 4 * i + j + 1)
                xa = xt[:, s, 0, t * P:(t + 1) * P]
                xb = xt[0:NV, s, 1, t * P:(t + 1) * P]
                for k, nb in ((3, 0), (0, 3), (1, 3), (2, 2)):
                    need(pe, bank_read[k], n)
                    if k == 1:
                        scalars(i, j, t)
                    if k == 3:
                        last = nc.tensor.matmul(tb[3][:, 0:EB * NV], xa[0:NS, :], w["l0_w3"][:, :], start=True, stop=True)
                    else:
                        view = tb[k][:, 0:nb * D].rearrange("p (b c) -> p b c", b=nb)
                        nc.tensor.matmul(view[:, :, 0:P], xa, w["l0_w14"][:, 3 * P * k:3 * P * k + nb * P], start=True, stop=True)
                        last = nc.tensor.matmul(view[:, :, P:D], xb, w["l0_w4"][:, 3 * NV * k:3 * NV * k + nb * NV], start=True, stop=True)
                    last.then_inc(bank_ready[k], 1)

            def scalars(i, j, t):
                n = 8 * i + 2 * j + t
                pe.wait_ge(dt_copied, n + 1)
                for k in range(2):
                    last = nc.tensor.matmul(p_dt[:, 2 * P:2 * P + NS], dott[:, t, k, :], w["l0_w2"][:, k * NS:(k + 1) * NS],
                                            start=(k == 0), stop=(k == 1))
                last.then_inc(s2_ready, 1)

            def sums(i, j):
                n = 4 * i + j
                if isinstance(i, int) and n < 0:
                    return
                s = j % 2
                need(pe, z_copied, n)
                pe.wait_ge(pair_done, n + 1)
                for k, (lo, hi) in enumerate(((0, P), (P, D + 1))):
                    z = p_z[0:hi - lo, 2 * P * k:2 * P * (k + 1)]
                    nc.tensor.matmul(z, tp[:, s, 1, lo:hi], same_b[:, s, :], start=True, stop=False)
                    last = nc.tensor.matmul(z[:, 0:P], tp[:, s, 0, lo:hi], same_a[:, s, :], start=False, stop=True)
                last.then_inc(z_ready, 1)

            def outputs(i, j):
                n = 4 * i + j
                if isinstance(i, int) and n < 0:
                    return
                need(pe, rows_ready, n)
                pe.wait_ge(z_copied, n + 1)
                for t in range(2):
                    o = p_out[:, t * D:(t + 1) * D]
                    nc.tensor.matmul(o, zt[:, j % 2, 0, t * P:(t + 1) * P], w["l0_out_a"][:, :], start=True, stop=False)
                    last = nc.tensor.matmul(o, zt[0:NV + 1, j % 2, 1, t * P:(t + 1) * P], w["l0_out_b"][:, :], start=False, stop=True)
                last.then_inc(out_ready, 1)

            def turn(i):
                for j in range(4):
                    transpose_dot(i, j, 0)
                    products(i, j, 0)
                    transpose_x(i, j + 1)
                    sums(i, j - 1)
                    transpose_dot(i, j, 1)
                    products(i, j, 1)
                    outputs(i, j - 1)
            transpose_x(0, 0)
            turns(pe, turn)
            sums(TURNS - 1, 3)
            outputs(TURNS - 1, 3)


def edge_conv(nc, w, dram, layer, table, acc, width, next_acc, next_width):
    conv = CONVS[layer]
    nf, hidden = conv["features"], conv["hidden"]
    find = layer == 1
    with ExitStack() as ctx:
        pre = f"c{layer}_"
        sem = lambda name: ctx.enter_context(nc.semaphore(pre + name))
        sb = lambda name, shape, dt=F32: ctx.enter_context(nc.sbuf_tensor("s_" + pre + name, shape, dt))
        pb = lambda name: ctx.enter_context(nc.psum_tensor(pre + name, [P, 512], F32))
        features = sb("features", [nf, 2, QUAD])
        target_row = sb("target_row", [P, 2, QUAD], I32)
        from_index = sb("from_index", [P, 2, 4], I32)
        to_index = sb("to_index", [P, 2, 4], I32)
        attr = sb("attr", [P, 2, 4, 4])
        rows = sb("rows", [P, 4, 2, D])
        hid = sb("hid", [hidden, 2, QUAD])
        pw = sb("pw", [P, 2, 2, 2, NS])
        vw = sb("vw", [P, 2, 2, 3, NV])
        dv = sb("dv", [P, 2, 2, 3, NV])
        ds = sb("ds", [P, 2, 2, 2, NV])
        mid = sb("mid", [P, 2, 2, 3, P])
        same_a = sb("same_a", [P, 2, P])
        same_b = sb("same_b", [P, 2, 2 * P])
        hits = sb("hits", [P, 2, 2 * P])
        away = sb("away", [P, 2, 2])
        move = sb("move", [P, 2, 2])
        slot = sb("slot", [P, 4, 2], I32)
        zt = sb("zt", [P, 2, 3, 2 * P])
        out = sb("out", [P, 2, 2, width])
        p_hid = pb("p_hid")
        p_w = [pb(f"p_w{r}") for r in range(2)]
        p_z = [ctx.enter_context(nc.psum_tensor(pre + f"p_z{r}", [P, 1024], F32)) for r in range(2)]
        p_out = pb("p_out")
        off = 1 if layer == 3 else 0
        ow = off + D

        loaded = [sem(f"loaded{c}") for c in range(2)]
        gathered = [sem(f"gathered{j}") for j in range(4)]
        index_loaded = sem("index_loaded")
        if next_acc is not None:
            zeroed = sem("zeroed")
        hid_ready, silu_done = sem("hid_ready"), sem("silu_done")
        w_ready = sem("w_ready")
        steps, pair_done = sem("steps"), sem("pair_done")
        z_ready, z_copied = sem("z_ready"), sem("z_copied")
        out_ready, rows_ready = sem("out_ready"), sem("rows_ready")
        scattered = sem("scattered")
        block = ctx.enter_context(nc.Block())

        @block.sync
        def _(sp):
            def load_from_index(i, c):
                if isinstance(i, int) and 2 * i + c >= QUADS:
                    return
                c, i = c % 2, i + c // 2
                q = 2 * i + c
                need(sp, index_loaded, 16 * q)
                sp.nop(nofuse=True)
                for j in (2 * c, 2 * c + 1):
                    need(sp, gathered[j], 32 * i)
                    sp.nop(nofuse=True)
                sp.dma_start(from_index[:, c, :], dram["from1"][bass.ds(q * P, P), :]).then_inc(index_loaded, 16)

            def turn(i):
                for c in range(2):
                    q = 2 * i + c
                    need(sp, pair_done, 2 * q - 2)
                    sp.nop(nofuse=True)
                    need(sp, hid_ready, q - 1)
                    sp.nop(nofuse=True)
                    sp.dma_start(target_row[:, c, :], dram["dst_row"][bass.ds(q, 1), :].to_broadcast([P, QUAD])).then_inc(loaded[c], 16)
                    sp.dma_start(to_index[:, c, :], dram["to1"][bass.ds(q * P, P), :]).then_inc(loaded[c], 16)
                    sp.dma_start(attr[:, c, :, :].rearrange("p t k -> p (t k)"), dram["attr4"][bass.ds(q * P, P), :]).then_inc(loaded[c], 16)
                    sp.dma_start(features[:, c, :], dram[f"features{nf}"][:, bass.ds(q * QUAD, QUAD)]).then_inc(loaded[c], 16)
                    load_from_index(i, c + 1)
                if next_acc is not None:
                    sp.dma_start(next_acc[bass.ds(i * STEP, STEP), :].rearrange("(p r) c -> p (r c)", p=P),
                                 w["zeros"][:, 0:8 * next_width]).then_inc(zeroed, 16)
            load_from_index(0, 0)
            turns(sp, turn)
            if next_acc is not None:
                sp.dma_start(next_acc[PADDED:ACC_ROWS, :].rearrange("(p r) c -> p (r c)", p=P),
                             w["zeros"][:, 0:2 * next_width]).then_inc(zeroed, 16)
                sp.wait_ge(zeroed, 16 * (TURNS + 1))

        @block.gpsimd
        def _(pool):
            def gather(i, j):
                if isinstance(i, int) and 4 * i + j >= PAIRS:
                    return
                j, i = j % 4, i + j // 4
                c, r = j // 2, j % 2
                need(pool, pair_done, 4 * i + j - 3)
                pool.wait_ge(index_loaded, 16 * (2 * i + c + 1))
                for t in range(2):
                    pool.nop(nofuse=True)
                    pool.indirect_dma_start(rows[:, j, t, :], None, table,
                                            bass.IndirectOffsetOnAxis(ap=from_index[:, c, 2 * r + t:2 * r + t + 1], axis=0)
                                            ).then_inc(gathered[j], 16)

            def scatter(i, j):
                if isinstance(i, int) and 4 * i + j < 0:
                    return
                need(pool, scattered, 32 * (4 * i + j))
                pool.wait_ge(rows_ready, 4 * i + j + 1)
                for t in range(2):
                    pool.nop(nofuse=True)
                    pool.indirect_dma_start(acc, bass.IndirectOffsetOnAxis(ap=slot[:, j % 4, t:t + 1], axis=0),
                                            out[:, j % 2, t, :], None, compute_op=ALU.add).then_inc(scattered, 16)

            def turn(i):
                for j in range(4):
                    gather(i, j + 2)
                    scatter(i, j - 1)
            gather(0, 0)
            gather(0, 1)
            turns(pool, turn)
            scatter(TURNS - 1, 3)
            pool.wait_ge(scattered, 32 * PAIRS)

        @block.scalar
        def _(act):
            def silu(i, c):
                if isinstance(i, int) and 2 * i + c >= QUADS:
                    return
                c, i = c % 2, i + c // 2
                q = 2 * i + c
                need(act, w_ready, 2 * q - 2)
                act.wait_ge(hid_ready, q + 1)
                nc.scalar.activation(hid[:, c, :], p_hid[0:hidden, :], ACT.Silu, scale=1.0 / math.sqrt(nf)).then_inc(silu_done, 1)

            def copy_z(i, j):
                n = 4 * i + j
                need(act, out_ready, n - 1)
                act.wait_ge(z_ready, n + 1)
                nc.scalar.copy(zt[:, j % 2, :, :].rearrange("p k e -> p (k e)"), p_z[j % 2][:, 0:6 * P]).then_inc(z_copied, 1)

            def copy_out(i, j):
                n = 4 * i + j
                if isinstance(i, int) and n < 0:
                    return
                need(act, scattered, 32 * (n - 1))
                act.wait_ge(out_ready, n + 1)
                src = p_out[:, 0:2 * ow].rearrange("p (t c) -> p t c", t=2)
                last = nc.scalar.copy(out[:, j % 2, :, 0:ow], src)
                if layer == 3:
                    last = nc.scalar.copy(out[:, j % 2, :, D + 1:D + 2], w["seen"][:, bass.ds(2 * n, 2)].unsqueeze(2))
                last.then_inc(rows_ready, 1)

            def turn(i):
                for j in range(4):
                    if j % 2 == 0:
                        silu(i, j // 2 + 1)
                    copy_z(i, j)
                    copy_out(i, j - 1)
            silu(0, 0)
            turns(act, turn)
            copy_out(TURNS - 1, 3)

        @block.vector
        def _(dve):
            chain = Chain(dve, steps, 9 if find else 5)

            def pair(i, j):
                c, r, s = j // 2, j % 2, j % 2
                n = 4 * i + j
                chain.start(n)
                dve.wait_ge(loaded[c], 64 * (i + 1))
                need(dve, pair_done, n)
                need(dve, z_ready, n - 1)
                need(dve, scattered, 32 * (n - 3))
                mine = to_index[:, c, 2 * r:2 * r + 2]
                pair_row = target_row[:, c, 2 * P * r:2 * P * (r + 1)]
                nc.vector.tensor_scalar(same_a[:, s, :], pair_row[:, 0:P], mine[:, 0:1], None, ALU.is_equal)
                nc.vector.tensor_scalar(same_b[:, s, :], pair_row, mine[:, 1:2], None, ALU.is_equal)
                if find:
                    for t in range(2):
                        last = nc.vector.scalar_tensor_tensor(hits[:, t, :], pair_row, mine[:, t:t + 1], w["mask"][:, t, :],
                                                              ALU.is_equal, ALU.mult, accum_out=w["seen"][:, bass.ds(2 * n + t, 1)])
                    chain.did(last)
                    k = chain.did(nc.vector.tensor_tensor(away[:, s, :], w["spare"][:, :], mine, ALU.subtract))
                    chain.wait(k)
                    k = chain.did(nc.vector.scalar_tensor_tensor(move[:, s, :], w["seen"][:, bass.ds(2 * n, 2)], REPEAT, away[:, s, :],
                                                                 ALU.is_ge, ALU.mult))
                    chain.wait(k)
                    k = chain.did(nc.vector.tensor_tensor(slot[:, j, :], move[:, s, :], mine, ALU.add))
                    chain.wait(k)
                    nc.vector.tensor_copy(w["slots"][:, bass.ds(2 * n, 2)], slot[:, j, :])
                else:
                    nc.vector.tensor_copy(slot[:, j, :], w["slots"][:, bass.ds(2 * n, 2)])
                dve.wait_ge(gathered[j], 32 * (i + 1))
                y = attr[:, c, 2 * r:2 * r + 2, :]
                e0 = rows[:, j, :, 0:NS]
                e1 = rows[:, j, :, NS:D].rearrange("p t (k u) -> p t k u", k=3)
                y1 = y[:, :, 1:4].unsqueeze(3)
                k_dv = chain.did(nc.vector.tensor_tensor(dv[:, s], e1, y1.to_broadcast([P, 2, 3, NV]), ALU.mult))
                dve.wait_ge(w_ready, n + 1)
                pwv = p_w[r][:, 0:384].rearrange("p (t m) -> p t m", t=2)
                k_pw = chain.did(nc.vector.tensor_tensor(
                    pw[:, s], pwv[:, :, 0:2 * NS].rearrange("p t (k u) -> p t k u", k=2),
                    e0.unsqueeze(2).to_broadcast([P, 2, 2, NS]), ALU.mult))
                k_vw = chain.did(nc.vector.tensor_tensor(
                    vw[:, s], pwv[:, :, 2 * NS:2 * NS + NV].unsqueeze(2).to_broadcast([P, 2, 3, NV]), e1, ALU.mult))
                chain.wait(k_dv)
                k_ds = chain.did(nc.vector.tensor_tensor(ds[:, s, :, 0, :], dv[:, s, :, 0, :], dv[:, s, :, 1, :], ALU.add))
                chain.wait(k_pw)
                nc.vector.tensor_tensor(mid[:, s, :, :, 0:NS], pw[:, s, :, 1, :].unsqueeze(2).to_broadcast([P, 2, 3, NS]),
                                        y1.to_broadcast([P, 2, 3, NS]), ALU.mult)
                chain.wait(k_ds)
                k_ds = chain.did(nc.vector.tensor_tensor(ds[:, s, :, 1, :], ds[:, s, :, 0, :], dv[:, s, :, 2, :], ALU.add))
                nc.vector.tensor_tensor(mid[:, s, :, :, NS:NS + NV], vw[:, s], y[:, :, 0:1].unsqueeze(3).to_broadcast([P, 2, 3, NV]), ALU.mult)
                nc.vector.tensor_tensor(mid[:, s, :, 1:3, NS + NV:], pw[:, s, :, 0, :].rearrange("p t (k u) -> p t k u", k=2),
                                        y[:, :, 0:1].unsqueeze(3).to_broadcast([P, 2, 2, NV]), ALU.mult)
                chain.wait(k_ds)
                nc.vector.tensor_tensor(mid[:, s, :, 0, NS + NV:], pwv[:, :, 2 * NS + NV:], ds[:, s, :, 1, :], ALU.mult).then_inc(pair_done, 1)

            def turn(i):
                for j in range(4):
                    pair(i, j)
            turns(dve, turn)

        @block.tensor
        def _(pe):
            def hidden_layer(i, c):
                if isinstance(i, int) and 2 * i + c >= QUADS:
                    return
                c, i = c % 2, i + c // 2
                q = 2 * i + c
                need(pe, silu_done, q)
                pe.wait_ge(loaded[c], 64 * (i + 1))
                nc.tensor.matmul(p_hid[0:hidden, :], w[pre + "fc1"][:, :], features[:, c, :], start=True, stop=True).then_inc(hid_ready, 1)

            def edge_weights(i, j):
                if isinstance(i, int) and 4 * i + j >= PAIRS:
                    return
                j, i = j % 4, i + j // 4
                c, r = j // 2, j % 2
                need(pe, pair_done, 4 * i + j - 1)
                pe.wait_ge(silu_done, 2 * i + c + 1)
                for t in range(2):
                    last = nc.tensor.matmul(p_w[r][:, t * 192:(t + 1) * 192], hid[:, c, (2 * r + t) * P:(2 * r + t + 1) * P],
                                            w[pre + "fc2"][:, :], start=True, stop=True)
                last.then_inc(w_ready, 1)

            def sums(i, j):
                n, s = 4 * i + j, j % 2
                need(pe, z_copied, n - 1)
                pe.wait_ge(pair_done, n + 1)
                for k in range(3):
                    z = p_z[s][:, 2 * P * k:2 * P * (k + 1)]
                    nc.tensor.matmul(z, mid[:, s, 1, k, :], same_b[:, s, :], start=True, stop=False)
                    last = nc.tensor.matmul(z[:, 0:P], mid[:, s, 0, k, :], same_a[:, s, :], start=False, stop=True)
                last.then_inc(z_ready, 1)

            def outputs(i, j):
                n = 4 * i + j
                if isinstance(i, int) and n < 0:
                    return
                need(pe, rows_ready, n)
                pe.wait_ge(z_copied, n + 1)
                for t in range(2):
                    for a, k in enumerate((2, 0, 1)):
                        cols = off + NS + NV * (k + 1)
                        last = nc.tensor.matmul(p_out[:, t * ow:t * ow + cols], zt[:, j % 2, k, t * P:(t + 1) * P],
                                                w[pre + "out"][:, k * ow:k * ow + cols], start=(a == 0), stop=(a == 2))
                last.then_inc(out_ready, 1)

            def turn(i):
                for j in range(4):
                    if j % 2 == 0:
                        hidden_layer(i, j // 2 + 1)
                    edge_weights(i, j + 1)
                    sums(i, j)
                    outputs(i, j - 1)
            hidden_layer(0, 0)
            edge_weights(0, 0)
            turns(pe, turn)
            outputs(TURNS - 1, 3)


def node_pass(nc, w, dram, after, source, acc, width, table, base, result):
    first, final = after == 0, after == 3
    off = 1 if final else 0
    with ExitStack() as ctx:
        pre = f"n{after}_"
        sem = lambda name: ctx.enter_context(nc.semaphore(pre + name))
        sb = lambda name, shape, dt=F32: ctx.enter_context(nc.sbuf_tensor("s_" + pre + name, shape, dt))
        pb = lambda name: ctx.enter_context(nc.psum_tensor(pre + name, [P, 512], F32))
        src = sb("src", [P, RING, 4, D])
        agg = sb("agg", [P, RING, 4, width])
        coef = sb("coef", [P, RING, 5, 4])
        xr = sb("xr", [P, RING, 4, D])
        part = sb("part", [P, RING, 4, D])
        total = sb("total", [P, RING, 4])
        nmean = sb("nmean", [P, RING, 4])
        square = sb("square", [P, RING, 4, D])
        ssq = sb("ssq", [P, RING, 4])
        std = sb("std", [P, RING, 4])
        rstd = sb("rstd", [P, RING, 4])
        xn = sb("xn", [P, RING, 4, D])
        xta = sb("xta", [P, 2, 4 * P])
        xtb = sb("xtb", [NV + 1, 2, 4 * P])
        fta = sb("fta", [P, 2, 4 * P])
        ftb = sb("ftb", [NV + 1, 2, 4 * P])
        bout = sb("bout", [P, 2, 4, D])
        tout = sb("tout", [P, 2, 4, D])
        p_ta, p_tb = pb("p_ta"), pb("p_tb")
        p_o = [pb(f"p_o{t}") for t in range(4)]
        p_u = [pb(f"p_u{t}") for t in range(2)]

        stores = RING if final else 2
        loaded = [sem(f"loaded{c}") for c in range(RING)]
        if first:
            ones = sem("ones")
            f_ready, f_copied, u_ready = sem("f_ready"), sem("f_copied"), sem("u_ready")
        steps, sum_done = sem("steps"), sem("sum_done")
        std_steps = sem("std_steps")
        norm_steps = sem("norm_steps")
        if not final:
            t_ready, t_copied, o_ready = sem("t_ready"), sem("t_copied"), sem("o_ready")
            base_done, table_done = sem("base_done"), sem("table_done")
        stored = [sem(f"stored{c}") for c in range(stores)]
        block = ctx.enter_context(nc.Block())
        view = lambda a, q: a[bass.ds(q * QUAD, QUAD), :].rearrange("(p r) c -> p (r c)", p=P)
        flat = lambda a, c: a[:, c].rearrange("p t k -> p (t k)")
        z_of = lambda q, t: w["z_node"][:, bass.ds(4 * q + t, 1)]
        per_store = 16 if final else 32

        def quad(i, c):
            i, c = i + c // RING, c % RING
            q = RING * i + c
            if isinstance(q, int) and not 0 <= q < QUADS:
                return None
            return i, c, q

        def steps_of(eng, step):
            def turn(i):
                for c in range(RING):
                    step(i, c)
            turn(-1)
            turn(0)
            with eng.Fori(1, NODE_TURNS - 2) as i:
                turn(i)
            turn(NODE_TURNS - 2)
            turn(NODE_TURNS - 1)

        def wait_stored(eng, i, c):
            if final:
                need(eng, stored[c], per_store * i)
            else:
                need(eng, stored[c % 2], per_store * (2 * i + c // 2))

        @block.sync
        def _(sp):
            def step(i, c):
                at = quad(i, c + 4)
                if at is None:
                    return
                i, c, q = at
                need(sp, sum_done, q - 3)
                sp.nop(nofuse=True)
                sp.dma_start(flat(src, c), view(source, q)).then_inc(loaded[c], 16)
                sp.dma_start(flat(agg, c), view(acc, q)).then_inc(loaded[c], 16)
            steps_of(sp, step)
            for c in range(stores):
                sp.wait_ge(stored[c], per_store * len(range(c, QUADS, stores)))

        @block.gpsimd
        def _(pool):
            def step(i, c):
                at = quad(i, c)
                if at is None:
                    return
                i, c, q = at
                if final:
                    pool.wait_ge(norm_steps, 2 * q + 2)
                    pool.nop(nofuse=True)
                    pool.dma_start(view(result, q), flat(xn, c)).then_inc(stored[c], 16)
                else:
                    pool.wait_ge(base_done, 4 * q + 4)
                    pool.nop(nofuse=True)
                    pool.dma_start(view(base, q), flat(bout, c % 2)).then_inc(stored[c % 2], 16)
                    pool.wait_ge(table_done, 4 * q + 4)
                    pool.nop(nofuse=True)
                    pool.dma_start(view(table, q), flat(tout, c % 2)).then_inc(stored[c % 2], 16)
            steps_of(pool, step)

        @block.scalar
        def _(act):
            def copy_front(at):
                if at is None:
                    return
                i, c, q = at
                need(act, u_ready, q - 1)
                act.wait_ge(f_ready, q + 1)
                nc.scalar.copy(fta[:, c % 2, :], p_ta[:, :])
                nc.scalar.copy(ftb[0:NV, c % 2, :], p_tb[0:NV, :]).then_inc(f_copied, 1)

            def squares(at):
                if at is None:
                    return
                i, c, q = at
                need(act, std_steps, 2 * (q - 3))
                need(act, norm_steps, 2 * (q - 3))
                act.wait_ge(sum_done, q + 1)
                for t in range(4):
                    last = nc.scalar.activation(square[:, c, t, :], xr[:, c, t, :], ACT.Square, bias=nmean[:, c, t:t + 1],
                                                accum_out=ssq[:, c, t:t + 1])
                last.then_inc(std_steps, 1)
                act.wait_ge(std_steps, 2 * q + 1)
                nc.scalar.activation(std[:, c, :], ssq[:, c, :], ACT.Sqrt, scale=1.0 / D, bias=w["eps"][:, :]).then_inc(std_steps, 1)

            def copy_t(at):
                if at is None:
                    return
                i, c, q = at
                need(act, o_ready, 4 * q - 4)
                act.wait_ge(t_ready, q + 1)
                nc.scalar.copy(xta[:, c % 2, :], p_ta[:, :])
                nc.scalar.copy(xtb[0:NV, c % 2, :], p_tb[0:NV, :]).then_inc(t_copied, 1)

            def messages(at):
                if at is None:
                    return
                i, c, q = at
                wait_stored(act, i, c)
                for t in range(4):
                    act.wait_ge(base_done, 4 * q + t + 1)
                    nc.scalar.activation(tout[:, c % 2, t, :], p_o[t][:, D:2 * D], ACT.Copy, scale=z_of(q, t)).then_inc(table_done, 1)

            def step(i, c):
                if first:
                    copy_front(quad(i, c + 4))
                squares(quad(i, c + 2))
                if not final:
                    copy_t(quad(i, c))
                    messages(quad(i, c - 1))
            steps_of(act, step)

        @block.vector
        def _(dve):
            chain = Chain(dve, steps, 6 if final else 2 if first else 1)

            def sums(at):
                if at is None:
                    return
                i, c, q = at
                if not final:
                    chain.start(q)
                dve.wait_ge(loaded[c], 32 * (i + 1))
                need(dve, norm_steps, 2 * (q - 3))
                if first:
                    dve.wait_ge(u_ready, q + 1)
                    for t in range(4):
                        ins = nc.vector.scalar_tensor_tensor(part[:, c, t, :], src[:, c, t, :], 2.0,
                                                             p_u[t // 2][:, (t % 2) * D:(t % 2 + 1) * D], ALU.mult, ALU.add)
                    chain.wait(chain.did(ins))
                    ins = [nc.vector.scalar_tensor_tensor(xr[:, c, t, :], part[:, c, t, :], 1.0, agg[:, c, t, :], ALU.mult,
                                                          ALU.add, accum_out=total[:, c, t:t + 1]) for t in range(4)][-1]
                elif final:
                    chain.wait(5)
                    ins = [nc.vector.scalar_tensor_tensor(xr[:, c, t, :], agg[:, c, t, 1:1 + D], coef[:, c, 4, t:t + 1],
                                                          src[:, c, t, :], ALU.mult, ALU.add,
                                                          accum_out=total[:, c, t:t + 1]) for t in range(4)][-1]
                else:
                    ins = [nc.vector.scalar_tensor_tensor(xr[:, c, t, :], agg[:, c, t, :], z_of(q, t), src[:, c, t, :],
                                                          ALU.mult, ALU.add,
                                                          accum_out=total[:, c, t:t + 1]) for t in range(4)][-1]
                chain.wait(chain.did(ins))
                nc.vector.tensor_scalar(nmean[:, c, :], total[:, c, :], -1.0 / D, None, ALU.mult).then_inc(sum_done, 1)

            def factor_step(at, k):
                if not final or at is None:
                    return
                i, c, q = at
                cf = lambda k: coef[:, c, k, :].unsqueeze(2)
                if k == 0:
                    chain.start(q)
                    dve.wait_ge(loaded[c], 32 * (i + 1))
                    need(dve, norm_steps, 2 * (q - 3))
                    chain.did(nc.vector.tensor_scalar(cf(0), agg[:, c, :, D + 1:D + 2], 1.0, None, ALU.max))
                    return
                chain.wait(k)
                if k == 1:
                    chain.did(nc.vector.reciprocal(cf(1), cf(0)))
                elif k == 2:
                    chain.did(nc.vector.tensor_tensor(coef[:, c, 2, :], coef[:, c, 1, :], w["z_node"][:, bass.ds(4 * q, 4)], ALU.mult))
                elif k == 3:
                    chain.did(nc.vector.tensor_tensor(cf(3), cf(2), cf(2), ALU.mult))
                else:
                    chain.did(nc.vector.tensor_tensor(cf(4), cf(3), agg[:, c, :, 0:1], ALU.mult))

            def norm(at, ahead):
                if at is None:
                    for k in range(5):
                        factor_step(ahead, k)
                    return
                i, c, q = at
                dve.wait_ge(std_steps, 2 * q + 2)
                nc.vector.reciprocal(rstd[:, c, :], std[:, c, :]).then_inc(norm_steps, 1)
                if final:
                    wait_stored(dve, i, c)
                else:
                    need(dve, t_ready, q - 3)
                    need(dve, base_done, 4 * q - 12)
                factor_step(ahead, 0)
                dve.wait_ge(norm_steps, 2 * q + 1)
                for t in range(4):
                    ins = nc.vector.tensor_scalar(xn[:, c, t, :], xr[:, c, t, :], nmean[:, c, t:t + 1], rstd[:, c, t:t + 1],
                                                  ALU.add, ALU.mult)
                    if t == 3:
                        ins.then_inc(norm_steps, 1)
                    factor_step(ahead, t + 1)

            def self_term(at):
                if at is None:
                    return
                i, c, q = at
                wait_stored(dve, i, c)
                for t in range(4):
                    dve.wait_ge(o_ready, 4 * q + t + 1)
                    nc.vector.scalar_tensor_tensor(bout[:, c % 2, t, :], p_o[t][:, 0:D], z_of(q, t), xn[:, c, t, :],
                                                   ALU.mult, ALU.add).then_inc(base_done, 1)

            def step(i, c):
                norm(quad(i, c + 1), quad(i, c + 3))
                sums(quad(i, c + 3))
                if not final:
                    self_term(quad(i, c - 1))
            if first:
                nc.vector.memset(ftb[:, :, :], 1.0).then_inc(ones, 1)
            steps_of(dve, step)

        if final:
            return

        @block.tensor
        def _(pe):
            def transpose(src_slot):
                for t in range(4):
                    nc.tensor.transpose(p_ta[:, t * P:(t + 1) * P], src_slot[:, t, 0:P], w["ident"][:, :])
                    last = nc.tensor.transpose(p_tb[0:NV, t * P:(t + 1) * P], src_slot[:, t, P:D], w["ident"][:, :])
                return last

            def front_transposes(at):
                if at is None:
                    return
                i, c, q = at
                need(pe, t_copied, q - 4)
                pe.wait_ge(loaded[c], 32 * (i + 1))
                transpose(src[:, c]).then_inc(f_ready, 1)

            def front_products(at):
                if at is None:
                    return
                i, c, q = at
                need(pe, sum_done, q)
                pe.wait_ge(f_copied, q + 1)
                for t in range(4):
                    o = p_u[t // 2][:, (t % 2) * D:(t % 2 + 1) * D]
                    nc.tensor.matmul(o, fta[:, c % 2, t * P:(t + 1) * P], w["u_a"][:, :], start=True, stop=False)
                    last = nc.tensor.matmul(o, ftb[:, c % 2, t * P:(t + 1) * P], w["u_b"][:, :], start=False, stop=True)
                last.then_inc(u_ready, 1)

            def transposes(at):
                if at is None:
                    return
                i, c, q = at
                need(pe, t_copied, q)
                if first:
                    pe.wait_ge(f_copied, min(q + 5, QUADS) if isinstance(q, int) else q + 5)
                pe.wait_ge(norm_steps, 2 * q + 2)
                transpose(xn[:, c]).then_inc(t_ready, 1)

            def products(at):
                if at is None:
                    return
                i, c, q = at
                pe.wait_ge(t_copied, q + 1)
                for t in range(4):
                    need(pe, table_done, 4 * (q - 1) + t + 1)
                    o = p_o[t][:, 0:2 * D].rearrange("p (k c) -> p k c", k=2)
                    nc.tensor.matmul(o[:, :, 0:P], xta[:, c % 2, t * P:(t + 1) * P], w[f"node{after + 1}_a"][:, :], start=True, stop=True)
                    nc.tensor.matmul(o[:, :, P:D], xtb[0:NV, c % 2, t * P:(t + 1) * P], w[f"node{after + 1}_b"][:, :],
                                     start=True, stop=True).then_inc(o_ready, 1)

            def step(i, c):
                if first:
                    front_transposes(quad(i, c + 4))
                    products(quad(i, c - 1))
                    transposes(quad(i, c))
                    front_products(quad(i, c + 4))
                else:
                    transposes(quad(i, c))
                    products(quad(i, c - 1))
            if first:
                pe.wait_ge(ones, 1)
            steps_of(pe, step)


CONVS = {
    1: dict(features=12, hidden=100, self_factor=math.sin(math.pi / 8), factor=math.cos(math.pi / 8) / math.sqrt(8.0 * 96 * 100)),
    2: dict(features=16, hidden=64, self_factor=math.sin(math.pi / 8), factor=math.cos(math.pi / 8) / math.sqrt(10.0 * 96 * 64)),
    3: dict(features=16, hidden=64, self_factor=1.0, factor=1.0 / math.sqrt(96.0 * 64)),
}

FACTORS = [
    ("l0_w14", (0, NS), (0, EB * P), 1 / math.sqrt(2.0 * NS * EB)),
    ("l0_w14", (NS, P), (0, EB * P), 1 / math.sqrt(2.0 * NV * EB)),
    ("l0_w4", (0, NV), (0, EB * NV), 1 / math.sqrt(2.0 * NV * EB)),
    ("l0_w3", (0, NS), (0, EB * NV), 1 / math.sqrt(2.0 * NS * EB)),
    ("l0_w2", (0, P), (0, 2 * NS), 1 / math.sqrt(3.0 * 2.0 * NV * EB)),
]
for _l, _c in CONVS.items():
    _ow = D + (_l == 3)
    FACTORS += [
        (f"c{_l}_out", (0, P - NV), (0, 3 * _ow), _c["factor"]),
        (f"c{_l}_out", (P - NV, P), (0, _ow), _c["factor"] / math.sqrt(3.0)),
        (f"c{_l}_out", (P - NV, P), (_ow, 3 * _ow), _c["factor"]),
        (f"node{_l}_a", (0, P), (0, NS), _c["self_factor"] / math.sqrt(NS)),
        (f"node{_l}_a", (0, P), (NS, P), _c["self_factor"] / math.sqrt(NV)),
        (f"node{_l}_a", (0, P), (P, P + NS), 1 / math.sqrt(NS)),
        (f"node{_l}_a", (0, P), (P + NS, 2 * P), 1 / math.sqrt(NV)),
        (f"node{_l}_b", (0, NV), (0, NV), _c["self_factor"] / math.sqrt(NV)),
        (f"node{_l}_b", (0, NV), (NV, 2 * NV), 1 / math.sqrt(NV)),
    ]


def build(nc, dram, result):
    scratch = lambda name, rows, cols: nc.dram_tensor(name, [rows, cols], F32).ap()
    table = scratch("table", PADDED, D)
    bases = [scratch(f"base{k}", PADDED, D) for k in range(2)]
    accs = [scratch(f"acc{k}", ACC_ROWS, D) for k in range(2)]
    acc3 = scratch("acc3", ACC_ROWS, D + 2)
    with ExitStack() as ctx:
        w = {}
        for name in WEIGHTS:
            w[name] = ctx.enter_context(nc.sbuf_tensor("w_" + name, list(dram[name].shape), F32))
        w["loads"], w["factors"] = WEIGHTS, FACTORS
        for name, shape, dt in (("ident", [P, P], F32), ("zeros", [P, 8 * (D + 2)], F32), ("tp", [P, 2, 2, D + 1], F32),
                                ("mask", [P, 2, 2 * P], F32), ("spare", [P, 2], I32), ("eps", [P, 1], F32),
                                ("l0_out_a", [P, D], F32), ("l0_out_b", [NV + 1, D], F32),
                                ("seen", [P, 2 * PAIRS], F32), ("slots", [P, 2 * PAIRS], I32)):
            w[name] = ctx.enter_context(nc.sbuf_tensor("w_" + name, shape, dt))
        prepare(nc, w, dram, accs[0], D)
        edge_layer0(nc, w, dram, dram["x"], accs[0], accs[1], D)
        node_pass(nc, w, dram, 0, dram["x"], accs[0], D, table, bases[0], None)
        edge_conv(nc, w, dram, 1, table, accs[1], D, accs[0], D)
        node_pass(nc, w, dram, 1, bases[0], accs[1], D, table, bases[1], None)
        edge_conv(nc, w, dram, 2, table, accs[0], D, acc3, D + 2)
        node_pass(nc, w, dram, 2, bases[1], accs[0], D, table, bases[0], None)
        edge_conv(nc, w, dram, 3, table, acc3, D + 2, None, 0)
        node_pass(nc, w, dram, 3, bases[0], acc3, D + 2, None, None, result)


WEIGHTS = (["z_node", "l0_w14", "l0_w4", "l0_w3", "l0_w2", "wm_t_a", "wm_t_b", "wu2_a", "wu2_b", "u_a", "u_b"]
           + [f"c{l}_{m}" for l in (1, 2, 3) for m in ("fc1", "fc2", "out")]
           + [f"node{l}_{m}" for l in (1, 2, 3) for m in ("a", "b")])


def lay_out(inputs):
    import numpy as np
    a = {k: np.asarray(v) for k, v in inputs.items()}
    extra = PADDED - ROWS

    def by_component(m, axis):
        m = np.moveaxis(m, axis, 0)
        v = m[NS:].reshape((NV, 3) + m.shape[1:])
        v = np.swapaxes(v, 0, 1).reshape((3 * NV,) + m.shape[1:])
        return np.moveaxis(np.concatenate([m[:NS], v]), 0, axis)

    def pad(m, value=0):
        return np.concatenate([m, np.full((extra,) + m.shape[1:], value, m.dtype)])

    d = {}
    d["x"] = pad(by_component(a["x"], 1))
    src, dst = pad(a["src"], ROWS), pad(a["dst"], ROWS)
    by_partition = lambda m: m.reshape(QUADS, 4, P, -1).transpose(0, 2, 1, 3).reshape(QUADS * P, -1)
    d["src_row"], d["dst_row"] = src.reshape(QUADS, QUAD), dst.reshape(QUADS, QUAD)
    d["index0"] = np.concatenate([by_partition(dst), by_partition(src)], axis=1)
    d["from1"], d["to1"] = by_partition(src), by_partition(dst)
    e = a["edge_attr_32"]
    ev = e[:, EB:].reshape(ROWS, EB, 3).transpose(0, 2, 1).reshape(ROWS, 3 * EB)
    d["attr32"] = by_partition(pad(np.concatenate([e[:, :EB], ev], axis=1)))
    d["attr4"] = by_partition(pad(a["edge_attr_4"]))
    d["features12"], d["features16"] = pad(a["edge_attr_12"]).T, pad(a["edge_attr_16"]).T
    d["z_node"] = pad(a["node_vec1"]).reshape(QUADS, P, 4).transpose(1, 0, 2).reshape(P, 4 * QUADS)

    w1, w2, w3, w4 = (a[f"L0_gnn_W{k}"] for k in (1, 2, 3, 4))
    w14 = np.zeros((P, EB, P), np.float32)
    w14[:NS, :, :NS] = w1
    w14[NS:NS + NV, :, NS:NS + NV] = w4
    w14[NS + NV:, :, NS + NV:] = w4
    d["l0_w14"], d["l0_w4"], d["l0_w3"] = w14.reshape(P, EB * P), w4.reshape(NV, EB * NV), w3.reshape(NS, EB * NV)
    d["l0_w2"] = w2.transpose(1, 0, 2).reshape(2, P, NS).transpose(1, 0, 2).reshape(P, 2 * NS)
    wm = np.concatenate([by_component(a["L0_gnn_Wm"], 0), a["L0_gnn_bm"][None]]).T
    d["wm_t_a"], d["wm_t_b"] = wm[:P], wm[P:]
    wu = by_component(a["L0_gnn_Wu"], 1)
    d["wu2_a"], d["wu2_b"] = wu[D:D + P], wu[D + P:]
    u = np.concatenate([by_component(wu[:D], 0), by_component(a["L0_gnn_bu"], 0)[None]])
    d["u_a"], d["u_b"] = u[:P], u[P:]

    names = {1: ("L1_gnn_W_fc1", "L1_gnn_W_fc2", "L1_gnn_W_sc0", "L1_gnn_W_sc1", "L1_gnn_W_l1_0", "L1_gnn_W_l1_1", "L1_gnn_W_l2_0", "L1_gnn_W_l2_1"),
             2: ("L2_gnn_fc_W1", "L2_gnn_fc_W2", "L2_gnn_W_sc0", "L2_gnn_W_sc1", "L2_gnn_W_l1_0", "L2_gnn_W_l1_1", "L2_gnn_W_l2_0", "L2_gnn_W_l2_1"),
             3: ("L3_gnn_Wfc1", "L3_gnn_Wfc2", "L3_gnn_Wsc0", "L3_gnn_Wsc1", "L3_gnn_Wl1_0", "L3_gnn_Wl1_1", "L3_gnn_Wl2_s", "L3_gnn_Wl2_v")}
    for l, keys in names.items():
        fc1, fc2, sc0, sc1, l10, l11, l20, l21 = (a[k] for k in keys)
        d[f"c{l}_fc1"], d[f"c{l}_fc2"] = fc1, fc2
        if l == 3:
            l20 = np.concatenate([a["L3_gnn_Wa"], l20], axis=1)
        ow = l20.shape[1] + 3 * NV
        out = np.zeros((P, 3, ow), np.float32)
        for k in range(3):
            at = l20.shape[1] + k * NV
            out[:NS + NV, k, at:at + NV] = l21
        out[P - NV:, 0, :l20.shape[1]] = l20[NS:]
        out[P - NV:, 1, :l20.shape[1]] = l20[:NV]
        out[P - NV:, 2, :l20.shape[1]] = l20[NV:NS]
        d[f"c{l}_out"] = out.reshape(P, 3 * ow)
        na = np.zeros((P, 2, P), np.float32)
        for k, (ws, wv) in enumerate(((sc0, sc1), (l10, l11))):
            na[:NS, k, :NS] = ws
            na[NS:NS + NV, k, NS:NS + NV] = wv
            na[NS + NV:, k, NS + NV:] = wv
        d[f"node{l}_a"] = na.reshape(P, 2 * P)
        d[f"node{l}_b"] = np.concatenate([sc1, l11], axis=1)
    return {k: np.ascontiguousarray(v) for k, v in d.items()}


def kernel(**inputs):
    import numpy as np
    import concourse.bacc as bacc
    from concourse.bass_utils import run_bass_kernel_spmd

    arrays = lay_out(inputs)
    nc = bacc.Bacc("TRN2", target_bir_lowering=False, num_devices=1)
    dram = {name: nc.dram_tensor(name, a.shape, mybir.dt.from_np(a.dtype), kind="ExternalInput").ap()
            for name, a in arrays.items()}
    result = nc.dram_tensor("result", (PADDED, D), F32, kind="ExternalOutput").ap()
    build(nc, dram, result)
    out = run_bass_kernel_spmd(nc, [arrays], core_ids=[0]).results[0]["result"][:ROWS]
    v = out[:, NS:].reshape(ROWS, 3, NV).transpose(0, 2, 1).reshape(ROWS, 3 * NV)
    return np.concatenate([out[:, :NS], v], axis=1)
```
